# Optimizing a Trainium2 kernel written in Bass

```python
import numpy as np
import jax
import jax.numpy as jnp

def _softmax(x, axis=-1):
    return jax.nn.softmax(x, axis=axis)

def _gelu(x):
    return jax.nn.gelu(x, approximate=True)

def _silu(x):
    return jax.nn.silu(x)

def _sigmoid(x):
    return jax.nn.sigmoid(x)

def _layernorm(x, axis=-1, eps=1e-05):
    m = jnp.mean(x, axis=axis, keepdims=True)
    v = jnp.var(x, axis=axis, keepdims=True)
    return (x - m) / jnp.sqrt(v + eps)

def _scatter_add(tgt, idx, src, axis=0):
    return tgt.at[idx].add(src)

def _segment_sum(src, seg, n):
    return jax.ops.segment_sum(src, seg, n)
kernel_name = 'mk_gps_d1_gnn_r8_277ce3'

def setup_inputs(seed: int=0):
    np.random.seed(seed)
    _w = jnp.asarray

    def _rec_inputs():
        import jax
        import jax.numpy as jnp
        _gk = jax.random.key(seed)
        x = -0.000364 + 1 * jax.random.normal(jax.random.fold_in(_gk, 1), (3750, 512), jnp.float32)
        _s = jax.random.randint(jax.random.fold_in(_gk, 2), (60000,), 0, 3750, jnp.int32)
        _d = jax.random.randint(jax.random.fold_in(_gk, 3), (60000,), 0, 3750, jnp.int32)
        _loop = jnp.arange(3750, dtype=jnp.int32)
        src = jnp.concatenate([_s, _d, _loop])
        dst = jnp.concatenate([_d, _s, _loop])
        _o = jnp.argsort(dst, stable=True)
        src = src[_o]
        dst = dst[_o]
        return (x, src, dst)
    x, src, dst = _rec_inputs()

    def _L0_gnn_setup():
        import jax, jax.numpy as jnp
        import numpy as np
        N = 3750
        E = 60000
        D_IN = 512
        D_HID = 512
        D_OUT = 512
        EPS = 1e-05

        def gcn_conv(x, W, b, src, dst, n_nodes):
            xw = x @ W
            loop = jnp.arange(n_nodes, dtype=src.dtype)
            s = jnp.concatenate([src, loop])
            d = jnp.concatenate([dst, loop])
            deg = jax.ops.segment_sum(jnp.ones_like(d, dtype=xw.dtype), d, num_segments=n_nodes)
            dinv = jnp.where(deg > 0, jax.lax.rsqrt(deg), 0.0)
            norm = dinv[s] * dinv[d]
            msg = norm[:, None] * xw[s]
            out = jax.ops.segment_sum(msg, d, num_segments=n_nodes)
            return out + b

        def layer_norm(x, gamma, beta):
            mu = jnp.mean(x, axis=-1, keepdims=True)
            var = jnp.mean(jnp.square(x - mu), axis=-1, keepdims=True)
            return (x - mu) * jax.lax.rsqrt(var + EPS) * gamma + beta
        key = jax.random.key(seed)
        ks = jax.random.split(key, 8)
        x = jax.random.normal(ks[0], (N, D_IN), dtype=jnp.float32)
        edge_index = jax.random.randint(ks[1], (2, E), 0, N, dtype=jnp.int64)
        batch = jnp.zeros((N,), dtype=jnp.int64)
        s1 = 1.0 / np.sqrt(D_IN)
        s2 = 1.0 / np.sqrt(D_HID)
        W1 = jax.random.uniform(ks[2], (D_IN, D_HID), jnp.float32, -s1, s1)
        b1 = jnp.zeros((D_HID,), jnp.float32)
        W2 = jax.random.uniform(ks[3], (D_HID, D_OUT), jnp.float32, -s2, s2)
        b2 = jnp.zeros((D_OUT,), jnp.float32)
        gamma1 = jnp.ones((D_HID,), jnp.float32)
        beta1 = jnp.zeros((D_HID,), jnp.float32)
        gamma2 = jnp.ones((D_OUT,), jnp.float32)
        beta2 = jnp.zeros((D_OUT,), jnp.float32)
        return {'x': x, 'edge_index': edge_index, 'batch': batch, 'W1': W1, 'b1': b1, 'gamma1': gamma1, 'beta1': beta1, 'W2': W2, 'b2': b2, 'gamma2': gamma2, 'beta2': beta2}
    _L0_gnn_all = _L0_gnn_setup()
    _L0_gnn_in = {k: v for k, v in _L0_gnn_all.items() if k in ('W1', 'b1', 'gamma1', 'beta1', 'W2', 'b2', 'gamma2', 'beta2')}
    del _L0_gnn_all

    def _L0_mix_setup():
        import jax, jax.numpy as jnp
        import numpy as np
        EPS_STAB = 1e-09
        BN_EPS = 1e-05
        key = jax.random.key(seed)
        ks = jax.random.split(key, 5)
        B, N, C = (2, 512, 512)
        s = 1.0 / np.sqrt(C)
        d = {'inputs': jax.random.normal(ks[0], (B, N, C), jnp.float32)}
        for i, w in enumerate(['Wq', 'Wk', 'Wv', 'Wo']):
            d[w] = jax.random.normal(ks[1 + i], (C, C), jnp.float32) * s
        for b in ['bq', 'bk', 'bv', 'bo']:
            d[b] = jnp.zeros((C,), jnp.float32)
        d['bn_scale'] = jnp.ones((C,), jnp.float32)
        d['bn_bias'] = jnp.zeros((C,), jnp.float32)
        d['bn_mean'] = jnp.zeros((C,), jnp.float32)
        d['bn_var'] = jnp.ones((C,), jnp.float32)
        return d
    _L0_mix_all = _L0_mix_setup()
    _L0_mix_in = {k: v for k, v in _L0_mix_all.items() if k in ('Wq', 'bq', 'Wk', 'bk', 'Wv', 'bv', 'Wo', 'bo', 'bn_scale', 'bn_bias', 'bn_mean', 'bn_var')}
    del _L0_mix_all

    def _L0_ffn_setup():
        import jax, jax.numpy as jnp
        import numpy as np
        FP8_MAX = 448.0
        K, N = (512, 512)
        key = jax.random.key(seed)
        kx, kw = jax.random.split(key)
        x = jax.random.normal(kx, (8, 1024, K), dtype=jnp.float32)
        weight = jax.random.normal(kw, (K, N), dtype=jnp.float32) * 0.02
        return {'x': x, 'weight': weight}
    _L0_ffn_all = _L0_ffn_setup()
    _L0_ffn_in = {k: v for k, v in _L0_ffn_all.items() if k in ('weight',)}
    del _L0_ffn_all
    return {'x': x, 'src': src, 'dst': dst, 'L0_gnn_W1': _L0_gnn_in['W1'], 'L0_gnn_b1': _L0_gnn_in['b1'], 'L0_gnn_gamma1': _L0_gnn_in['gamma1'], 'L0_gnn_beta1': _L0_gnn_in['beta1'], 'L0_gnn_W2': _L0_gnn_in['W2'], 'L0_gnn_b2': _L0_gnn_in['b2'], 'L0_gnn_gamma2': _L0_gnn_in['gamma2'], 'L0_gnn_beta2': _L0_gnn_in['beta2'], 'L0_mix_Wq': _L0_mix_in['Wq'], 'L0_mix_bq': _L0_mix_in['bq'], 'L0_mix_Wk': _L0_mix_in['Wk'], 'L0_mix_bk': _L0_mix_in['bk'], 'L0_mix_Wv': _L0_mix_in['Wv'], 'L0_mix_bv': _L0_mix_in['bv'], 'L0_mix_Wo': _L0_mix_in['Wo'], 'L0_mix_bo': _L0_mix_in['bo'], 'L0_mix_bn_scale': _L0_mix_in['bn_scale'], 'L0_mix_bn_bias': _L0_mix_in['bn_bias'], 'L0_mix_bn_mean': _L0_mix_in['bn_mean'], 'L0_mix_bn_var': _L0_mix_in['bn_var'], 'L0_ffn_weight': _L0_ffn_in['weight']}

def reference(x, src, dst, L0_gnn_W1, L0_gnn_b1, L0_gnn_gamma1, L0_gnn_beta1, L0_gnn_W2, L0_gnn_b2, L0_gnn_gamma2, L0_gnn_beta2, L0_mix_Wq, L0_mix_bq, L0_mix_Wk, L0_mix_bk, L0_mix_Wv, L0_mix_bv, L0_mix_Wo, L0_mix_bo, L0_mix_bn_scale, L0_mix_bn_bias, L0_mix_bn_mean, L0_mix_bn_var, L0_ffn_weight):
    import jax
    import jax.numpy as jnp

    def _L0_gnn_ref(x, edge_index, batch, W1, b1, gamma1, beta1, W2, b2, gamma2, beta2):
        import jax, jax.numpy as jnp
        import numpy as np
        N = 3750
        E = 60000
        D_IN = 512
        D_HID = 512
        D_OUT = 512
        EPS = 1e-05

        def gcn_conv(x, W, b, src, dst, n_nodes):
            xw = x @ W
            loop = jnp.arange(n_nodes, dtype=src.dtype)
            s = jnp.concatenate([src, loop])
            d = jnp.concatenate([dst, loop])
            deg = jax.ops.segment_sum(jnp.ones_like(d, dtype=xw.dtype), d, num_segments=n_nodes)
            dinv = jnp.where(deg > 0, jax.lax.rsqrt(deg), 0.0)
            norm = dinv[s] * dinv[d]
            msg = norm[:, None] * xw[s]
            out = jax.ops.segment_sum(msg, d, num_segments=n_nodes)
            return out + b

        def layer_norm(x, gamma, beta):
            mu = jnp.mean(x, axis=-1, keepdims=True)
            var = jnp.mean(jnp.square(x - mu), axis=-1, keepdims=True)
            return (x - mu) * jax.lax.rsqrt(var + EPS) * gamma + beta
        src, dst = (edge_index[0], edge_index[1])
        residual = x
        h = gcn_conv(x, W1, b1, src, dst, N)
        h = layer_norm(h, gamma1, beta1)
        h = jax.nn.gelu(h, approximate=False)
        h = gcn_conv(h, W2, b2, src, dst, N)
        h = layer_norm(h, gamma2, beta2)
        return jax.nn.gelu(h + residual, approximate=False)

    def _L0_mix_ref(inputs, Wq, bq, Wk, bk, Wv, bv, Wo, bo, bn_scale, bn_bias, bn_mean, bn_var):
        import jax, jax.numpy as jnp
        import numpy as np
        EPS_STAB = 1e-09
        BN_EPS = 1e-05
        q = inputs @ Wq + bq
        k = inputs @ Wk + bk
        v = inputs @ Wv + bv
        att = jax.nn.softmax(jnp.einsum('bmc,bnc->bmn', q, k), axis=-1)
        att = att / (EPS_STAB + jnp.sum(att, axis=1, keepdims=True))
        out = v * jnp.sum(att, axis=1)[..., None]
        out = out @ Wo + bo
        out = (out - bn_mean) * jax.lax.rsqrt(bn_var + BN_EPS) * bn_scale + bn_bias
        return jax.nn.relu(out) + inputs

    def _L0_ffn_ref(x, weight):
        import jax, jax.numpy as jnp
        import numpy as np
        FP8_MAX = 448.0
        K, N = (512, 512)
        B, S, _ = x.shape
        x2d = x.reshape(-1, K)
        x_amax = jnp.max(jnp.abs(x2d))
        x_scale = FP8_MAX / jnp.maximum(x_amax, 1e-12)
        x_fp8 = jnp.clip(x2d * x_scale, -FP8_MAX, FP8_MAX).astype(jnp.float8_e4m3fn)
        w_amax = jnp.max(jnp.abs(weight))
        w_scale = FP8_MAX / jnp.maximum(w_amax, 1e-12)
        w_fp8 = jnp.clip(weight.T * w_scale, -FP8_MAX, FP8_MAX).astype(jnp.float8_e4m3fn)
        res = jnp.matmul(x_fp8.astype(jnp.float32), w_fp8.astype(jnp.float32).T)
        out = res * (1.0 / x_scale * (1.0 / w_scale))
        return out.reshape(B, S, N).astype(x.dtype)
    edge_index = jnp.stack([src, dst])
    batch0 = jnp.zeros((3750,), jnp.int32)
    xn = _layernorm(x, axis=-1)
    x = x + _L0_gnn_ref(xn, edge_index, batch0, L0_gnn_W1, L0_gnn_b1, L0_gnn_gamma1, L0_gnn_beta1, L0_gnn_W2, L0_gnn_b2, L0_gnn_gamma2, L0_gnn_beta2) + _L0_mix_ref(xn[None], L0_mix_Wq, L0_mix_bq, L0_mix_Wk, L0_mix_bk, L0_mix_Wv, L0_mix_bv, L0_mix_Wo, L0_mix_bo, L0_mix_bn_scale, L0_mix_bn_bias, L0_mix_bn_mean, L0_mix_bn_var)[0]
    x = x + _L0_ffn_ref(_layernorm(x, axis=-1)[None], L0_ffn_weight)[0]
    return x

_drawn_inputs = setup_inputs


def setup_inputs(seed=0):
    import zlib

    import numpy as np

    out = dict(_drawn_inputs(seed))
    spreads = {'L0_gnn_b1': (0.0, 0.1),
     'L0_gnn_gamma1': (1.0, 0.2),
     'L0_gnn_beta1': (0.0, 0.1),
     'L0_gnn_b2': (0.0, 0.1),
     'L0_gnn_gamma2': (1.0, 0.2),
     'L0_gnn_beta2': (0.0, 0.323),
     'L0_mix_bq': (0.0, 0.8),
     'L0_mix_bk': (0.0, 0.8),
     'L0_mix_bv': (0.0, 0.302),
     'L0_mix_bo': (0.0, 0.322),
     'L0_mix_bn_scale': (1.0, 0.2),
     'L0_mix_bn_bias': (0.0, 0.307),
     'L0_mix_bn_mean': (0.0, 0.311),
     'L0_mix_bn_var': (1.0, 0.594)}
    factors = {'L0_mix_Wq': 8.0, 'L0_mix_Wk': 8.0}
    for name, (base, spread) in spreads.items():
        noise = np.random.default_rng([zlib.crc32(name.encode()), seed]).standard_normal(out[name].shape)
        drawn = base * np.exp(spread * noise) if base else spread * noise
        out[name] = jnp.asarray(drawn.astype(out[name].dtype))
    for name, factor in factors.items():
        out[name] = (out[name] * factor).astype(out[name].dtype)
    return out
```

```python
from contextlib import ExitStack

import concourse.bass as bass
from concourse import mybir

ALU = mybir.AluOpType
ACT = mybir.ActivationFunctionType
AX = mybir.AxisListType
F32 = mybir.dt.float32
F16 = mybir.dt.float16
BF16 = mybir.dt.bfloat16
I32 = mybir.dt.int32
RMAX = bass.bass_isa.ReduceOp.max

P = 128
N = 3750
D = 512
K = D // P
T = -(-N // P)
NP = T * P
E = 123750
CH = -(-E // P)
WIN = 16
WPT = P // WIN
NWIN = T * WPT
SPAN = 6
CODES = T * WIN
HALFW = NWIN // 2
GROUPS = [(g, min(512, N - g)) for g in range(0, N, 512)]
FAR = 16384.0
XSCALE = 1024.0
ROOT_D = 22.7
TOP = 32768.0
EXPONENT = 0x7F800000
FP8_MAX = 448.0
EPS = 1e-5
LOOPS = (T - 2) // 2

B1, G1, BE1, B2, G2, BE2, MIXC = range(7)
WQ, WK, WV, WO, W1, W2, WF = range(7)
(A_W1, A_W2, A_M, A_WVO, A_C, A_FFN, A_G1, A_BE1, S_W1, S_W2, S_M, S_WVO, S_G, S_Y1, S_H, S_Y2,
 F_G, F_S, F_U, R_Y1, R_Y2, R_H, R_W1, R_W2, X_SC, X_F, W_SC, TMP, TMP2, BQBK, A_X, R_WVO) = range(32)


def wait_apart(eng, s, value, passed):
    eng.wait_ge(s, value)
    eng.sem_inc(passed, 1)


def split_product(pe, out, lhs, at, rhs):
    for k in range(K):
        for l, r in ((0, 0), (0, 1), (1, 0)):
            ins = pe.matmul(out, lhs[:, l, k, at], rhs[:, r, k, :], start=(k == 0 and l == 0 and r == 0),
                            stop=(k == K - 1 and l == 1))
    return ins


def gps_layer_kernel(nc, x, edges, w, out):
    counts_dram = nc.dram_tensor("counts_dram", [T, P, NP], F16).ap()
    mix_dram = nc.dram_tensor("mix_dram", [T, P, D], F32).ap()
    x_t = x.rearrange("(t p) d -> t p d", p=P)
    out_t = out.rearrange("(t p) d -> t p d", p=P)

    ctx = ExitStack()
    with ctx:
        def sb(name, shape, dt=F32):
            return ctx.enter_context(nc.sbuf_tensor(name, shape, dt))

        def sem(name):
            return ctx.enter_context(nc.semaphore(name))

        regionA = sb("regionA", [P, T * D])
        regionB = sb("regionB", [P, T * D])
        regionZ = sb("regionZ", [P, 12376])
        mparts = sb("mparts", [P, 2, K, D], F16)
        w2parts = sb("w2parts", [P, 2, K, D], F16)
        wffn = sb("wffn", [P, K, D], BF16)
        rows = sb("rows", [P, 7, D])
        ident = sb("ident", [P, P])
        ident16 = sb("ident16", [P, P], F16)
        identb = sb("identb", [P, P], BF16)
        col16 = sb("col16", [P, D], F16)
        onerow = sb("onerow", [1, P])
        ones = sb("ones", [P, 1])
        ones16 = sb("ones16", [P, 1], F16)
        half = sb("half", [P, T])
        rowmask = sb("rowmask", [P, T])
        deg = sb("deg", [P, T])
        dinv = sb("dinv", [P, T])
        xmean = sb("xmean", [P, T])
        xrstd = sb("xrstd", [P, T])
        rowbias = sb("rowbias", [P, T])
        mixs = sb("mixs", [P, T])
        nmean = sb("nmean", [P, T])
        nrstd = sb("nrstd", [P, T])
        namax = sb("namax", [P, T])
        f_y1 = sb("f_y1", [P, T])
        f_z1 = sb("f_z1", [P, T])
        f_y2 = sb("f_y2", [P, T])
        f_z2 = sb("f_z2", [P, T])
        sc = sb("sc", [P, 32])
        wide = sb("wide", [P, 8])
        cg = sb("cg", [P, 2, K])
        stats = sb("stats", [P, 2, 6])
        nst = sb("nst", [P, 2, 6])
        nag = sb("nag", [P, 2, 2])
        nveps = sb("nveps", [P, 2])
        aggr = sb("aggr", [P, 2, 2])
        veps = sb("veps", [P, 2])
        xdot = sb("xdot", [P, 2])
        mx = sb("mx", [P, 2, 8])
        soft = sb("soft", [P, 2, 5])
        bcols = sb("bcols", [P, 3, K])
        ps = ctx.enter_context(nc.psum_tensor("ps", [P, 8, 512], F32))

        xparts = regionA[:, :].bitcast(F16).rearrange("p (h k n) -> p h k n", h=2, k=K)
        y1 = regionB[:, :].bitcast(F16).rearrange("p (t h n) -> p t h n", t=T, h=2)
        y2 = regionA[:, :].bitcast(F16).rearrange("p (t h n) -> p t h n", t=T, h=2)
        xnew = regionB[:, :].rearrange("p (t n) -> p t n", t=T)

        def z32(at, n):
            return regionZ[:, at:at + n]

        def c(i):
            return sc[:, i:i + 1]

        passed = sem("waits_passed")

        code = z32(0, SPAN * NWIN).rearrange("p (s w) -> p s w", s=SPAN)
        low = z32(1440, SPAN * NWIN).rearrange("p (s w) -> p s w", s=SPAN)
        w1parts = z32(2880, 2048).bitcast(F16).rearrange("p (h k n) -> p h k n", h=2, k=K)
        wvoparts = z32(4928, 2048).bitcast(F16).rearrange("p (h k n) -> p h k n", h=2, k=K)
        bvorow = z32(6976, D)
        wqbkrow = z32(7488, D)

        wraw = regionA[:, 0:7 * K * D].rearrange("p (w k n) -> p w k n", w=7, k=K)
        mixrows = regionB[:, 12800:12800 + 5 * D].rearrange("p (r n) -> p r n", r=5)
        BO, MEAN, VAR, SCALE, BIAS = range(5)
        tables = regionB[0:HALFW, 0:12 * 256].bitcast(I32).rearrange("p (j v e) -> p j v e", j=2 * SPAN, v=2)
        t_src, t_dst = tables[:, :, 0, :], tables[:, :, 1, :]
        NE = 2 * SPAN * P

        def etab(i, dt=F32):
            return regionB[0:HALFW, 3072 + i * NE:3072 + (i + 1) * NE].bitcast(dt).rearrange(
                "p (j e) -> p j e", j=2 * SPAN)

        lastdst = regionZ[0:1, 2880:2880 + CH]
        lastdst_f = regionZ[0:1, 3848:3848 + CH]
        behind = z32(4816, 512)
        thr = sb("thr", [P, 2])
        starts = sb("starts", [P, 2, 3])
        chunkf = sb("chunkf", [P, 2 * SPAN])
        chunki = sb("chunki", [P, 2 * SPAN], I32)

        wsem = [sem(f"weight_loaded{i}") for i in range(7)]
        rows_loaded = sem("rows_loaded")
        mixrows_loaded = sem("mix_rows_loaded")
        cols_loaded = sem("bias_columns_loaded")
        last_loaded = sem("last_destinations_loaded")
        p1_const = sem("p1_constants")
        p1_zeroed = sem("p1_zeroed")
        p1_lastf = sem("p1_last_destinations_float")
        p1_rep = sem("p1_last_destinations_repeated")
        p1_vec = sem("p1_vector_steps")
        p1_chunks = sem("p1_chunks_of_windows")
        p1_gathered = sem("p1_edges_gathered")
        p1_coded = sem("p1_edges_coded")
        p1_turned = sem("p1_codes_transposed")
        p1_kept = sem("p1_codes_kept")

        def chain(eng, s, start=0):
            n = [start]

            def link(ins):
                n[0] += 1
                ins.then_inc(s, 1)
                eng.wait_ge(s, n[0])
            return link

        with nc.Block() as block:
            @block.sync
            def _(sp):
                with nc.allow_non_contiguous_dma(reason="one word of each chunk, 967 in all"):
                    sp.dma_start(lastdst.bitcast(I32), edges[0:CH, 1, P - 1:P].rearrange("c e -> e c")
                                 ).then_inc(last_loaded, 16)
                for i, name in ((WQ, "Wq"), (WK, "Wk"), (WV, "Wv"), (WO, "Wo"), (W1, "W1"), (W2, "W2"), (WF, "Wf")):
                    sp.dma_start(wraw[:, i], w[name].rearrange("(k p) n -> p k n", p=P)).then_inc(wsem[i], 16)
                for r, name in ((B1, "b1"), (G1, "g1"), (BE1, "be1"), (B2, "b2"), (G2, "g2"), (BE2, "be2")):
                    sp.dma_start(rows[:, r], w[name].rearrange("(a n) -> a n", a=1).to_broadcast([P, D])
                                 ).then_inc(rows_loaded, 16)
                for r, name in ((BO, "bo"), (MEAN, "mean"), (VAR, "var"), (SCALE, "scale"), (BIAS, "bias")):
                    sp.dma_start(mixrows[:, r], w[name].rearrange("(a n) -> a n", a=1).to_broadcast([P, D])
                                 ).then_inc(mixrows_loaded, 16)
                with nc.allow_non_contiguous_dma(reason="three vectors of 512 words down the partitions"):
                    for r, name in enumerate(("bq", "bk", "bv")):
                        sp.dma_start(bcols[:, r], w[name].rearrange("(k p) -> p k", p=P)).then_inc(cols_loaded, 16)

            @block.gpsimd
            def _(pool):
                pool.memset(ident[:], 0.0).then_inc(p1_zeroed, 1)
                pool.memset(ident16[:], 0.0).then_inc(p1_zeroed, 1)
                pool.memset(identb[:], 0.0).then_inc(p1_zeroed, 1)
                pool.memset(rowmask[:], 1.0).then_inc(p1_zeroed, 1)
                pool.wait_ge(p1_zeroed, 4)
                for t in (ident, ident16, identb):
                    pool.affine_select(out=t[:], in_=t[:], compare_op=ALU.not_equal, fill=1.0, base=0,
                                       pattern=[[-1, P]], channel_multiplier=1).then_inc(p1_const, 1)
                pool.affine_select(out=rowmask[:], in_=rowmask[:], compare_op=ALU.is_gt, fill=0.0, base=N,
                                   pattern=[[-P, T]], channel_multiplier=-1).then_inc(p1_const, 1)
                pool.iota(col16[:], pattern=[[1, D]], base=0, channel_multiplier=0,
                          allow_small_or_imprecise_dtypes=True).then_inc(p1_const, 1)
                pool.iota(thr[:], pattern=[[WIN * HALFW, 2]], base=0, channel_multiplier=WIN,
                          allow_small_or_imprecise_dtypes=True).then_inc(p1_const, 1)
                pool.memset(onerow[:], 1.0).then_inc(p1_const, 1)
                pool.memset(ones[:], 1.0).then_inc(p1_const, 1)
                pool.memset(ones16[:], 1.0).then_inc(p1_const, 1)
                pool.memset(half[:], -0.5).then_inc(p1_const, 1)
                pool.wait_ge(p1_chunks, 1)
                for j in range(2 * SPAN):
                    pool.indirect_dma_start(
                        out=tables[:, j].rearrange("p v e -> p (v e)"), out_offset=None,
                        in_=edges.rearrange("c v e -> c (v e)"),
                        in_offset=bass.IndirectOffsetOnAxis(ap=chunki[0:HALFW, j:j + 1], axis=0),
                    ).then_inc(p1_gathered, 16)

            @block.vector
            def _(dve):
                link = chain(dve, p1_vec)
                dve.wait_ge(last_loaded, 16)
                dve.tensor_copy(lastdst_f, lastdst.bitcast(I32)).then_inc(p1_lastf, 1)
                dve.wait_ge(p1_const, 10)
                dve.wait_ge(p1_rep, 1)
                for g in range(2):
                    for h, (a, n) in enumerate(((0, 512), (512, CH - 512))):
                        link(dve.tensor_scalar(behind[:, 0:n], ps[:, h, 0:n], thr[:, g:g + 1], None, ALU.is_lt,
                                               ALU.add, accum_out=starts[:, g, h:h + 1]))
                    link(dve.tensor_tensor(starts[:, g, 2:3], starts[:, g, 0:1], starts[:, g, 1:2], ALU.add))
                    for s in range(SPAN):
                        link(dve.tensor_scalar(chunkf[:, g * SPAN + s:g * SPAN + s + 1], starts[:, g, 2:3],
                                               float(s), float(CH), ALU.add, ALU.min))
                dve.tensor_copy(chunki[:], chunkf[:]).then_inc(p1_chunks, 1)
                dve.wait_ge(p1_gathered, 16 * 2 * SPAN)
                link(dve.tensor_scalar(etab(0, I32), t_src, 7, None, ALU.logical_shift_right))
                link(dve.tensor_scalar(etab(1, I32), t_src, P - 1, None, ALU.bitwise_and))
                link(dve.tensor_copy(etab(2), etab(0, I32)))
                link(dve.tensor_copy(etab(0), etab(1, I32)))
                link(dve.tensor_copy(etab(3), t_dst))
                for g in range(2):
                    js = slice(g * SPAN, (g + 1) * SPAN)
                    link(dve.tensor_scalar(etab(1)[:, js], etab(3)[:, js], thr[0:HALFW, g:g + 1], None, ALU.subtract))
                link(dve.scalar_tensor_tensor(out=etab(2), in0=etab(2), scalar=float(WIN), in1=etab(1),
                                              op0=ALU.mult, op1=ALU.add))
                link(dve.tensor_scalar(etab(3), etab(1), 0.0, FAR, ALU.is_lt, ALU.mult))
                link(dve.tensor_scalar(etab(1), etab(1), float(WIN), FAR, ALU.is_ge, ALU.mult))
                link(dve.tensor_tensor(etab(3), etab(3), etab(1), ALU.add))
                dve.tensor_tensor(etab(2), etab(2), etab(3), ALU.add).then_inc(p1_coded, 1)
                for j in range(2 * SPAN):
                    g, s = divmod(j, SPAN)
                    dve.wait_ge(p1_turned, j + 1)
                    b = 2 + 2 * (j % 3)
                    dve.tensor_copy(code[:, s, g * HALFW:(g + 1) * HALFW], ps[:, b, 0:HALFW])
                    dve.tensor_copy(low[:, s, g * HALFW:(g + 1) * HALFW], ps[:, b + 1, 0:HALFW]).then_inc(p1_kept, 1)

            @block.tensor
            def _(pe):
                pe.wait_ge(p1_const, 10)
                pe.wait_ge(p1_lastf, 1)
                pe.matmul(ps[:, 0, 0:512], onerow[:], lastdst_f[:, 0:512], start=True, stop=True)
                pe.matmul(ps[:, 1, 0:CH - 512], onerow[:], lastdst_f[:, 512:CH], start=True, stop=True
                          ).then_inc(p1_rep, 1)
                pe.wait_ge(p1_coded, 1)
                for j in range(2 * SPAN):
                    if j >= 3:
                        pe.wait_ge(p1_kept, j - 2)
                    b = 2 + 2 * (j % 3)
                    pe.transpose(ps[:, b, 0:HALFW], etab(2)[:, j], ident[0:HALFW, 0:HALFW])
                    pe.transpose(ps[:, b + 1, 0:HALFW], etab(0)[:, j], ident[0:HALFW, 0:HALFW]
                                 ).then_inc(p1_turned, 1)

        wt = regionB[:, 0:3 * K * D].rearrange("p (w k n) -> p w k n", w=3, k=K)
        mraw = regionB[:, 3 * K * D:4 * K * D].rearrange("p (k n) -> p k n", k=K)
        wvoraw = regionB[:, 4 * K * D:5 * K * D].rearrange("p (k n) -> p k n", k=K)
        wtmp = z32(8000, K * D).rearrange("p (k n) -> p k n", k=K)
        wpow = z32(10048, K * D).rearrange("p (k n) -> p k n", k=K)
        reps = regionA[:, 7 * K * D:7 * K * D + 2 * D].rearrange("p (b k n) -> p b k n", b=2, k=K)
        reps2 = regionB[:, 5 * K * D:5 * K * D + D].rearrange("p (k n) -> p k n", k=K)
        BQ, BK, BV = range(3)
        rep = [reps[:, 0], reps[:, 1], reps2]
        p2_rep = sem("p2_bias_columns_repeated")
        p2_turned = sem("p2_weights_transposed")
        p2_turned_out = sem("p2_transposes_copied")
        p2_made = sem("p2_products_made")
        p2_out = sem("p2_products_copied")
        p2_vec = sem("p2_vector_steps")
        p2_var = sem("p2_variance_ready")
        p2_root = sem("p2_root_ready")
        p2_max = sem("p2_maxima_ready")
        p2_all = sem("p2_maxima_over_partitions")

        with nc.Block() as block:
            @block.gpsimd
            def _(pool):
                pool.wait_ge(p2_var, 1)
                pool.tensor_tensor(mixrows[:, VAR], mixrows[:, VAR], wtmp[:, 0], ALU.pow).then_inc(p2_root, 1)
                pool.wait_ge(p2_max, 1)
                pool.partition_all_reduce(sc[:, 0:8], wide[:], P, RMAX).then_inc(p2_all, 1)

            @block.tensor
            def _(pe):
                for j in range(3 * K):
                    m, i = divmod(j, K)
                    if j == 0:
                        for s in wsem:
                            pe.wait_ge(s, 16)
                    if j >= 8:
                        pe.wait_ge(p2_turned_out, j - 7)
                    for a in range(K):
                        ins = pe.transpose(ps[:, j % 8, a * P:(a + 1) * P], wraw[:, m, a, i * P:(i + 1) * P], ident[:])
                    ins.then_inc(p2_turned, 1)
                pe.wait_ge(p2_turned_out, 3 * K)
                pe.wait_ge(p2_rep, 1)
                for a in range(K):
                    for i in range(K):
                        ins = pe.matmul(ps[:, a, :], wt[:, WQ, i, a * P:(a + 1) * P], wt[:, WK, i, :],
                                        start=(i == 0), stop=(i == K - 1))
                    ins.then_inc(p2_made, 1)
                for a in range(K):
                    for i in range(K):
                        ins = pe.matmul(ps[:, 4 + a, :], wt[:, WV, i, a * P:(a + 1) * P], wraw[:, WO, i, :],
                                        start=(i == 0), stop=(i == K - 1))
                    ins.then_inc(p2_made, 1)
                pe.wait_ge(p2_out, 1)
                for b in range(K):
                    for i in range(K):
                        ins = pe.matmul(ps[:, 0, b:b + 1], wt[:, WK, i, b * P:(b + 1) * P], bcols[:, BQ, i:i + 1],
                                        start=(i == 0), stop=(i == K - 1))
                ins.then_inc(p2_made, 1)
                pe.wait_ge(p2_out, 2)
                for i in range(K):
                    ins = pe.matmul(ps[:, 1, :], rep[BK][:, i], wt[:, WQ, i, :], start=(i == 0), stop=(i == K - 1))
                ins.then_inc(p2_made, 1)
                pe.wait_ge(p2_out, 3)
                for i in range(K):
                    ins = pe.matmul(ps[:, 2, :], rep[BV][:, i], wraw[:, WO, i, :], start=(i == 0), stop=(i == K - 1))
                ins.then_inc(p2_made, 1)
                pe.wait_ge(p2_out, 4)
                for i in range(K):
                    ins = pe.matmul(ps[:, 3, 0:1], rep[BQ][:, i], bcols[:, BK, i:i + 1],
                                    start=(i == 0), stop=(i == K - 1))
                ins.then_inc(p2_made, 1)

            @block.scalar
            def _(act):
                for j in range(3 * K):
                    m, i = divmod(j, K)
                    act.wait_ge(p2_turned, j + 1)
                    act.copy(wt[:, m, i, :], ps[:, j % 8, :]).then_inc(p2_turned_out, 1)

            @block.vector
            def _(dve):
                link = chain(dve, p2_vec)
                dve.wait_ge(rows_loaded, 16 * 6)
                dve.wait_ge(mixrows_loaded, 16 * 5)
                dve.wait_ge(cols_loaded, 16 * 3)
                link(dve.memset(wtmp[:, 0], -0.5))
                dve.tensor_scalar(mixrows[:, VAR], mixrows[:, VAR], EPS, None, ALU.add).then_inc(p2_var, 1)
                link(dve.memset(wtmp[:, 1:3], 1.0))
                for b in range(3):
                    for i in range(K):
                        ins = dve.tensor_scalar(rep[b][:, i], wtmp[:, 1, 0:P], bcols[:, b, i:i + 1], None, ALU.mult)
                link(ins)
                dve.sem_inc(p2_rep, 1)
                dve.wait_ge(p2_root, 1)
                link(dve.tensor_tensor(mixrows[:, SCALE], mixrows[:, SCALE], mixrows[:, VAR], ALU.mult))
                link(dve.tensor_tensor(mixrows[:, BO], mixrows[:, BO], mixrows[:, MEAN], ALU.subtract))
                link(dve.tensor_tensor(mixrows[:, BO], mixrows[:, BO], mixrows[:, SCALE], ALU.mult))
                link(dve.tensor_tensor(rows[:, MIXC], mixrows[:, BO], mixrows[:, BIAS], ALU.add))
                for a in range(K):
                    dve.wait_ge(p2_made, a + 1)
                    dve.tensor_copy(mraw[:, a, :], ps[:, a, :]).then_inc(p2_out, 1)
                for a in range(K):
                    dve.wait_ge(p2_made, K + a + 1)
                    link(dve.tensor_tensor(wvoraw[:, a, :], ps[:, 4 + a, :], mixrows[:, SCALE], ALU.mult))
                dve.wait_ge(p2_out, K)
                dve.wait_ge(p2_made, 2 * K + 1)
                link(dve.tensor_copy(cg[:, 0, :], ps[:, 0, 0:K]))
                dve.wait_ge(p2_made, 2 * K + 2)
                link(dve.tensor_copy(wqbkrow, ps[:, 1, :]))
                dve.wait_ge(p2_made, 2 * K + 3)
                link(dve.tensor_tensor(bvorow, ps[:, 2, :], mixrows[:, SCALE], ALU.mult))
                dve.wait_ge(p2_made, 2 * K + 4)
                link(dve.tensor_copy(c(BQBK), ps[:, 3, 0:1]))

                def flat(ap):
                    return ap.rearrange("p k n -> p (k n)")
                for i, ap in ((A_W1, flat(wraw[:, W1])), (A_W2, flat(wraw[:, W2])), (A_M, flat(mraw)),
                              (A_WVO, flat(wvoraw)), (A_C, cg[:, 0, :]), (A_FFN, flat(wraw[:, WF])),
                              (A_G1, rows[:, G1]), (A_BE1, rows[:, BE1])):
                    ins = dve.tensor_reduce(wide[:, i:i + 1], ap, AX.X, ALU.max, apply_absolute_value=True)
                link(ins)
                dve.sem_inc(p2_max, 1)
                dve.wait_ge(p2_all, 1)

                def lin(dst, a, m, b):
                    link(dve.scalar_tensor_tensor(out=c(dst), in0=c(a), scalar=m, in1=c(b), op0=ALU.mult, op1=ALU.add))

                def power(dst, bound):
                    link(dve.tensor_scalar(c(TMP2), c(bound), 1e-20, None, ALU.max))
                    link(dve.reciprocal(c(dst), c(TMP2)))
                    link(dve.tensor_scalar(c(dst), c(dst), TOP, None, ALU.mult))
                    link(dve.tensor_scalar(c(dst).bitcast(I32), c(dst).bitcast(I32), EXPONENT, None, ALU.bitwise_and))

                def inverse(dst, s, m):
                    link(dve.reciprocal(c(TMP2), c(s)))
                    link(dve.tensor_scalar(c(dst), c(TMP2), m, None, ALU.mult))

                power(S_W1, A_W1)
                power(S_W2, A_W2)
                power(S_M, A_M)
                power(S_WVO, A_WVO)
                lin(TMP, A_M, ROOT_D * ROOT_D, A_C)
                power(S_G, TMP)
                link(dve.tensor_scalar(c(TMP), c(A_W1), ROOT_D * ROOT_D, None, ALU.mult))
                power(S_Y1, TMP)
                lin(TMP, A_G1, ROOT_D, A_BE1)
                power(S_H, TMP)
                link(dve.tensor_tensor(c(TMP), c(A_G1), c(A_BE1), ALU.add))
                link(dve.tensor_scalar(c(TMP), c(TMP), ROOT_D * ROOT_D, c(A_W2), ALU.mult, ALU.mult))
                power(S_Y2, TMP)
                inverse(R_Y1, S_Y1, 1.0)
                inverse(R_Y2, S_Y2, 1.0)
                inverse(R_W1, S_W1, 1.0 / XSCALE)
                link(dve.tensor_tensor(c(R_W1), c(R_W1), c(S_Y1), ALU.mult))
                inverse(R_W2, S_W2, 1.0)
                inverse(R_H, S_H, 1.0)
                link(dve.tensor_tensor(c(R_W2), c(R_W2), c(R_H), ALU.mult))
                link(dve.tensor_tensor(c(R_W2), c(R_W2), c(S_Y2), ALU.mult))
                inverse(F_U, S_WVO, 1.0 / XSCALE)
                inverse(F_G, S_M, 1.0 / XSCALE)
                link(dve.tensor_tensor(c(F_G), c(F_G), c(S_G), ALU.mult))
                inverse(F_S, S_G, 1.0 / XSCALE)
                link(dve.tensor_scalar(cg[:, 1, :], cg[:, 0, :], c(S_G), None, ALU.mult))
                for parts, raw, s in ((w1parts, wraw[:, W1], S_W1), (w2parts, wraw[:, W2], S_W2),
                                      (mparts, mraw, S_M), (wvoparts, wvoraw, S_WVO)):
                    link(dve.tensor_scalar(parts[:, 0], raw, c(s), None, ALU.mult))
                    link(dve.scalar_tensor_tensor(out=parts[:, 1], in0=raw, scalar=c(s), in1=parts[:, 0],
                                                  op0=ALU.mult, op1=ALU.subtract))
                link(dve.tensor_scalar(c(TMP), c(A_FFN), 1e-12, None, ALU.max))
                link(dve.reciprocal(c(TMP2), c(TMP)))
                link(dve.tensor_scalar(c(W_SC), c(TMP2), FP8_MAX, None, ALU.mult))
                link(dve.tensor_scalar(wtmp, wraw[:, WF], c(W_SC), FP8_MAX, ALU.mult, ALU.min))
                link(dve.tensor_scalar(wtmp, wtmp, -FP8_MAX, None, ALU.max))
                link(dve.tensor_scalar(wpow.bitcast(I32), wtmp.bitcast(I32), EXPONENT, None, ALU.bitwise_and))
                link(dve.tensor_scalar(wpow, wpow, 2.0 ** -6, 1.5 * 2.0 ** 20, ALU.max, ALU.mult))
                link(dve.tensor_tensor(wtmp, wtmp, wpow, ALU.add))
                link(dve.tensor_tensor(wffn[:], wtmp, wpow, ALU.subtract))

        RING = 2 * SPAN
        lowhot = regionA[:, 0:RING * P // 2].bitcast(F16).rearrange("p (r n) -> p r n", r=RING)
        codehot = regionA[:, 1024:1024 + RING * CODES // 2].bitcast(F16).rearrange("p (r n) -> p r n", r=RING)
        ctile = regionA[:, 4096:4096 + NP].bitcast(F16).rearrange("p (b t n) -> p b t n", b=2, t=T)
        p3_hot = sem("p3_onehots_ready")
        p3_used = sem("p3_onehots_used")
        p3_copied = sem("p3_window_copied")
        p3_loops = sem("p3_self_loops_added")
        p3_stored = [sem(f"p3_tile_stored{b}") for b in range(2)]
        p3_deg = sem("p3_degrees_ready")
        p3_degout = sem("p3_degrees_copied")

        with nc.Block() as block:
            @block.vector
            def _(dve):
                with dve.Fori(0, NWIN // 2) as pair:
                    for j in range(RING):
                        u, s = divmod(j, SPAN)
                        dve.wait_ge(p3_used, pair * RING + (j + 1))
                        at = bass.ds(pair * 2 + u, 1)
                        dve.tensor_scalar(lowhot[:, j], col16[:, 0:P], low[:, s, at], None, ALU.is_equal)
                        dve.tensor_scalar(codehot[:, j], col16[:, 0:CODES], code[:, s, at], None, ALU.is_equal
                                          ).then_inc(p3_hot, 1)

            @block.tensor
            def _(pe):
                pe.sem_inc(p3_used, RING)
                with pe.Fori(0, T // 2) as pairt:
                    for b in range(2):
                        with pe.Fori(0, WPT // 2) as q:
                            for u in range(2):
                                pe.wait_ge(p3_copied, (pairt * 2 + b) * WPT + q * 2 + (u + 1))
                                for s in range(SPAN):
                                    pe.wait_ge(p3_hot, ((pairt * 2 + b) * WPT + q * 2 + u) * SPAN + (s + 1))
                                    r = u * SPAN + s
                                    ins = pe.matmul(ps[:, u, 0:CODES], lowhot[:, r], codehot[:, r],
                                                    start=(s == 0), stop=(s == SPAN - 1))
                                    ins.then_inc(p3_used, 1)
                        pe.wait_ge(p3_loops, pairt * 2 + (b + 1))
                        pe.wait_ge(p3_degout, pairt * 2 + (b + 1))
                        for i in range(T):
                            ins = pe.matmul(ps[:, 2 + b, 0:1], ctile[:, b, i, :], ones16[:],
                                            start=(i == 0), stop=(i == T - 1))
                        ins.then_inc(p3_deg, 1)

            @block.scalar
            def _(act):
                act.sem_inc(p3_copied, 2)
                act.sem_inc(p3_degout, 2)
                with act.Fori(0, T // 2) as pairt:
                    for b in range(2):
                        act.wait_ge(p3_stored[b], pairt * 16)
                        with act.Fori(0, WPT // 2) as q:
                            for u in range(2):
                                act.wait_ge(p3_used, ((pairt * 2 + b) * WPT + q * 2 + (u + 1)) * SPAN + RING)
                                act.copy(ctile[:, b, :, bass.ds(q * 2 * WIN + u * WIN, WIN)],
                                         ps[:, u, 0:CODES].rearrange("p (t n) -> p t n", t=T)
                                         ).then_inc(p3_copied, 1)
                        act.wait_ge(p3_deg, pairt * 2 + (b + 1))
                        act.copy(deg[:, bass.ds(pairt * 2 + b, 1)], ps[:, 2 + b, 0:1]).then_inc(p3_degout, 1)

            @block.gpsimd
            def _(pool):
                with pool.Fori(0, T // 2) as pairt:
                    for b in range(2):
                        pool.wait_ge(p3_copied, (pairt * 2 + (b + 1)) * WPT + 2)
                        blk = ctile[:, b, bass.ds(pairt * 2 + b, 1), :].rearrange("p t n -> p (t n)")
                        pool.tensor_tensor(blk, blk, ident16[:], ALU.add).then_inc(p3_loops, 1)

            @block.sync
            def _(sp):
                with sp.Fori(0, T // 2) as pairt:
                    for b in range(2):
                        sp.wait_ge(p3_loops, pairt * 2 + (b + 1))
                        sp.dma_start(counts_dram[bass.ds(pairt * 2 + b, 1)].rearrange("t p n -> (t p) n"),
                                     ctile[:, b].rearrange("p t n -> p (t n)")).then_inc(p3_stored[b], 16)
                for b in range(2):
                    sp.wait_ge(p3_stored[b], 16 * (T // 2))

        xin = z32(8000, 2 * D).rearrange("p (b n) -> p b n", b=2)
        xn = z32(9024, 2 * D).rearrange("p (b n) -> p b n", b=2)
        ubuf = z32(10048, 2 * D).rearrange("p (b n) -> p b n", b=2)
        junk = z32(11072, D)
        p4_x = [sem(f"p4_x_loaded{b}") for b in range(2)]
        p4_u = [sem(f"p4_mix_stored{b}") for b in range(2)]
        p4_dinv = sem("p4_dinv_ready")
        p4_setup = sem("p4_vector_setup")
        p4_stats = sem("p4_stats")
        p4_aggr = sem("p4_variance_ready")
        p4_var = sem("p4_variance_plus_eps")
        p4_rstd = sem("p4_rstd_ready")
        p4_xn = sem("p4_xn_ready")
        p4_bias = sem("p4_row_bias_done")
        p4_turned = sem("p4_xn_transposed")
        p4_xh = sem("p4_high_parts")
        p4_xl = sem("p4_low_parts")
        p4_w1 = sem("p4_w1_product")
        p4_wvo = sem("p4_wvo_product")
        p4_y1h = sem("p4_y1_high")
        p4_y1l = sem("p4_y1_low")
        p4_ubuf = sem("p4_mix_tile_ready")

        def turn_slots(eng, loop_slot, last):
            with eng.Fori(0, LOOPS) as i:
                for b in range(2):
                    loop_slot(i * 2 + b, b, i)
            last()

        with nc.Block() as block:
            @block.sync
            def _(sp):
                def load(t, b, i):
                    sp.wait_ge(p4_xn, t + 1)
                    sp.dma_start(xin[:, b], x_t[bass.ds(t + 2, 1)].rearrange("t p n -> (t p) n")).then_inc(p4_x[b], 16)

                for b in range(2):
                    sp.dma_start(xin[:, b], x_t[b]).then_inc(p4_x[b], 16)
                turn_slots(sp, load, lambda: None)

            @block.gpsimd
            def _(pool):
                pool.tensor_tensor(dinv[:], deg[:], half[:], ALU.pow).then_inc(p4_dinv, 1)

                def rstd(t, b):
                    pool.wait_ge(p4_var, t + 1)
                    pool.tensor_tensor(xrstd[:, bass.ds(t, 1)], veps[:, b:b + 1], half[:, 0:1], ALU.pow
                                       ).then_inc(p4_rstd, 1)
                with pool.Fori(0, T // 2) as i:
                    for b in range(2):
                        rstd(i * 2 + b, b)

            @block.vector
            def _(dve):
                link = chain(dve, p4_setup)
                dve.wait_ge(p4_dinv, 1)
                link(dve.tensor_scalar(f_y1[:], dinv[:], c(R_W1), None, ALU.mult))
                link(dve.tensor_scalar(f_z1[:], dinv[:], c(R_Y1), None, ALU.mult))
                link(dve.tensor_scalar(f_y2[:], dinv[:], c(R_W2), None, ALU.mult))
                link(dve.tensor_scalar(f_z2[:], dinv[:], c(R_Y2), None, ALU.mult))

                def norm(t, b, i):
                    dve.wait_ge(p4_x[b], i * 16 + 16)
                    dve.bn_stats(stats[:, b], xin[:, b]).then_inc(p4_stats, 1)
                    wait_apart(dve, p4_stats, t + 1, passed)
                    dve.bn_aggr(aggr[:, b], stats[:, b]).then_inc(p4_aggr, 1)
                    dve.wait_ge(p4_aggr, t + 1)
                    dve.tensor_scalar(veps[:, b:b + 1], aggr[:, b, 1:2], EPS, None, ALU.add).then_inc(p4_var, 1)
                    dve.tensor_copy(xmean[:, bass.ds(t, 1)], aggr[:, b, 0:1])
                    dve.wait_ge(p4_rstd, t + 1)
                    dve.wait_ge(p4_turned, t + 1)
                    dve.tensor_scalar(xn[:, b], xin[:, b], aggr[:, b, 0:1], xrstd[:, bass.ds(t, 1)],
                                      ALU.subtract, ALU.mult).then_inc(p4_xn, 1)
                    dve.wait_ge(p4_xn, t + 1)
                    dve.tensor_tensor_reduce(out=junk, in0=xn[:, b], in1=wqbkrow, scale=1.0, scalar=0.0,
                                             op0=ALU.mult, op1=ALU.add, accum_out=xdot[:, b:b + 1]).then_inc(p4_bias, 1)
                    dve.wait_ge(p4_bias, t + 1)
                    dve.tensor_scalar(rowbias[:, bass.ds(t, 1)], xdot[:, b:b + 1], c(BQBK), None, ALU.add)

                def low_parts(t, b):
                    dve.wait_ge(p4_xh, t + 1)
                    at = bass.ds(t * P, P)
                    dve.scalar_tensor_tensor(out=xparts[:, 1, :, at], in0=ps[:, b, :].rearrange("p (k n) -> p k n", k=K),
                                             scalar=XSCALE, in1=xparts[:, 0, :, at], op0=ALU.mult, op1=ALU.subtract
                                             ).then_inc(p4_xl, 1)

                def products(t, b, i):
                    dve.wait_ge(p4_y1h, t + 1)
                    one = bass.ds(t, 1)
                    dve.scalar_tensor_tensor(out=y1[:, one, 1, :].rearrange("p t n -> p (t n)"), in0=ps[:, 2 + b, :],
                                             scalar=f_y1[:, one], in1=y1[:, one, 0, :].rearrange("p t n -> p (t n)"),
                                             op0=ALU.mult, op1=ALU.subtract).then_inc(p4_y1l, 1)
                    dve.wait_ge(p4_wvo, t + 1)
                    dve.wait_ge(p4_u[b], i * 16)
                    dve.scalar_tensor_tensor(out=ubuf[:, b], in0=ps[:, 4 + b, :], scalar=c(F_U), in1=bvorow,
                                             op0=ALU.mult, op1=ALU.add).then_inc(p4_ubuf, 1)

                norm(0, 0, 0)
                norm(1, 1, 0)
                low_parts(0, 0)
                with dve.Fori(0, LOOPS) as i:
                    for b in range(2):
                        norm(i * 2 + (b + 2), b, i + 1)
                        low_parts(i * 2 + (b + 1), 1 - b)
                        products(i * 2 + b, b, i)
                low_parts(T - 1, 1)
                products(T - 2, 0, LOOPS)
                products(T - 1, 1, LOOPS)

            @block.scalar
            def _(act):
                def high_parts(t, b):
                    act.wait_ge(p4_turned, t + 3)
                    act.activation(xparts[:, 0, :, bass.ds(t * P, P)], ps[:, b, :].rearrange("p (k n) -> p k n", k=K),
                                   ACT.Copy, scale=XSCALE).then_inc(p4_xh, 1)

                def y1_high(t, b):
                    act.wait_ge(p4_w1, t + 1)
                    one = bass.ds(t, 1)
                    act.activation(y1[:, one, 0, :].rearrange("p t n -> p (t n)"), ps[:, 2 + b, :], ACT.Copy,
                                   scale=f_y1[:, one]).then_inc(p4_y1h, 1)

                def store_mix(t, b):
                    act.wait_ge(p4_ubuf, t + 3)
                    act.dma_start(mix_dram[bass.ds(t, 1)].rearrange("t p n -> (t p) n"), ubuf[:, b]
                                  ).then_inc(p4_u[b], 16)

                high_parts(0, 0)
                with act.Fori(0, LOOPS) as i:
                    for b in range(2):
                        high_parts(i * 2 + (b + 1), 1 - b)
                        y1_high(i * 2 + b, b)
                        store_mix(i * 2 + b, b)
                high_parts(T - 1, 1)
                for b in range(2):
                    y1_high(T - 2 + b, b)
                    store_mix(T - 2 + b, b)
                for b in range(2):
                    act.wait_ge(p4_u[b], 16 * (T // 2))

            @block.tensor
            def _(pe):
                def turn(t, b, first=False):
                    pe.wait_ge(p4_xn, t + 1)
                    if not first:
                        pe.wait_ge(p4_xl, t - 1)
                    for k in range(K):
                        ins = pe.transpose(ps[:, b, k * P:(k + 1) * P], xn[:, b, k * P:(k + 1) * P], ident[:])
                    ins.then_inc(p4_turned, 1)

                def multiply(t, b):
                    pe.wait_ge(p4_xl, t + 1)
                    at = bass.ds(t * P, P)
                    pe.wait_ge(p4_y1l, t + 1)
                    split_product(pe, ps[:, 2 + b, :], xparts, at, w1parts).then_inc(p4_w1, 1)
                    pe.wait_ge(p4_ubuf, t + 1)
                    split_product(pe, ps[:, 4 + b, :], xparts, at, wvoparts).then_inc(p4_wvo, 1)

                pe.sem_inc(p4_turned, 2)
                pe.sem_inc(p4_y1l, 2)
                pe.sem_inc(p4_ubuf, 2)
                turn(0, 0, True)
                with pe.Fori(0, LOOPS) as i:
                    for b in range(2):
                        turn(i * 2 + (b + 1), 1 - b)
                        multiply(i * 2 + b, b)
                turn(T - 1, 1)
                multiply(T - 2, 0)
                multiply(T - 1, 1)


        score = z32(0, 2 * N).rearrange("p (b n) -> p b n", b=2)
        acc = z32(2 * N, N)
        gparts = z32(3 * N, 1024).bitcast(F16).rearrange("p (b h k n) -> p b h k n", b=2, h=2, k=K)
        cs = deg
        NG = len(GROUPS)
        SB = 4
        p5_g = sem("p5_g_product")
        p5_gb = sem("p5_g_scaled")
        p5_gh = sem("p5_g_high")
        p5_gl = sem("p5_g_low")
        p5_s = sem("p5_scores")
        p5_sc = sem("p5_scores_copied")
        p5_m = sem("p5_softmax_steps")
        p5_nb = sem("p5_bias_ready")
        p5_e = sem("p5_exponentials")
        p5_rz = sem("p5_reciprocal_steps")
        p5_acc = sem("p5_columns_added")
        p5_zero = sem("p5_zeroed")
        p5_col = sem("p5_column_sums")
        p5_fin = sem("p5_final_steps")

        with nc.Block() as block:
            @block.tensor
            def _(pe):
                def g_product(t, b):
                    pe.wait_ge(p5_gl, t + 1)
                    at = bass.ds(t * P, P)
                    for j in range(K):
                        for k in range(K):
                            for l, r in ((0, 0), (0, 1), (1, 0)):
                                ins = pe.matmul(ps[:, b, j * P:(j + 1) * P], mparts[:, l, k, j * P:(j + 1) * P],
                                                xparts[:, r, k, at], start=(k == 0 and l == 0 and r == 0),
                                                stop=(k == K - 1 and l == 1))
                    ins.then_inc(p5_g, 1)

                def scores(t, b):
                    pe.wait_ge(p5_gl, t + 3)
                    for g, (a, n) in enumerate(GROUPS):
                        pe.wait_ge(p5_sc, t * NG + (g + 1))
                        for k in range(K):
                            for l, r in ((0, 0), (0, 1), (1, 0)):
                                ins = pe.matmul(ps[:, 2 + g % SB, 0:n], gparts[:, b, l, k, :], xparts[:, r, k, a:a + n],
                                                start=(k == 0 and l == 0 and r == 0), stop=(k == K - 1 and l == 1))
                        ins.then_inc(p5_s, 1)

                pe.sem_inc(p5_gl, 2)
                pe.sem_inc(p5_sc, SB)
                g_product(0, 0)
                g_product(1, 1)
                scores(0, 0)
                with pe.Fori(0, LOOPS) as i:
                    for b in (1, 0):
                        t = i * 2 + (2 - b)
                        g_product(t + 1, 1 - b)
                        scores(t, b)
                scores(T - 1, 1)
                pe.wait_ge(p5_acc, T + 2)
                for t in range(T):
                    n = min(P, N - t * P)
                    ins = pe.matmul(ps[0:n, 0, t:t + 1], acc[:, t * P:t * P + n], ones[:], start=True, stop=True)
                ins.then_inc(p5_col, 1)

            @block.scalar
            def _(act):
                def g_scale(t, b):
                    act.wait_ge(p5_g, t + 1)
                    for j in range(K):
                        bank = ps[:, b, j * P:(j + 1) * P]
                        ins = act.activation(bank, bank, ACT.Identity, bias=cg[:, 1, j:j + 1], scale=c(F_G))
                    ins.then_inc(p5_gb, 1)

                def exponentials(t, b):
                    act.wait_ge(p5_nb, t + 1)
                    act.activation(score[:, b], score[:, b], ACT.Exp, bias=soft[:, b, 2:3], scale=c(F_S),
                                   accum_out=soft[:, b, 3:4]).then_inc(p5_e, 1)

                g_scale(0, 0)
                g_scale(1, 1)
                exponentials(0, 0)
                with act.Fori(0, LOOPS) as i:
                    for b in (1, 0):
                        t = i * 2 + (2 - b)
                        g_scale(t + 1, 1 - b)
                        exponentials(t, b)
                exponentials(T - 1, 1)

            @block.vector
            def _(dve):
                def g_split(t, b):
                    dve.wait_ge(p5_gb, t + 1)
                    if not isinstance(t, int):
                        dve.wait_ge(p5_s, (t - 1) * NG)
                    bank = ps[:, b, :].rearrange("p (k n) -> p k n", k=K)
                    dve.tensor_copy(gparts[:, b, 0], bank).then_inc(p5_gh, 1)
                    dve.wait_ge(p5_gh, t + 1)
                    dve.tensor_tensor(gparts[:, b, 1], bank, gparts[:, b, 0], ALU.subtract).then_inc(p5_gl, 1)

                def row_maximum(t, b):
                    dve.wait_ge(p5_acc, t + 1)
                    for g, (a, n) in enumerate(GROUPS):
                        dve.wait_ge(p5_s, t * NG + (g + 1))
                        dve.tensor_scalar(score[:, b, a:a + n], ps[:, 2 + g % SB, 0:n], 1.0, None, ALU.mult, ALU.max,
                                          accum_out=mx[:, b, g:g + 1]).then_inc(p5_sc, 1)
                    dve.wait_ge(p5_sc, t * NG + (NG + SB))
                    dve.tensor_reduce(soft[:, b, 0:1], mx[:, b, 0:NG], AX.X, ALU.max).then_inc(p5_m, 1)
                    dve.wait_ge(p5_m, t * 2 + 1)
                    one = bass.ds(t, 1)
                    dve.tensor_scalar(soft[:, b, 1:2], soft[:, b, 0:1], c(F_S), rowbias[:, one], ALU.mult, ALU.add
                                      ).then_inc(p5_m, 1)
                    dve.wait_ge(p5_m, t * 2 + 2)
                    dve.tensor_tensor(soft[:, b, 2:3], rowbias[:, one], soft[:, b, 1:2], ALU.subtract
                                      ).then_inc(p5_nb, 1)

                def add_columns(t, b):
                    dve.wait_ge(p5_e, t + 1)
                    dve.reciprocal(soft[:, b, 4:5], soft[:, b, 3:4]).then_inc(p5_rz, 1)
                    dve.wait_ge(p5_rz, t * 2 + 1)
                    dve.tensor_tensor(soft[:, b, 4:5], soft[:, b, 4:5], rowmask[:, bass.ds(t, 1)], ALU.mult
                                      ).then_inc(p5_rz, 1)
                    dve.wait_ge(p5_rz, t * 2 + 2)
                    dve.wait_ge(p5_acc, t + 2)
                    dve.scalar_tensor_tensor(out=acc, in0=score[:, b], scalar=soft[:, b, 4:5], in1=acc,
                                             op0=ALU.mult, op1=ALU.add).then_inc(p5_acc, 1)

                dve.memset(acc, 0.0).then_inc(p5_zero, 1)
                dve.wait_ge(p5_zero, 1)
                dve.sem_inc(p5_acc, 2)
                g_split(0, 0)
                g_split(1, 1)
                row_maximum(0, 0)
                with dve.Fori(0, LOOPS) as i:
                    for b in (1, 0):
                        t = i * 2 + (2 - b)
                        g_split(t + 1, 1 - b)
                        row_maximum(t, b)
                        add_columns(t - 1, 1 - b)
                row_maximum(T - 1, 1)
                add_columns(T - 2, 0)
                add_columns(T - 1, 1)
                link = chain(dve, p5_fin)
                link(dve.memset(cs[:], 0.0))
                dve.wait_ge(p5_col, 1)
                link(dve.tensor_copy(cs[:, 0:T - 1], ps[:, 0, 0:T - 1]))
                link(dve.tensor_copy(cs[0:N - (T - 1) * P, T - 1:T], ps[0:N - (T - 1) * P, 0, T - 1:T]))
                link(dve.tensor_scalar(mixs[:], cs[:], 1e-9, None, ALU.add))
                link(dve.reciprocal(mixs[:], mixs[:]))
                link(dve.tensor_tensor(mixs[:], mixs[:], cs[:], ALU.mult))

        cbuf = z32(0, NP).bitcast(F16).rearrange("p (b t n) -> p b t n", b=2, t=T)

        def pair_of(at):
            return z32(at, 2 * D).rearrange("p (b n) -> p b n", b=2)

        zbuf = pair_of(3840)

        def load_counts(sp, loaded, used):
            for b in range(2):
                sp.dma_start(cbuf[:, b].rearrange("p t n -> p (t n)"), counts_dram[b]).then_inc(loaded[b], 16)
            with sp.Fori(0, LOOPS) as i:
                for b in range(2):
                    sp.wait_ge(used, i * 2 + (b + 1))
                    sp.dma_start(cbuf[:, b].rearrange("p t n -> p (t n)"),
                                 counts_dram[bass.ds(i * 2 + (b + 2), 1)].rearrange("t p n -> (t p) n")
                                 ).then_inc(loaded[b], 16)

        def aggregate(pe, y, b):
            for i in range(T):
                for h in range(2):
                    ins = pe.matmul(ps[:, b, :], cbuf[:, b, i, :], y[:, i, h, :], start=(i == 0 and h == 0),
                                    stop=(i == T - 1 and h == 1))
            return ins

        hbuf = pair_of(4864)
        hparts = z32(5888, 1024).bitcast(F16).rearrange("p (b h k n) -> p b h k n", b=2, h=2, k=K)
        p6_c = [sem(f"p6_counts_loaded{b}") for b in range(2)]
        p6_agg = sem("p6_aggregated")
        p6_z = sem("p6_z_ready")
        p6_stats = sem("p6_stats")
        p6_aggr = sem("p6_moments")
        p6_var = sem("p6_variance_plus_eps")
        p6_rstd = sem("p6_rstd_ready")
        p6_norm = sem("p6_normalised")
        p6_gam = sem("p6_gamma_applied")
        p6_beta = sem("p6_beta_applied")
        p6_h = sem("p6_h_ready")
        p6_turned = sem("p6_h_transposed")
        p6_hh = sem("p6_h_high")
        p6_hl = sem("p6_h_low")
        p6_w2 = sem("p6_w2_product")
        p6_y2h = sem("p6_y2_high")
        p6_y2l = sem("p6_y2_low")
        rstd6 = wide

        with nc.Block() as block:
            @block.sync
            def _(sp):
                load_counts(sp, p6_c, p6_agg)

            @block.tensor
            def _(pe):
                def agg(t, b, i):
                    pe.wait_ge(p6_c[b], i * 16 + 16)
                    pe.wait_ge(p6_z, t + 1)
                    aggregate(pe, y1, b).then_inc(p6_agg, 1)

                def turn(t, b):
                    pe.wait_ge(p6_h, t + 1)
                    pe.wait_ge(p6_hl, t + 1)
                    for k in range(K):
                        ins = pe.transpose(ps[:, 2 + b, k * P:(k + 1) * P], hbuf[:, b, k * P:(k + 1) * P], ident[:])
                    ins.then_inc(p6_turned, 1)

                def multiply(t, b):
                    pe.wait_ge(p6_hl, t + 3)
                    pe.wait_ge(p6_y2l, t + 1)
                    split_product(pe, ps[:, 4 + b, :], hparts[:, b], slice(0, P), w2parts).then_inc(p6_w2, 1)

                pe.sem_inc(p6_z, 2)
                pe.sem_inc(p6_hl, 2)
                pe.sem_inc(p6_y2l, 2)
                agg(0, 0, 0)
                agg(1, 1, 0)
                with pe.Fori(0, LOOPS) as i:
                    for b in range(2):
                        turn(i * 2 + b, b)
                        agg(i * 2 + (b + 2), b, i + 1)
                        multiply(i * 2 + b, b)
                for b in range(2):
                    turn(T - 2 + b, b)
                    multiply(T - 2 + b, b)

            @block.vector
            def _(dve):
                def norm(t, b):
                    one = bass.ds(t, 1)
                    dve.wait_ge(p6_agg, t + 1)
                    dve.wait_ge(p6_h, t - 1) if not isinstance(t, int) or t > 1 else None
                    dve.scalar_tensor_tensor(out=zbuf[:, b], in0=ps[:, b, :], scalar=f_z1[:, one], in1=rows[:, B1],
                                             op0=ALU.mult, op1=ALU.add).then_inc(p6_z, 1)
                    dve.wait_ge(p6_z, t + 3)
                    dve.bn_stats(stats[:, b], zbuf[:, b]).then_inc(p6_stats, 1)
                    wait_apart(dve, p6_stats, t + 1, passed)
                    dve.bn_aggr(aggr[:, b], stats[:, b]).then_inc(p6_aggr, 1)
                    dve.wait_ge(p6_aggr, t + 1)
                    dve.tensor_scalar(veps[:, b:b + 1], aggr[:, b, 1:2], EPS, None, ALU.add).then_inc(p6_var, 1)
                    dve.wait_ge(p6_rstd, t + 1)
                    dve.tensor_scalar(zbuf[:, b], zbuf[:, b], aggr[:, b, 0:1], rstd6[:, b:b + 1],
                                      ALU.subtract, ALU.mult).then_inc(p6_norm, 1)

                def h_low(t, b):
                    dve.wait_ge(p6_hh, t + 1)
                    dve.scalar_tensor_tensor(out=hparts[:, b, 1], in0=ps[:, 2 + b, :].rearrange("p (k n) -> p k n", k=K),
                                             scalar=c(S_H), in1=hparts[:, b, 0], op0=ALU.mult, op1=ALU.subtract
                                             ).then_inc(p6_hl, 1)

                def y2_low(t, b):
                    one = bass.ds(t, 1)
                    dve.wait_ge(p6_y2h, t + 1)
                    dve.scalar_tensor_tensor(out=y2[:, one, 1, :].rearrange("p t n -> p (t n)"), in0=ps[:, 4 + b, :],
                                             scalar=f_y2[:, one], in1=y2[:, one, 0, :].rearrange("p t n -> p (t n)"),
                                             op0=ALU.mult, op1=ALU.subtract).then_inc(p6_y2l, 1)

                norm(0, 0)
                norm(1, 1)
                with dve.Fori(0, LOOPS) as i:
                    for b in range(2):
                        h_low(i * 2 + b, b)
                        norm(i * 2 + (b + 2), b)
                        y2_low(i * 2 + b, b)
                for b in range(2):
                    h_low(T - 2 + b, b)
                    y2_low(T - 2 + b, b)

            @block.gpsimd
            def _(pool):
                with pool.Fori(0, T // 2) as i:
                    for b in range(2):
                        t = i * 2 + b
                        pool.wait_ge(p6_var, t + 1)
                        pool.tensor_tensor(rstd6[:, b:b + 1], veps[:, b:b + 1], half[:, 0:1], ALU.pow
                                           ).then_inc(p6_rstd, 1)
                        pool.wait_ge(p6_norm, t + 1)
                        pool.tensor_tensor(zbuf[:, b], zbuf[:, b], rows[:, G1], ALU.mult).then_inc(p6_gam, 1)
                        pool.wait_ge(p6_gam, t + 1)
                        pool.tensor_tensor(zbuf[:, b], zbuf[:, b], rows[:, BE1], ALU.add).then_inc(p6_beta, 1)

            @block.scalar
            def _(act):
                def gelu(t, b):
                    act.wait_ge(p6_beta, t + 1)
                    act.wait_ge(p6_turned, t + 1)
                    act.activation(hbuf[:, b], zbuf[:, b], ACT.Gelu).then_inc(p6_h, 1)

                def h_high(t, b):
                    act.wait_ge(p6_turned, t + 3)
                    act.wait_ge(p6_w2, t - 1) if not isinstance(t, int) or t > 1 else None
                    act.activation(hparts[:, b, 0], ps[:, 2 + b, :].rearrange("p (k n) -> p k n", k=K), ACT.Copy,
                                   scale=c(S_H)).then_inc(p6_hh, 1)

                def y2_high(t, b):
                    one = bass.ds(t, 1)
                    act.wait_ge(p6_w2, t + 1)
                    act.activation(y2[:, one, 0, :].rearrange("p t n -> p (t n)"), ps[:, 4 + b, :], ACT.Copy,
                                   scale=f_y2[:, one]).then_inc(p6_y2h, 1)

                act.sem_inc(p6_turned, 2)
                gelu(0, 0)
                h_high(0, 0)
                gelu(1, 1)
                y2_high(0, 0)
                with act.Fori(0, LOOPS) as i:
                    for b in (1, 0):
                        t = i * 2 + (2 - b)
                        h_high(t, b)
                        gelu(t + 1, 1 - b)
                        y2_high(t, b)
                h_high(T - 1, 1)
                y2_high(T - 1, 1)

        xbuf = pair_of(4864)
        ubuf7 = pair_of(5888)
        xnbuf = pair_of(6912)
        dev = pair_of(7936)
        p7_c = [sem(f"p7_counts_loaded{b}") for b in range(2)]
        p7_xu = [sem(f"p7_x_and_mix_loaded{b}") for b in range(2)]
        p7_agg = sem("p7_aggregated")
        p7_z = sem("p7_z_ready")
        p7_stats = sem("p7_stats")
        p7_aggr = sem("p7_moments")
        p7_var = sem("p7_variance_plus_eps")
        p7_rstd = sem("p7_rstd_ready")
        p7_norm = sem("p7_normalised")
        p7_xn = sem("p7_xn_ready")
        p7_mix = sem("p7_mix_steps")
        p7_pre = sem("p7_pool_steps")
        p7_gelu = sem("p7_gelu_done")
        p7_new = sem("p7_new_x_ready")
        p7_nst = sem("p7_new_stats")
        p7_nag = sem("p7_new_moments")
        p7_nvar = sem("p7_new_variance_plus_eps")
        p7_nrstd = sem("p7_new_rstd")
        p7_dev = sem("p7_deviation")
        p7_amax = sem("p7_row_maximum")

        with nc.Block() as block:
            @block.sync
            def _(sp):
                load_counts(sp, p7_c, p7_agg)

            @block.tensor
            def _(pe):
                pe.sem_inc(p7_z, 2)
                with pe.Fori(0, T // 2) as i:
                    for b in range(2):
                        pe.wait_ge(p7_c[b], i * 16 + 16)
                        pe.wait_ge(p7_z, i * 2 + (b + 1))
                        aggregate(pe, y2, b).then_inc(p7_agg, 1)

            @block.scalar
            def _(act):
                act.sem_inc(p7_new, 2)
                with act.Fori(0, T // 2) as i:
                    for b in range(2):
                        t = i * 2 + b
                        one = bass.ds(t, 1)
                        act.wait_ge(p7_new, t + 1)
                        act.dma_start(xbuf[:, b], x_t[one].rearrange("t p n -> (t p) n")).then_inc(p7_xu[b], 16)
                        act.dma_start(ubuf7[:, b], mix_dram[one].rearrange("t p n -> (t p) n")).then_inc(p7_xu[b], 16)
                        act.wait_ge(p7_pre, t * 4 + 3)
                        act.activation(zbuf[:, b], zbuf[:, b], ACT.Gelu).then_inc(p7_gelu, 1)

            @block.vector
            def _(dve):
                def first_half(t, b, i):
                    one = bass.ds(t, 1)
                    dve.wait_ge(p7_xu[b], i * 32 + 32)
                    dve.tensor_scalar(xnbuf[:, b], xbuf[:, b], xmean[:, one], xrstd[:, one], ALU.subtract, ALU.mult
                                      ).then_inc(p7_xn, 1)
                    dve.scalar_tensor_tensor(out=ubuf7[:, b], in0=ubuf7[:, b], scalar=mixs[:, one], in1=rows[:, MIXC],
                                             op0=ALU.mult, op1=ALU.add).then_inc(p7_mix, 1)
                    dve.wait_ge(p7_xn, t + 1)
                    dve.wait_ge(p7_mix, t * 2 + 1)
                    dve.scalar_tensor_tensor(out=ubuf7[:, b], in0=ubuf7[:, b], scalar=0.0, in1=xnbuf[:, b],
                                             op0=ALU.max, op1=ALU.add).then_inc(p7_mix, 1)
                    dve.wait_ge(p7_agg, t + 1)
                    dve.scalar_tensor_tensor(out=zbuf[:, b], in0=ps[:, b, :], scalar=f_z2[:, one], in1=rows[:, B2],
                                             op0=ALU.mult, op1=ALU.add).then_inc(p7_z, 1)
                    dve.wait_ge(p7_z, t + 3)
                    dve.bn_stats(stats[:, b], zbuf[:, b]).then_inc(p7_stats, 1)
                    wait_apart(dve, p7_stats, t + 1, passed)
                    dve.bn_aggr(aggr[:, b], stats[:, b]).then_inc(p7_aggr, 1)
                    dve.wait_ge(p7_aggr, t + 1)
                    dve.tensor_scalar(veps[:, b:b + 1], aggr[:, b, 1:2], EPS, None, ALU.add).then_inc(p7_var, 1)
                    dve.wait_ge(p7_rstd, t + 1)
                    dve.tensor_scalar(zbuf[:, b], zbuf[:, b], aggr[:, b, 0:1], rstd6[:, b:b + 1],
                                      ALU.subtract, ALU.mult).then_inc(p7_norm, 1)

                def second_half(t, b):
                    one = bass.ds(t, 1)
                    new = xnew[:, one, :].rearrange("p t n -> p (t n)")
                    dve.wait_ge(p7_gelu, t + 1)
                    dve.wait_ge(p7_pre, t * 4 + 4)
                    dve.tensor_tensor(new, ubuf7[:, b], zbuf[:, b], ALU.add).then_inc(p7_new, 1)
                    wait_apart(dve, p7_new, t + 3, passed)
                    dve.bn_stats(nst[:, b], new).then_inc(p7_nst, 1)
                    wait_apart(dve, p7_nst, t + 1, passed)
                    dve.bn_aggr(nag[:, b], nst[:, b]).then_inc(p7_nag, 1)
                    dve.wait_ge(p7_nag, t + 1)
                    dve.tensor_copy(nmean[:, one], nag[:, b, 0:1])
                    dve.tensor_scalar(nveps[:, b:b + 1], nag[:, b, 1:2], EPS, None, ALU.add).then_inc(p7_nvar, 1)
                    dve.wait_ge(p7_nrstd, t + 1)
                    dve.tensor_scalar(dev[:, b], new, nag[:, b, 0:1], nrstd[:, one], ALU.subtract, ALU.mult
                                      ).then_inc(p7_dev, 1)
                    dve.wait_ge(p7_dev, t + 1)
                    dve.tensor_reduce(namax[:, one], dev[:, b], AX.X, ALU.max, apply_absolute_value=True
                                      ).then_inc(p7_amax, 1)

                first_half(0, 0, 0)
                first_half(1, 1, 0)
                second_half(0, 0)
                with dve.Fori(0, LOOPS) as i:
                    for b in range(2):
                        first_half(i * 2 + (b + 2), b, i + 1)
                        second_half(i * 2 + (b + 1), 1 - b)
                second_half(T - 1, 1)

            @block.gpsimd
            def _(pool):
                def first_half(t, b):
                    pool.wait_ge(p7_var, t + 1)
                    pool.tensor_tensor(rstd6[:, b:b + 1], veps[:, b:b + 1], half[:, 0:1], ALU.pow).then_inc(p7_rstd, 1)
                    pool.wait_ge(p7_norm, t + 1)
                    pool.tensor_tensor(zbuf[:, b], zbuf[:, b], rows[:, G2], ALU.mult).then_inc(p7_pre, 1)
                    pool.wait_ge(p7_pre, t * 4 + 1)
                    pool.tensor_tensor(zbuf[:, b], zbuf[:, b], rows[:, BE2], ALU.add).then_inc(p7_pre, 1)
                    pool.wait_ge(p7_pre, t * 4 + 2)
                    pool.tensor_tensor(zbuf[:, b], zbuf[:, b], xnbuf[:, b], ALU.add).then_inc(p7_pre, 1)
                    pool.wait_ge(p7_mix, t * 2 + 2)
                    pool.tensor_tensor(ubuf7[:, b], ubuf7[:, b], xbuf[:, b], ALU.add).then_inc(p7_pre, 1)

                def second_half(t, b):
                    pool.wait_ge(p7_nvar, t + 1)
                    pool.tensor_tensor(nrstd[:, bass.ds(t, 1)], nveps[:, b:b + 1], half[:, 0:1], ALU.pow
                                       ).then_inc(p7_nrstd, 1)

                first_half(0, 0)
                first_half(1, 1)
                second_half(0, 0)
                with pool.Fori(0, LOOPS) as i:
                    for b in range(2):
                        first_half(i * 2 + (b + 2), b)
                        second_half(i * 2 + (b + 1), 1 - b)
                second_half(T - 1, 1)

        q32 = pair_of(0)
        qpow = pair_of(1024)
        qbf = z32(2048, D).bitcast(BF16).rearrange("p (b n) -> p b n", b=2)
        qT = z32(2560, D).bitcast(BF16).rearrange("p (b k n) -> p b k n", b=2, k=K)
        obuf = pair_of(3072)
        p8_setup = sem("p8_setup_steps")
        p8_max = sem("p8_maximum_ready")
        p8_all = sem("p8_maximum_over_partitions")
        p8_q = sem("p8_quantise_steps")
        p8_big = sem("p8_rounding_added")
        p8_qbf = sem("p8_rounded")
        p8_turned = sem("p8_transposed")
        p8_qt = sem("p8_transposes_copied")
        p8_mm = sem("p8_products")
        p8_o = sem("p8_outputs_ready")
        p8_out = [sem(f"p8_outputs_stored{b}") for b in range(2)]
        QS = 5

        with nc.Block() as block:
            @block.gpsimd
            def _(pool):
                pool.wait_ge(p8_max, 1)
                pool.partition_all_reduce(c(A_X), c(TMP), P, RMAX).then_inc(p8_all, 1)
                with pool.Fori(0, T // 2) as i:
                    for b in range(2):
                        t = i * 2 + b
                        pool.wait_ge(p8_q, t * QS + QS)
                        pool.tensor_tensor(q32[:, b], q32[:, b], qpow[:, b], ALU.add).then_inc(p8_big, 1)

            @block.vector
            def _(dve):
                link = chain(dve, p8_setup)
                link(dve.tensor_tensor(namax[:], namax[:], rowmask[:], ALU.mult))
                dve.tensor_reduce(c(TMP), namax[:], AX.X, ALU.max).then_inc(p8_max, 1)
                dve.wait_ge(p8_all, 1)
                link(dve.tensor_scalar(c(TMP), c(A_X), 1e-12, None, ALU.max))
                link(dve.reciprocal(c(TMP2), c(TMP)))
                link(dve.tensor_scalar(c(X_SC), c(TMP2), FP8_MAX, None, ALU.mult))
                link(dve.reciprocal(c(TMP), c(X_SC)))
                link(dve.reciprocal(c(TMP2), c(W_SC)))
                link(dve.tensor_tensor(c(X_F), c(TMP), c(TMP2), ALU.mult))

                def quantise(t, b):
                    one = bass.ds(t, 1)
                    new = xnew[:, one, :].rearrange("p t n -> p (t n)")
                    dve.wait_ge(p8_qbf, t - 1) if not isinstance(t, int) or t > 1 else None
                    n = t * QS
                    dve.tensor_scalar(q32[:, b], new, nmean[:, one], nrstd[:, one], ALU.subtract, ALU.mult
                                      ).then_inc(p8_q, 1)
                    dve.wait_ge(p8_q, n + 1)
                    dve.tensor_scalar(q32[:, b], q32[:, b], c(X_SC), FP8_MAX, ALU.mult, ALU.min).then_inc(p8_q, 1)
                    dve.wait_ge(p8_q, n + 2)
                    dve.tensor_scalar(q32[:, b], q32[:, b], -FP8_MAX, None, ALU.max).then_inc(p8_q, 1)
                    dve.wait_ge(p8_q, n + 3)
                    dve.tensor_scalar(qpow[:, b].bitcast(I32), q32[:, b].bitcast(I32), EXPONENT, None,
                                      ALU.bitwise_and).then_inc(p8_q, 1)
                    dve.wait_ge(p8_q, n + 4)
                    dve.tensor_scalar(qpow[:, b], qpow[:, b], 2.0 ** -6, 1.5 * 2.0 ** 20, ALU.max, ALU.mult
                                      ).then_inc(p8_q, 1)

                def rounded(t, b):
                    dve.wait_ge(p8_big, t + 1)
                    dve.wait_ge(p8_turned, t + 1)
                    dve.tensor_tensor(qbf[:, b], q32[:, b], qpow[:, b], ALU.subtract).then_inc(p8_qbf, 1)

                def output(t, b, i):
                    dve.wait_ge(p8_mm, t + 1)
                    dve.wait_ge(p8_out[b], i * 16)
                    dve.scalar_tensor_tensor(out=obuf[:, b], in0=ps[:, 2 + b, :], scalar=c(X_F),
                                             in1=xnew[:, bass.ds(t, 1), :].rearrange("p t n -> p (t n)"),
                                             op0=ALU.mult, op1=ALU.add).then_inc(p8_o, 1)

                quantise(0, 0)
                quantise(1, 1)
                rounded(0, 0)
                with dve.Fori(0, LOOPS) as i:
                    for b in range(2):
                        quantise(i * 2 + (b + 2), b)
                        rounded(i * 2 + (b + 1), 1 - b)
                        output(i * 2 + b, b, i)
                rounded(T - 1, 1)
                for b in range(2):
                    output(T - 2 + b, b, LOOPS)

            @block.tensor
            def _(pe):
                def turn(t, b):
                    pe.wait_ge(p8_qbf, t + 1)
                    pe.wait_ge(p8_qt, t + 1)
                    bank = ps[:, b, 0:D // 2].bitcast(BF16)
                    for k in range(K):
                        ins = pe.transpose(bank[:, k * P:(k + 1) * P], qbf[:, b, k * P:(k + 1) * P], identb[:])
                    ins.then_inc(p8_turned, 1)

                def multiply(t, b):
                    pe.wait_ge(p8_qt, t + 3)
                    pe.wait_ge(p8_o, t + 1)
                    for k in range(K):
                        ins = pe.matmul(ps[:, 2 + b, :], qT[:, b, k, :], wffn[:, k, :], start=(k == 0), stop=(k == K - 1))
                    ins.then_inc(p8_mm, 1)

                pe.sem_inc(p8_qt, 2)
                pe.sem_inc(p8_o, 2)
                pe.sem_inc(p8_turned, 2)
                turn(0, 0)
                with pe.Fori(0, LOOPS) as i:
                    for b in range(2):
                        turn(i * 2 + (b + 1), 1 - b)
                        multiply(i * 2 + b, b)
                turn(T - 1, 1)
                multiply(T - 2, 0)
                multiply(T - 1, 1)

            @block.scalar
            def _(act):
                with act.Fori(0, T // 2) as i:
                    for b in range(2):
                        t = i * 2 + b
                        act.wait_ge(p8_turned, t + 3)
                        act.wait_ge(p8_o, t + 1)
                        act.copy(qT[:, b].rearrange("p k n -> p (k n)"), ps[:, b, 0:D // 2].bitcast(BF16)
                                 ).then_inc(p8_qt, 1)

            @block.sync
            def _(sp):
                with sp.Fori(0, T // 2) as i:
                    for b in range(2):
                        t = i * 2 + b
                        sp.wait_ge(p8_o, t + 3)
                        sp.dma_start(out_t[bass.ds(t, 1)].rearrange("t p n -> (t p) n"), obuf[:, b]
                                     ).then_inc(p8_out[b], 16)
                for b in range(2):
                    sp.wait_ge(p8_out[b], 16 * (T // 2))


_VECTORS = {"b1": "L0_gnn_b1", "g1": "L0_gnn_gamma1", "be1": "L0_gnn_beta1", "b2": "L0_gnn_b2",
            "g2": "L0_gnn_gamma2", "be2": "L0_gnn_beta2", "bq": "L0_mix_bq", "bk": "L0_mix_bk", "bv": "L0_mix_bv",
            "bo": "L0_mix_bo", "scale": "L0_mix_bn_scale", "bias": "L0_mix_bn_bias", "mean": "L0_mix_bn_mean",
            "var": "L0_mix_bn_var"}
_MATRICES = {"Wq": "L0_mix_Wq", "Wk": "L0_mix_Wk", "Wv": "L0_mix_Wv", "Wo": "L0_mix_Wo", "W1": "L0_gnn_W1",
             "W2": "L0_gnn_W2", "Wf": "L0_ffn_weight"}


def kernel(**inputs):
    import numpy as np
    import concourse.bacc as bacc
    from concourse import mybir as mb
    from concourse.bass_utils import run_bass_kernel_spmd as run

    nc = bacc.Bacc("TRN2", target_bir_lowering=False, num_devices=1)
    x = np.zeros((NP, D), np.asarray(inputs["x"]).dtype)
    x[:N] = inputs["x"]
    src, dst = np.asarray(inputs["src"]), np.asarray(inputs["dst"])
    edges = np.zeros(((CH + 1), 2, P), src.dtype)
    edges[:, 1] = 2 * NP
    for v, a in enumerate((src, dst)):
        full = E // P
        edges[:full, v] = a[:full * P].reshape(full, P)
        edges[full, v, :E - full * P] = a[full * P:]
    arrays = {"in_x": x, "in_edges": edges}
    for short, name in {**_VECTORS, **_MATRICES}.items():
        arrays["in_" + short] = np.ascontiguousarray(inputs[name])
    aps = {k: nc.dram_tensor(k, v.shape, mb.dt.from_np(v.dtype), kind="ExternalInput").ap() for k, v in arrays.items()}
    out = nc.dram_tensor("out", (NP, D), mb.dt.float32, kind="ExternalOutput").ap()
    gps_layer_kernel(nc, aps["in_x"], aps["in_edges"], {k[3:]: v for k, v in aps.items()}, out)
    r = run(nc, [arrays], core_ids=[0])
    return r.results[0]["out"][:N]
```

```python
from contextlib import ExitStack

import concourse.bass as bass
from concourse import mybir

ALU = mybir.AluOpType
ACT = mybir.ActivationFunctionType
AX = mybir.AxisListType
F32 = mybir.dt.float32
F16 = mybir.dt.float16
BF16 = mybir.dt.bfloat16
I32 = mybir.dt.int32
RMAX = bass.bass_isa.ReduceOp.max
RADD = bass.bass_isa.ReduceOp.add

P = 128
N = 3750
D = 512
K = D // P
T = -(-N // P)
NP = T * P
E = 123750
CH = -(-E // P)
WIN = 8
WPT = P // WIN
NWIN = T * WPT
SPAN = 4
POOL_SPAN = 2
CODES = T * WIN
QW = 4
PW = NWIN // QW
GROUPS = [(g, min(512, N - g)) for g in range(0, N, 512)]
FAR = 16384.0
XSCALE = 1024.0
ROOT_D = 22.7
TOP = 32768.0
EXPONENT = 0x7F800000
FP8_MAX = 448.0
EPS = 1e-5
LOOPS = (T - 2) // 2

B1, G1, BE1, B2, G2, BE2, MIXC = range(7)
WQ, WK, WV, WO, W1, W2, WF = range(7)
(A_W1, A_W2, A_M, A_WVO, A_C, A_FFN, A_G1, A_BE1, S_W1, S_W2, S_M, S_WVO, S_G, S_Y1, S_H, S_Y2,
 F_G, F_S, F_U, R_Y1, R_Y2, R_H, R_W1, R_W2, X_SC, X_F, W_SC, TMP, TMP2, BQBK, A_X, R_WVO) = range(32)


def wait_apart(eng, s, value, passed):
    eng.wait_ge(s, value)
    eng.sem_inc(passed, 1)


def split_weight(dve, parts, raw, scale, link):
    link(dve.tensor_scalar(parts[:, 0], raw, scale, None, ALU.mult))
    link(dve.scalar_tensor_tensor(out=parts[:, 1], in0=raw, scalar=scale, in1=parts[:, 0],
                                  op0=ALU.mult, op1=ALU.subtract))


def split_product(pe, out, lhs, at, rhs):
    for k in range(K):
        for l, r in ((0, 0), (0, 1), (1, 0)):
            ins = pe.matmul(out, lhs[:, l, k, at], rhs[:, r, k, :], start=(k == 0 and l == 0 and r == 0),
                            stop=(k == K - 1 and l == 1))
    return ins


def gps_layer_kernel(nc, x, edges, w, out):
    counts_dram = nc.dram_tensor("counts_dram", [T, P, NP], F16).ap()
    low_counts_dram = nc.dram_tensor("low_counts_dram", [T, P, NP], F16).ap()
    mix_dram = nc.dram_tensor("mix_dram", [T, P, D], F32).ap()
    x_t = x.rearrange("(t p) d -> t p d", p=P)
    out_t = out.rearrange("(t p) d -> t p d", p=P)

    ctx = ExitStack()
    with ctx:
        def sb(name, shape, dt=F32):
            return ctx.enter_context(nc.sbuf_tensor(name, shape, dt))

        def sem(name):
            return ctx.enter_context(nc.semaphore(name))

        regionA = sb("regionA", [P, T * D])
        regionB = sb("regionB", [P, T * D])
        regionZ = sb("regionZ", [P, 12376])
        mparts = sb("mparts", [P, 2, K, D], F16)
        w12parts = sb("w12parts", [P, 2, K, D], F16)
        wffn = sb("wffn", [P, K, D], BF16)
        rows = sb("rows", [P, 7, D])
        ident = sb("ident", [P, P])
        ident16 = sb("ident16", [P, P], F16)
        identb = sb("identb", [P, P], BF16)
        col16 = sb("col16", [P, D], F16)
        ones = sb("ones", [P, 1])
        ones16 = sb("ones16", [P, 1], F16)
        half = sb("half", [P, T])
        rowmask = sb("rowmask", [P, T])
        deg = sb("deg", [P, T])
        cs = sb("cs", [P, T])
        missed = sb("missed", [P, 2])
        recount = sb("recount", [P, 1], I32)
        dinv = sb("dinv", [P, T])
        xmean = sb("xmean", [P, T])
        xrstd = sb("xrstd", [P, T])
        rowbias = sb("rowbias", [P, T])
        mixs = sb("mixs", [P, T])
        nmean = sb("nmean", [P, T])
        nrstd = sb("nrstd", [P, T])
        namax = sb("namax", [P, T])
        f_y1 = sb("f_y1", [P, T])
        f_z1 = sb("f_z1", [P, T])
        f_y2 = sb("f_y2", [P, T])
        f_z2 = sb("f_z2", [P, T])
        sc = sb("sc", [P, 32])
        wide = sb("wide", [P, 8])
        cg = sb("cg", [P, 2, K])
        stats = sb("stats", [P, 2, 6])
        nst = sb("nst", [P, 2, 6])
        nag = sb("nag", [P, 2, 2])
        nveps = sb("nveps", [P, 2])
        aggr = sb("aggr", [P, 2, 2])
        veps = sb("veps", [P, 2])
        xdot = sb("xdot", [P, 2])
        mx = sb("mx", [P, 2, 8])
        soft = sb("soft", [P, 2, 5])
        bcols = sb("bcols", [P, 4, K])
        ps = ctx.enter_context(nc.psum_tensor("ps", [P, 8, 512], F32))

        xparts = regionA[:, :].bitcast(F16).rearrange("p (h k n) -> p h k n", h=2, k=K)
        y1 = regionB[:, :].bitcast(F16).rearrange("p (t h n) -> p t h n", t=T, h=2)
        y2 = regionA[:, :].bitcast(F16).rearrange("p (t h n) -> p t h n", t=T, h=2)
        xnew = regionB[:, :].rearrange("p (t n) -> p t n", t=T)

        def z32(at, n):
            return regionZ[:, at:at + n]

        def c(i):
            return sc[:, i:i + 1]

        passed = sem("waits_passed")


        wvoparts = z32(0, 2048).bitcast(F16).rearrange("p (h k n) -> p h k n", h=2, k=K)
        bvorow = z32(2048, D)
        wqbkrow = z32(2560, D)
        wtmp = z32(3072, K * D).rearrange("p (k n) -> p k n", k=K)
        wpow = z32(5120, K * D).rearrange("p (k n) -> p k n", k=K)
        NJ = QW * SPAN
        NE = NJ * P
        tables = regionZ[0:PW, 7168:7168 + 2 * NE].bitcast(I32).rearrange("p (j v e) -> p j v e", j=NJ, v=2)
        t_src, t_dst = tables[:, :, 0, :], tables[:, :, 1, :]
        lastdst = regionZ[0:1, 3072:3072 + CH]
        lastdst_f = regionZ[0:1, 4096:4096 + CH]
        behind = z32(5120, 512)
        wraw = regionA[:, 0:7 * K * D].rearrange("p (w k n) -> p w k n", w=7, k=K)
        reps = regionA[:, 7 * K * D:7 * K * D + 2 * D].rearrange("p (b k n) -> p b k n", b=2, k=K)

        def etab(i, dt=F32):
            return regionA[0:PW, i * NE:(i + 1) * NE].bitcast(dt).rearrange("p (j e) -> p j e", j=NJ)

        wt = regionB[:, 0:3 * K * D].rearrange("p (w k n) -> p w k n", w=3, k=K)
        mraw = regionB[:, 3 * K * D:4 * K * D].rearrange("p (k n) -> p k n", k=K)
        wvoraw = regionB[:, 4 * K * D:5 * K * D].rearrange("p (k n) -> p k n", k=K)
        reps2 = regionB[:, 5 * K * D:5 * K * D + D].rearrange("p (k n) -> p k n", k=K)
        vardiag = regionB[:, 10752:10752 + D].rearrange("p (k n) -> p k n", k=K)
        onesq = regionB[:, 11264:11264 + P]
        onerow = regionB[0:1, 11392:11392 + P]
        mixrows = regionB[:, 12800:12800 + 4 * D].rearrange("p (r n) -> p r n", r=4)
        BO, MEAN, SCALE, BIAS = range(4)
        BQ, BK, BV, VAR = range(4)
        rep = [reps[:, 0], reps[:, 1], reps2]
        code = regionB[:, 0:SPAN * NWIN].rearrange("p (s w) -> p s w", s=SPAN)
        low = regionB[:, SPAN * NWIN:2 * SPAN * NWIN].rearrange("p (s w) -> p s w", s=SPAN)

        lowcols = sb("lowcols", [P, 2, POOL_SPAN, 1])
        thr = sb("thr", [P, QW])
        starts = sb("starts", [P, QW, 3])
        chunkf = sb("chunkf", [P, NJ])
        chunki = sb("chunki", [P, NJ], I32)

        wsem = [sem(f"weight_loaded{i}") for i in range(7)]
        rows_loaded = sem("rows_loaded")
        mixrows_loaded = sem("mix_rows_loaded")
        cols_loaded = sem("bias_columns_loaded")
        last_loaded = sem("last_destinations_loaded")
        p1_const = sem("p1_constants")
        p1_zeroed = sem("p1_zeroed")
        p1_lastf = sem("p1_last_destinations_float")
        p1_rep = sem("p1_last_destinations_repeated")
        p1_vec = sem("p1_vector_steps")
        p1_chunks = sem("p1_chunks_of_windows")
        p1_gathered = sem("p1_edges_gathered")
        p1_coded = sem("p1_edges_coded")
        p1_turned = sem("p1_codes_transposed")
        p1_kept = sem("p1_codes_kept")
        p2_rep = sem("p2_bias_columns_repeated")
        p2_turned = sem("p2_weights_transposed")
        p2_turned_out = sem("p2_transposes_copied")
        p2_made = sem("p2_products_made")
        p2_out = sem("p2_products_copied")
        p2_vec = sem("p2_vector_steps")
        p2_var = sem("p2_variance_ready")
        p2_root = sem("p2_root_ready")
        p2_diag = sem("p2_root_diagonal_ready")
        p2_max = sem("p2_maxima_ready")
        p2_all = sem("p2_maxima_over_partitions")

        def chain(eng, s, start=0):
            n = [start]

            def link(ins):
                n[0] += 1
                ins.then_inc(s, 1)
                eng.wait_ge(s, n[0])
            return link

        with nc.Block() as block:
            @block.sync
            def _(sp):
                with nc.allow_non_contiguous_dma(reason="one word of each chunk, 967 in all"):
                    sp.dma_start(lastdst.bitcast(I32), edges[0:CH, 1, P - 1:P].rearrange("c e -> e c")
                                 ).then_inc(last_loaded, 16)
                with nc.allow_non_contiguous_dma(reason="four vectors of 512 words down the partitions"):
                    for r, name in enumerate(("bq", "bk", "bv", "var")):
                        sp.dma_start(bcols[:, r], w[name].rearrange("(k p) -> p k", p=P)).then_inc(cols_loaded, 16)
                for i, name in ((WQ, "Wq"), (WK, "Wk"), (WV, "Wv"), (WO, "Wo"), (W1, "W1"), (W2, "W2"), (WF, "Wf")):
                    sp.dma_start(wraw[:, i], w[name].rearrange("(k p) n -> p k n", p=P)).then_inc(wsem[i], 16)
                for r, name in ((BO, "bo"), (MEAN, "mean"), (SCALE, "scale"), (BIAS, "bias")):
                    sp.dma_start(mixrows[:, r], w[name].rearrange("(a n) -> a n", a=1).to_broadcast([P, D])
                                 ).then_inc(mixrows_loaded, 16)
                for r, name in ((B1, "b1"), (G1, "g1"), (BE1, "be1"), (B2, "b2"), (G2, "g2"), (BE2, "be2")):
                    sp.dma_start(rows[:, r], w[name].rearrange("(a n) -> a n", a=1).to_broadcast([P, D])
                                 ).then_inc(rows_loaded, 16)

            @block.gpsimd
            def _(pool):
                pool.memset(ident[:], 0.0).then_inc(p1_zeroed, 1)
                pool.memset(ident16[:], 0.0).then_inc(p1_zeroed, 1)
                pool.memset(identb[:], 0.0).then_inc(p1_zeroed, 1)
                pool.memset(rowmask[:], 1.0).then_inc(p1_zeroed, 1)
                pool.iota(thr[:], pattern=[[WIN * PW, QW]], base=0, channel_multiplier=WIN,
                          allow_small_or_imprecise_dtypes=True).then_inc(p1_const, 1)
                pool.memset(onerow, 1.0).then_inc(p1_const, 1)
                pool.memset(half[:], -0.5).then_inc(p1_const, 1)
                pool.wait_ge(p1_zeroed, 4)
                for t in (ident, ident16, identb):
                    pool.affine_select(out=t[:], in_=t[:], compare_op=ALU.not_equal, fill=1.0, base=0,
                                       pattern=[[-1, P]], channel_multiplier=1).then_inc(p1_const, 1)
                pool.affine_select(out=rowmask[:], in_=rowmask[:], compare_op=ALU.is_gt, fill=0.0, base=N,
                                   pattern=[[-P, T]], channel_multiplier=-1).then_inc(p1_const, 1)
                pool.iota(col16[:], pattern=[[1, D]], base=0, channel_multiplier=0,
                          allow_small_or_imprecise_dtypes=True).then_inc(p1_const, 1)
                pool.memset(ones[:], 1.0).then_inc(p1_const, 1)
                pool.memset(ones16[:], 1.0).then_inc(p1_const, 1)
                pool.wait_ge(p1_const, 10)
                pool.wait_ge(p2_var, 1)
                pool.tensor_tensor(bcols[:, VAR], bcols[:, VAR], half[:, 0:K], ALU.pow).then_inc(p2_root, 1)
                pool.wait_ge(p1_chunks, 1)
                for j in range(NJ):
                    pool.indirect_dma_start(
                        out=tables[:, j].rearrange("p v e -> p (v e)"), out_offset=None,
                        in_=edges.rearrange("c v e -> c (v e)"),
                        in_offset=bass.IndirectOffsetOnAxis(ap=chunki[0:PW, j:j + 1], axis=0),
                    ).then_inc(p1_gathered, 16)
                pool.wait_ge(p2_max, 1)
                pool.partition_all_reduce(sc[:, 0:8], wide[:], P, RMAX).then_inc(p2_all, 1)

            @block.tensor
            def _(pe):
                pe.wait_ge(p1_const, 10)
                pe.wait_ge(p1_lastf, 1)
                pe.matmul(ps[:, 0, 0:512], onerow, lastdst_f[:, 0:512], start=True, stop=True)
                pe.matmul(ps[:, 1, 0:CH - 512], onerow, lastdst_f[:, 512:CH], start=True, stop=True
                          ).then_inc(p1_rep, 1)
                pe.wait_ge(p1_chunks, 1)
                for j in range(3 * K):
                    m, i = divmod(j, K)
                    if i == 0:
                        pe.wait_ge(wsem[m], 16)
                    if j >= 8:
                        pe.wait_ge(p2_turned_out, j - 7)
                    for a in range(K):
                        ins = pe.transpose(ps[:, j % 8, a * P:(a + 1) * P], wraw[:, m, a, i * P:(i + 1) * P], ident[:])
                    ins.then_inc(p2_turned, 1)
                pe.wait_ge(p2_turned_out, 3 * K)
                for a in range(K):
                    for i in range(K):
                        ins = pe.matmul(ps[:, a, :], wt[:, WQ, i, a * P:(a + 1) * P], wt[:, WK, i, :],
                                        start=(i == 0), stop=(i == K - 1))
                    ins.then_inc(p2_made, 1)
                pe.wait_ge(wsem[WO], 16)
                for a in range(K):
                    for i in range(K):
                        ins = pe.matmul(ps[:, 4 + a, :], wt[:, WV, i, a * P:(a + 1) * P], wraw[:, WO, i, :],
                                        start=(i == 0), stop=(i == K - 1))
                    ins.then_inc(p2_made, 1)
                pe.wait_ge(p2_diag, 1)
                pe.wait_ge(p2_out, 1)
                for k in range(K):
                    ins = pe.matmul(ps[:, 0, k * P:(k + 1) * P], onesq, vardiag[:, k], start=True, stop=True)
                ins.then_inc(p2_made, 1)
                pe.wait_ge(p2_out, 2)
                pe.wait_ge(p2_rep, 1)
                for i in range(K):
                    ins = pe.matmul(ps[:, 1, :], rep[BK][:, i], wt[:, WQ, i, :], start=(i == 0), stop=(i == K - 1))
                ins.then_inc(p2_made, 1)
                pe.wait_ge(p2_out, 3)
                for i in range(K):
                    ins = pe.matmul(ps[:, 2, :], rep[BV][:, i], wraw[:, WO, i, :], start=(i == 0), stop=(i == K - 1))
                ins.then_inc(p2_made, 1)
                pe.wait_ge(p2_out, 4)
                for b in range(K):
                    for i in range(K):
                        ins = pe.matmul(ps[:, 3, b:b + 1], wt[:, WK, i, b * P:(b + 1) * P], bcols[:, BQ, i:i + 1],
                                        start=(i == 0), stop=(i == K - 1))
                for i in range(K):
                    ins = pe.matmul(ps[:, 3, K:K + 1], rep[BQ][:, i], bcols[:, BK, i:i + 1],
                                    start=(i == 0), stop=(i == K - 1))
                ins.then_inc(p2_made, 1)
                pe.wait_ge(p1_coded, 1)
                for j in range(NJ):
                    if j >= 3:
                        pe.wait_ge(p1_kept, j - 2)
                    b = 2 + 2 * (j % 3)
                    pe.transpose(ps[:, b, 0:PW], etab(2)[:, j], ident[0:PW, 0:PW])
                    pe.transpose(ps[:, b + 1, 0:PW], etab(0)[:, j], ident[0:PW, 0:PW]).then_inc(p1_turned, 1)

            @block.scalar
            def _(act):
                for j in range(3 * K):
                    m, i = divmod(j, K)
                    act.wait_ge(p2_turned, j + 1)
                    act.copy(wt[:, m, i, :], ps[:, j % 8, :]).then_inc(p2_turned_out, 1)

            @block.vector
            def _(dve):
                link = chain(dve, p1_vec)
                dve.wait_ge(last_loaded, 16)
                dve.tensor_copy(lastdst_f, lastdst.bitcast(I32)).then_inc(p1_lastf, 1)
                dve.wait_ge(cols_loaded, 16 * 4)
                dve.tensor_scalar(bcols[:, VAR], bcols[:, VAR], EPS, None, ALU.add).then_inc(p2_var, 1)
                dve.wait_ge(p1_const, 10)
                dve.wait_ge(p1_rep, 1)
                for g in range(QW):
                    for h, (a, n) in enumerate(((0, 512), (512, CH - 512))):
                        link(dve.tensor_scalar(behind[:, 0:n], ps[:, h, 0:n], thr[:, g:g + 1], None, ALU.is_lt,
                                               ALU.add, accum_out=starts[:, g, h:h + 1]))
                    link(dve.tensor_tensor(starts[:, g, 2:3], starts[:, g, 0:1], starts[:, g, 1:2], ALU.add))
                    for s in range(SPAN):
                        ins = dve.tensor_scalar(chunkf[:, g * SPAN + s:g * SPAN + s + 1], starts[:, g, 2:3],
                                                float(s), float(CH), ALU.add, ALU.min)
                    link(ins)
                dve.tensor_copy(chunki[:], chunkf[:]).then_inc(p1_chunks, 1)

                link = chain(dve, p2_vec)
                dve.wait_ge(p1_chunks, 1)
                link(dve.memset(wtmp[:, 1:3], 1.0))
                for b in range(3):
                    for i in range(K):
                        ins = dve.tensor_scalar(rep[b][:, i], wtmp[:, 1, 0:P], bcols[:, b, i:i + 1], None, ALU.mult)
                link(ins)
                dve.sem_inc(p2_rep, 1)
                dve.wait_ge(p2_root, 1)
                for k in range(K):
                    ins = dve.tensor_scalar(vardiag[:, k], ident[:], bcols[:, VAR, k:k + 1], None, ALU.mult)
                link(ins)
                dve.memset(onesq, 1.0).then_inc(p2_diag, 1)
                dve.wait_ge(mixrows_loaded, 16 * 4)
                for a in range(K):
                    dve.wait_ge(p2_made, a + 1)
                    dve.tensor_copy(mraw[:, a, :], ps[:, a, :]).then_inc(p2_out, 1)
                dve.wait_ge(p2_made, 2 * K + 1)
                link(dve.tensor_tensor(mixrows[:, SCALE], mixrows[:, SCALE], ps[:, 0, :], ALU.mult))
                link(dve.tensor_tensor(mixrows[:, BO], mixrows[:, BO], mixrows[:, MEAN], ALU.subtract))
                link(dve.tensor_tensor(mixrows[:, BO], mixrows[:, BO], mixrows[:, SCALE], ALU.mult))
                link(dve.tensor_tensor(rows[:, MIXC], mixrows[:, BO], mixrows[:, BIAS], ALU.add))
                for a in range(K):
                    ins = dve.tensor_tensor(wvoraw[:, a, :], ps[:, 4 + a, :], mixrows[:, SCALE], ALU.mult)
                link(ins)
                dve.wait_ge(p2_made, 2 * K + 2)
                link(dve.tensor_copy(wqbkrow, ps[:, 1, :]))
                dve.wait_ge(p2_made, 2 * K + 3)
                link(dve.tensor_tensor(bvorow, ps[:, 2, :], mixrows[:, SCALE], ALU.mult))
                dve.wait_ge(p2_made, 2 * K + 4)
                link(dve.tensor_copy(cg[:, 0, :], ps[:, 3, 0:K]))
                link(dve.tensor_copy(c(BQBK), ps[:, 3, K:K + 1]))

                def flat(ap):
                    return ap.rearrange("p k n -> p (k n)")
                for i in (W1, W2, WF):
                    dve.wait_ge(wsem[i], 16)
                dve.wait_ge(rows_loaded, 16 * 6)
                for i, ap in ((A_W1, flat(wraw[:, W1])), (A_W2, flat(wraw[:, W2])), (A_M, flat(mraw)),
                              (A_WVO, flat(wvoraw)), (A_C, cg[:, 0, :]), (A_FFN, flat(wraw[:, WF])),
                              (A_G1, rows[:, G1]), (A_BE1, rows[:, BE1])):
                    ins = dve.tensor_reduce(wide[:, i:i + 1], ap, AX.X, ALU.max, apply_absolute_value=True)
                link(ins)
                dve.sem_inc(p2_max, 1)
                dve.wait_ge(p2_all, 1)
                def lin(dst, a, m, b):
                    link(dve.scalar_tensor_tensor(out=c(dst), in0=c(a), scalar=m, in1=c(b), op0=ALU.mult, op1=ALU.add))

                def power(dst, bound):
                    link(dve.tensor_scalar(c(TMP2), c(bound), 1e-20, None, ALU.max))
                    link(dve.reciprocal(c(dst), c(TMP2)))
                    link(dve.tensor_scalar(c(dst), c(dst), TOP, None, ALU.mult))
                    link(dve.tensor_scalar(c(dst).bitcast(I32), c(dst).bitcast(I32), EXPONENT, None, ALU.bitwise_and))

                def inverse(dst, s, m):
                    link(dve.reciprocal(c(TMP2), c(s)))
                    link(dve.tensor_scalar(c(dst), c(TMP2), m, None, ALU.mult))

                power(S_W1, A_W1)
                power(S_W2, A_W2)
                power(S_M, A_M)
                power(S_WVO, A_WVO)
                lin(TMP, A_M, ROOT_D * ROOT_D, A_C)
                power(S_G, TMP)
                link(dve.tensor_scalar(c(TMP), c(A_W1), ROOT_D * ROOT_D, None, ALU.mult))
                power(S_Y1, TMP)
                lin(TMP, A_G1, ROOT_D, A_BE1)
                power(S_H, TMP)
                link(dve.tensor_tensor(c(TMP), c(A_G1), c(A_BE1), ALU.add))
                link(dve.tensor_scalar(c(TMP), c(TMP), ROOT_D * ROOT_D, c(A_W2), ALU.mult, ALU.mult))
                power(S_Y2, TMP)
                inverse(R_Y1, S_Y1, 1.0)
                inverse(R_Y2, S_Y2, 1.0)
                inverse(R_W1, S_W1, 1.0 / XSCALE)
                link(dve.tensor_tensor(c(R_W1), c(R_W1), c(S_Y1), ALU.mult))
                inverse(R_W2, S_W2, 1.0)
                inverse(R_H, S_H, 1.0)
                link(dve.tensor_tensor(c(R_W2), c(R_W2), c(R_H), ALU.mult))
                link(dve.tensor_tensor(c(R_W2), c(R_W2), c(S_Y2), ALU.mult))
                inverse(F_U, S_WVO, 1.0 / XSCALE)
                inverse(F_G, S_M, 1.0 / XSCALE)
                link(dve.tensor_tensor(c(F_G), c(F_G), c(S_G), ALU.mult))
                inverse(F_S, S_G, 1.0 / XSCALE)
                link(dve.tensor_scalar(cg[:, 1, :], cg[:, 0, :], c(S_G), None, ALU.mult))
                for parts, raw, s in ((w12parts, wraw[:, W1], S_W1), (mparts, mraw, S_M), (wvoparts, wvoraw, S_WVO)):
                    split_weight(dve, parts, raw, c(s), link)
                link(dve.tensor_scalar(c(TMP), c(A_FFN), 1e-12, None, ALU.max))
                link(dve.reciprocal(c(TMP2), c(TMP)))
                link(dve.tensor_scalar(c(W_SC), c(TMP2), FP8_MAX, None, ALU.mult))
                link(dve.tensor_scalar(wtmp, wraw[:, WF], c(W_SC), FP8_MAX, ALU.mult, ALU.min))
                link(dve.tensor_scalar(wtmp, wtmp, -FP8_MAX, None, ALU.max))
                link(dve.tensor_scalar(wpow.bitcast(I32), wtmp.bitcast(I32), EXPONENT, None, ALU.bitwise_and))
                link(dve.tensor_scalar(wpow, wpow, 2.0 ** -6, 1.5 * 2.0 ** 20, ALU.max, ALU.mult))
                link(dve.tensor_tensor(wtmp, wtmp, wpow, ALU.add))
                link(dve.tensor_tensor(wffn[:], wtmp, wpow, ALU.subtract))
                dve.wait_ge(p1_gathered, 16 * NJ)
                link(dve.tensor_scalar(etab(0, I32), t_src, 7, None, ALU.logical_shift_right))
                link(dve.tensor_scalar(etab(1, I32), t_src, P - 1, None, ALU.bitwise_and))
                link(dve.tensor_copy(etab(2), etab(0, I32)))
                link(dve.tensor_copy(etab(0), etab(1, I32)))
                link(dve.tensor_copy(etab(3), t_dst))
                for g in range(QW):
                    js = slice(g * SPAN, (g + 1) * SPAN)
                    ins = dve.tensor_scalar(etab(1)[:, js], etab(3)[:, js], thr[0:PW, g:g + 1], None, ALU.subtract)
                link(ins)
                link(dve.scalar_tensor_tensor(out=etab(2), in0=etab(2), scalar=float(WIN), in1=etab(1),
                                              op0=ALU.mult, op1=ALU.add))
                link(dve.tensor_scalar(etab(3), etab(1), 0.0, FAR, ALU.is_lt, ALU.mult))
                link(dve.tensor_scalar(etab(1), etab(1), float(WIN), FAR, ALU.is_ge, ALU.mult))
                link(dve.tensor_tensor(etab(3), etab(3), etab(1), ALU.add))
                dve.tensor_tensor(etab(2), etab(2), etab(3), ALU.add).then_inc(p1_coded, 1)
                for j in range(NJ):
                    g, s = divmod(j, SPAN)
                    dve.wait_ge(p1_turned, j + 1)
                    b = 2 + 2 * (j % 3)
                    dve.tensor_copy(code[:, s, g * PW:(g + 1) * PW], ps[:, b, 0:PW])
                    dve.tensor_copy(low[:, s, g * PW:(g + 1) * PW], ps[:, b + 1, 0:PW]).then_inc(p1_kept, 1)

        xin = z32(3072, 2 * D).rearrange("p (b n) -> p b n", b=2)
        xn = z32(4096, 2 * D).rearrange("p (b n) -> p b n", b=2)
        ubuf = z32(5120, 2 * D).rearrange("p (b n) -> p b n", b=2)
        junk = z32(6144, D)
        p4_x = [sem(f"p4_x_loaded{b}") for b in range(2)]
        p4_u = [sem(f"p4_mix_stored{b}") for b in range(2)]
        p4_ufree = sem("p4_mix_buffers_free")
        p4_stats = sem("p4_stats")
        p4_aggr = sem("p4_variance_ready")
        p4_var = sem("p4_variance_plus_eps")
        p4_rstd = sem("p4_rstd_ready")
        p4_xn = sem("p4_xn_ready")
        p4_bias = sem("p4_row_bias_done")
        p4_turned = sem("p4_xn_transposed")
        p4_xh = sem("p4_high_parts")
        p4_xl = sem("p4_low_parts")
        p4_wvo = sem("p4_wvo_product")
        p4_ubuf = sem("p4_mix_tile_ready")

        with nc.Block() as block:
            @block.sync
            def _(sp):
                with sp.Fori(0, T // 2) as i:
                    for b in range(2):
                        t = i * 2 + b
                        sp.wait_ge(p4_ubuf, t + 3)
                        sp.dma_start(mix_dram[bass.ds(t, 1)].rearrange("t p n -> (t p) n"), ubuf[:, b]
                                     ).then_inc(p4_u[b], 16)
                    for b in range(2):
                        sp.wait_ge(p4_u[b], i * 16 + 16)
                    sp.sem_inc(p4_ufree, 2)

            @block.gpsimd
            def _(pool):
                with pool.Fori(0, T // 2) as i:
                    for b in range(2):
                        t = i * 2 + b
                        pool.wait_ge(p4_var, t + 1)
                        pool.tensor_tensor(xrstd[:, bass.ds(t, 1)], veps[:, b:b + 1], half[:, 0:1], ALU.pow
                                           ).then_inc(p4_rstd, 1)

            @block.vector
            def _(dve):
                def norm(t, b, i):
                    dve.wait_ge(p4_x[b], i * 16 + 16)
                    dve.bn_stats(stats[:, b], xin[:, b]).then_inc(p4_stats, 1)
                    wait_apart(dve, p4_stats, t + 1, passed)
                    dve.bn_aggr(aggr[:, b], stats[:, b]).then_inc(p4_aggr, 1)
                    dve.wait_ge(p4_aggr, t + 1)
                    dve.tensor_scalar(veps[:, b:b + 1], aggr[:, b, 1:2], EPS, None, ALU.add).then_inc(p4_var, 1)
                    dve.tensor_copy(xmean[:, bass.ds(t, 1)], aggr[:, b, 0:1])

                def normalise(t, b):
                    dve.wait_ge(p4_rstd, t + 1)
                    dve.wait_ge(p4_turned, t + 1)
                    dve.tensor_scalar(xn[:, b], xin[:, b], aggr[:, b, 0:1], xrstd[:, bass.ds(t, 1)],
                                      ALU.subtract, ALU.mult).then_inc(p4_xn, 1)
                    dve.wait_ge(p4_xn, t + 1)
                    dve.tensor_tensor_reduce(out=junk, in0=xn[:, b], in1=wqbkrow, scale=1.0, scalar=0.0,
                                             op0=ALU.mult, op1=ALU.add, accum_out=xdot[:, b:b + 1]).then_inc(p4_bias, 1)
                    dve.wait_ge(p4_bias, t + 1)
                    dve.tensor_scalar(rowbias[:, bass.ds(t, 1)], xdot[:, b:b + 1], c(BQBK), None, ALU.add)

                def low_parts(t, b):
                    dve.wait_ge(p4_xh, t + 1)
                    at = bass.ds(t * P, P)
                    dve.scalar_tensor_tensor(out=xparts[:, 1, :, at], in0=ps[:, b, :].rearrange("p (k n) -> p k n", k=K),
                                             scalar=XSCALE, in1=xparts[:, 0, :, at], op0=ALU.mult, op1=ALU.subtract
                                             ).then_inc(p4_xl, 1)

                def product(t, b):
                    dve.wait_ge(p4_wvo, t + 1)
                    dve.wait_ge(p4_ufree, t + 1)
                    dve.scalar_tensor_tensor(out=ubuf[:, b], in0=ps[:, 4 + b, :], scalar=c(F_U), in1=bvorow,
                                             op0=ALU.mult, op1=ALU.add).then_inc(p4_ubuf, 1)

                dve.sem_inc(p4_ufree, 2)
                norm(0, 0, 0)
                normalise(0, 0)
                norm(1, 1, 0)
                normalise(1, 1)
                low_parts(0, 0)
                with dve.Fori(0, LOOPS) as i:
                    for b in range(2):
                        norm(i * 2 + (b + 2), b, i + 1)
                        low_parts(i * 2 + (b + 1), 1 - b)
                        normalise(i * 2 + (b + 2), b)
                        product(i * 2 + b, b)
                low_parts(T - 1, 1)
                product(T - 2, 0)
                product(T - 1, 1)

            @block.scalar
            def _(act):
                def load(t, b):
                    act.dma_start(xin[:, b], x_t[bass.ds(t, 1)].rearrange("t p n -> (t p) n")).then_inc(p4_x[b], 16)

                def high_parts(t, b):
                    act.wait_ge(p4_turned, t + 3)
                    act.activation(xparts[:, 0, :, bass.ds(t * P, P)], ps[:, b, :].rearrange("p (k n) -> p k n", k=K),
                                   ACT.Copy, scale=XSCALE).then_inc(p4_xh, 1)

                load(0, 0)
                load(1, 1)
                with act.Fori(0, LOOPS) as i:
                    for b in range(2):
                        high_parts(i * 2 + b, b)
                        act.wait_ge(p4_bias, i * 2 + (b + 1))
                        load(i * 2 + (b + 2), b)
                high_parts(T - 2, 0)
                high_parts(T - 1, 1)

            @block.tensor
            def _(pe):
                def turn(t, b):
                    pe.wait_ge(p4_xn, t + 1)
                    pe.wait_ge(p4_xl, t + 1)
                    for k in range(K):
                        ins = pe.transpose(ps[:, b, k * P:(k + 1) * P], xn[:, b, k * P:(k + 1) * P], ident[:])
                    ins.then_inc(p4_turned, 1)

                def multiply(t, b):
                    pe.wait_ge(p4_xl, t + 3)
                    pe.wait_ge(p4_ubuf, t + 1)
                    split_product(pe, ps[:, 4 + b, :], xparts, bass.ds(t * P, P), wvoparts).then_inc(p4_wvo, 1)

                pe.sem_inc(p4_turned, 2)
                pe.sem_inc(p4_xl, 2)
                pe.sem_inc(p4_ubuf, 2)
                turn(0, 0)
                with pe.Fori(0, LOOPS) as i:
                    for b in range(2):
                        turn(i * 2 + (b + 1), 1 - b)
                        multiply(i * 2 + b, b)
                turn(T - 1, 1)
                multiply(T - 2, 0)
                multiply(T - 1, 1)

        score = z32(0, 2 * N).rearrange("p (b n) -> p b n", b=2)
        acc = z32(2 * N, N)
        gparts = z32(3 * N, 1024).bitcast(F16).rearrange("p (b h k n) -> p b h k n", b=2, h=2, k=K)
        NG = len(GROUPS)
        SB = 4
        WPG = WPT // NG
        assert WPT == NG * WPG and WPG == 2
        RING = 8
        at = 2 * SPAN * NWIN
        lowhot = regionB[:, at:at + RING * SPAN * P // 2].bitcast(F16).rearrange("p (r s n) -> p r s n", r=RING, s=SPAN)
        at += RING * SPAN * P // 2
        codehot = regionB[:, at:at + RING * SPAN * CODES // 2].bitcast(F16).rearrange(
            "p (r s n) -> p r s n", r=RING, s=SPAN)
        at += RING * SPAN * CODES // 2
        ctile = regionB[:, at:at + NP].bitcast(F16).rearrange("p (b t n) -> p b t n", b=2, t=T)
        p5_g = sem("p5_g_product")
        p5_gb = sem("p5_g_scaled")
        p5_gh = sem("p5_g_high")
        p5_gl = sem("p5_g_low")
        p5_s = sem("p5_scores")
        p5_sc = sem("p5_scores_copied")
        p5_m = sem("p5_softmax_steps")
        p5_nb = sem("p5_bias_ready")
        p5_e = sem("p5_exponentials")
        p5_rz = sem("p5_reciprocal_steps")
        p5_acc = sem("p5_columns_added")
        p5_zero = sem("p5_zeroed")
        p5_col = sem("p5_column_sums")
        p5_fin = sem("p5_final_steps")
        p5_cols = sem("p5_source_columns_copied")
        p5_low = sem("p5_source_onehots")
        p5_code = sem("p5_code_onehots")
        p5_count = sem("p5_windows_counted")
        p5_wout = sem("p5_windows_copied")
        p5_loops = sem("p5_self_loops_added")
        p5_stored = [sem(f"p5_counts_stored{b}") for b in range(2)]
        p5_cfree = sem("p5_count_buffers_free")
        p5_deg = sem("p5_degrees_ready")
        p5_degout = sem("p5_degrees_copied")

        with nc.Block() as block:
            @block.tensor
            def _(pe):
                def g_product(t, b):
                    pe.wait_ge(p5_gl, t + 1)
                    if not isinstance(t, int):
                        pe.wait_ge(p5_degout, t - 1)
                    at = bass.ds(t * P, P)
                    for j in range(K):
                        for k in range(K):
                            for l, r in ((0, 0), (0, 1), (1, 0)):
                                ins = pe.matmul(ps[:, b, j * P:(j + 1) * P], mparts[:, l, k, j * P:(j + 1) * P],
                                                xparts[:, r, k, at], start=(k == 0 and l == 0 and r == 0),
                                                stop=(k == K - 1 and l == 1))
                    ins.then_inc(p5_g, 1)

                def degrees(t, b):
                    pe.wait_ge(p5_loops, t + 1)
                    for i in range(T):
                        ins = pe.matmul(ps[:, 1 - b, 0:1], ctile[:, b, i, :], ones16[:], start=(i == 0), stop=(i == T - 1))
                    ins.then_inc(p5_deg, 1)

                def scores_and_counts(t, b, degrees_of=None):
                    pe.wait_ge(p5_gl, t + 3)
                    for g, (a, n) in enumerate(GROUPS):
                        pe.wait_ge(p5_sc, t * NG + (g + 1))
                        for k in range(K):
                            for l, r in ((0, 0), (0, 1), (1, 0)):
                                ins = pe.matmul(ps[:, 2 + g % SB, 0:n], gparts[:, b, l, k, :], xparts[:, r, k, a:a + n],
                                                start=(k == 0 and l == 0 and r == 0), stop=(k == K - 1 and l == 1))
                        ins.then_inc(p5_s, 1)
                        for v in range(WPG):
                            u = g * WPG + v
                            pe.wait_ge(p5_low, t * WPT + (u + 1))
                            pe.wait_ge(p5_code, t * WPT + (u + 1))
                            pe.wait_ge(p5_wout, t * WPT + (u + 1))
                            for s in range(SPAN):
                                ins = pe.matmul(ps[:, 6 + v, 0:CODES], lowhot[:, u % RING, s], codehot[:, u % RING, s],
                                                start=(s == 0), stop=(s == SPAN - 1))
                            ins.then_inc(p5_count, 1)
                        if g == NG // 2 and degrees_of is not None:
                            degrees(degrees_of, 1 - b)

                pe.sem_inc(p5_gl, 2)
                pe.sem_inc(p5_sc, SB)
                pe.sem_inc(p5_count, RING)
                g_product(0, 0)
                g_product(1, 1)
                scores_and_counts(0, 0)
                with pe.Fori(0, LOOPS) as i:
                    for b in (1, 0):
                        t = i * 2 + (2 - b)
                        g_product(t + 1, 1 - b)
                        scores_and_counts(t, b, t - 1)
                scores_and_counts(T - 1, 1, T - 2)
                degrees(T - 1, 1)
                pe.wait_ge(p5_acc, T + 2)
                for t in range(T):
                    n = min(P, N - t * P)
                    ins = pe.matmul(ps[0:n, 2, t:t + 1], acc[:, t * P:t * P + n], ones[:], start=True, stop=True)
                ins.then_inc(p5_col, 1)

            @block.scalar
            def _(act):
                def g_scale(t, b):
                    act.wait_ge(p5_g, t + 1)
                    for j in range(K):
                        bank = ps[:, b, j * P:(j + 1) * P]
                        ins = act.activation(bank, bank, ACT.Identity, bias=cg[:, 1, j:j + 1], scale=c(F_G))
                    ins.then_inc(p5_gb, 1)

                def exponentials(t, b):
                    act.wait_ge(p5_nb, t + 1)
                    act.activation(score[:, b], score[:, b], ACT.Exp, bias=soft[:, b, 2:3], scale=c(F_S),
                                   accum_out=soft[:, b, 3:4]).then_inc(p5_e, 1)

                def windows(t, b):
                    act.wait_ge(p5_cfree, t + 1)
                    for u in range(WPT):
                        if u == WPT // 2 + 4 and (not isinstance(t, int) or t > 0):
                            degree(t - 1, 1 - b)
                        act.wait_ge(p5_count, t * WPT + (u + 1 + RING))
                        act.copy(ctile[:, b, :, u * WIN:(u + 1) * WIN],
                                 ps[:, 6 + u % 2, 0:CODES].rearrange("p (t n) -> p t n", t=T)).then_inc(p5_wout, 1)

                def degree(t, b):
                    act.wait_ge(p5_deg, t + 1)
                    act.copy(deg[:, bass.ds(t, 1)], ps[:, 1 - b, 0:1]).then_inc(p5_degout, 1)

                act.sem_inc(p5_wout, 2)
                act.sem_inc(p5_degout, 1)
                g_scale(0, 0)
                g_scale(1, 1)
                windows(0, 0)
                exponentials(0, 0)
                with act.Fori(0, LOOPS) as i:
                    for b in (1, 0):
                        t = i * 2 + (2 - b)
                        g_scale(t + 1, 1 - b)
                        windows(t, b)
                        exponentials(t, b)
                windows(T - 1, 1)
                exponentials(T - 1, 1)
                degree(T - 1, 1)

            @block.gpsimd
            def _(pool):
                def source_onehots(t, u):
                    n = t * WPT + (u + 1)
                    pool.tensor_copy(lowcols[:, u % 2], low[:, 0:POOL_SPAN, bass.ds(t * WPT + u, 1)]).then_inc(p5_cols, 1)
                    pool.wait_ge(p5_cols, n)
                    wait_apart(pool, p5_count, n, passed)
                    for s in range(POOL_SPAN):
                        ins = pool.tensor_scalar(lowhot[:, u % RING, s], col16[:, 0:P], lowcols[:, u % 2, s], None,
                                                 ALU.is_equal)
                    ins.then_inc(p5_low, 1)

                def self_loops(t, b):
                    pool.wait_ge(p5_wout, t * WPT + (WPT + 2))
                    blk = ctile[:, b, bass.ds(t, 1), :].rearrange("p t n -> p (t n)")
                    pool.tensor_tensor(blk, blk, ident16[:], ALU.add).then_inc(p5_loops, 1)

                for u in range(WPT):
                    source_onehots(0, u)
                with pool.Fori(0, LOOPS) as i:
                    for b in (1, 0):
                        t = i * 2 + (2 - b)
                        for u in range(WPT):
                            source_onehots(t, u)
                            if u == RING // 2:
                                self_loops(t - 1, 1 - b)
                for u in range(WPT):
                    source_onehots(T - 1, u)
                    if u == RING // 2:
                        self_loops(T - 2, 0)
                self_loops(T - 1, 1)

            @block.sync
            def _(sp):
                sp.sem_inc(p5_cfree, 2)
                with sp.Fori(0, T // 2) as i:
                    for b in range(2):
                        t = i * 2 + b
                        sp.wait_ge(p5_loops, t + 1)
                        sp.dma_start(counts_dram[bass.ds(t, 1)].rearrange("t p n -> (t p) n"),
                                     ctile[:, b].rearrange("p t n -> p (t n)")).then_inc(p5_stored[b], 16)
                        sp.wait_ge(p5_deg, t + 1)
                        sp.wait_ge(p5_stored[b], i * 16 + 16)
                        sp.sem_inc(p5_cfree, 1)

            @block.vector
            def _(dve):
                def g_split(t, b):
                    dve.wait_ge(p5_gb, t + 1)
                    if not isinstance(t, int):
                        dve.wait_ge(p5_s, (t - 1) * NG)
                    bank = ps[:, b, :].rearrange("p (k n) -> p k n", k=K)
                    dve.tensor_copy(gparts[:, b, 0], bank).then_inc(p5_gh, 1)
                    dve.wait_ge(p5_gh, t + 1)
                    dve.tensor_tensor(gparts[:, b, 1], bank, gparts[:, b, 0], ALU.subtract).then_inc(p5_gl, 1)

                def code_onehots(t, u):
                    dve.wait_ge(p5_count, t * WPT + (u + 1))
                    for s in range(SPAN):
                        ins = dve.tensor_scalar(codehot[:, u % RING, s], col16[:, 0:CODES],
                                                code[:, s, bass.ds(t * WPT + u, 1)], None, ALU.is_equal)
                    for s in range(POOL_SPAN, SPAN):
                        ins = dve.tensor_scalar(lowhot[:, u % RING, s], col16[:, 0:P],
                                                low[:, s, bass.ds(t * WPT + u, 1)], None, ALU.is_equal)
                    ins.then_inc(p5_code, 1)

                def row_maximum(t, b, midway):
                    dve.wait_ge(p5_acc, t + 1)
                    for g, (a, n) in enumerate(GROUPS):
                        if g < NG - 1 or not isinstance(t, int) or t < T - 1:
                            for v in range(WPG):
                                code_onehots(t, (g + 1) * WPG + v)
                        dve.wait_ge(p5_s, t * NG + (g + 1))
                        dve.tensor_scalar(score[:, b, a:a + n], ps[:, 2 + g % SB, 0:n], 1.0, None, ALU.mult, ALU.max,
                                          accum_out=mx[:, b, g:g + 1]).then_inc(p5_sc, 1)
                        midway(g)
                    dve.wait_ge(p5_sc, t * NG + (NG + SB))
                    dve.tensor_reduce(soft[:, b, 0:1], mx[:, b, 0:NG], AX.X, ALU.max).then_inc(p5_m, 1)
                    dve.wait_ge(p5_m, t * 2 + 1)
                    one = bass.ds(t, 1)
                    dve.tensor_scalar(soft[:, b, 1:2], soft[:, b, 0:1], c(F_S), rowbias[:, one], ALU.mult, ALU.add
                                      ).then_inc(p5_m, 1)
                    dve.wait_ge(p5_m, t * 2 + 2)
                    dve.tensor_tensor(soft[:, b, 2:3], rowbias[:, one], soft[:, b, 1:2], ALU.subtract
                                      ).then_inc(p5_nb, 1)

                def add_columns(t, b):
                    dve.wait_ge(p5_e, t + 1)
                    dve.reciprocal(soft[:, b, 4:5], soft[:, b, 3:4]).then_inc(p5_rz, 1)
                    dve.wait_ge(p5_rz, t * 2 + 1)
                    dve.tensor_tensor(soft[:, b, 4:5], soft[:, b, 4:5], rowmask[:, bass.ds(t, 1)], ALU.mult
                                      ).then_inc(p5_rz, 1)
                    dve.wait_ge(p5_rz, t * 2 + 2)
                    dve.wait_ge(p5_acc, t + 2)
                    dve.scalar_tensor_tensor(out=acc, in0=score[:, b], scalar=soft[:, b, 4:5], in1=acc,
                                             op0=ALU.mult, op1=ALU.add).then_inc(p5_acc, 1)

                dve.memset(acc, 0.0).then_inc(p5_zero, 1)
                dve.wait_ge(p5_zero, 1)
                dve.sem_inc(p5_acc, 2)
                g_split(0, 0)
                g_split(1, 1)
                for u in range(WPG):
                    code_onehots(0, u)
                row_maximum(0, 0, lambda g: None)
                with dve.Fori(0, LOOPS) as i:
                    for b in (1, 0):
                        t = i * 2 + (2 - b)

                        def midway(g):
                            if g == 1:
                                g_split(t + 1, 1 - b)
                            if g == NG // 2:
                                add_columns(t - 1, 1 - b)
                        row_maximum(t, b, midway)
                row_maximum(T - 1, 1, lambda g: add_columns(T - 2, 0) if g == NG // 2 else None)
                add_columns(T - 1, 1)
                link = chain(dve, p5_fin)
                link(dve.memset(cs[:], 0.0))
                dve.wait_ge(p5_col, 1)
                link(dve.tensor_copy(cs[:, 0:T - 1], ps[:, 2, 0:T - 1]))
                link(dve.tensor_copy(cs[0:N - (T - 1) * P, T - 1:T], ps[0:N - (T - 1) * P, 2, T - 1:T]))
                link(dve.tensor_scalar(mixs[:], cs[:], 1e-9, None, ALU.add))
                link(dve.reciprocal(mixs[:], mixs[:]))
                link(dve.tensor_tensor(mixs[:], mixs[:], cs[:], ALU.mult))

        CHP = CH + 1
        CB = NP // 8
        assert CHP % 2 == 0
        etables = regionB[:, 0:5 * CHP].rearrange("p (v c) -> p v c", v=5)
        SRC_TILE, SRC_LOW, DST, ECODE, EFAR = range(5)
        at = 5 * CHP
        colwide = regionB[:, at:at + NP]
        at += NP
        countf = regionB[:, at:at + NP]
        at += NP
        eraw = regionB[:, at:at + 2 * P].bitcast(I32).rearrange("p (v e) -> p v e", v=2)
        at += 2 * P
        eint = regionB[:, at:at + 2 * P].bitcast(I32).rearrange("p (v e) -> p v e", v=2)
        at += 2 * P
        eflt = regionB[:, at:at + 3 * P].rearrange("p (v e) -> p v e", v=3)
        widehot = z32(0, NP).bitcast(F16).rearrange("p (b n) -> p b n", b=2)
        narrowhot = z32(NP, P).bitcast(F16).rearrange("p (b n) -> p b n", b=2)
        countparts = z32(NP + P, NP).bitcast(F16).rearrange("p (h t n) -> p h t n", h=2, t=T)
        zero16 = z32(2 * NP + P, 256).bitcast(F16)
        fb_sum = sem("sum_of_degrees_ready")
        fb_all = sem("sum_of_degrees_over_partitions")
        fb_flag = sem("recount_flag_ready")
        fb_check = sem("recount_check_steps")
        fb_iota = sem("recount_columns_ready")
        fb_zero = sem("recount_zeros_ready")
        fb_loaded = sem("recount_chunks_loaded")
        fb_steps = sem("recount_load_steps")
        fb_turned = sem("recount_chunks_transposed")
        fb_kept = sem("recount_chunks_kept")
        fb_tile = sem("recount_tile_steps")
        fb_hot = sem("recount_onehots")
        fb_used = sem("recount_chunks_used")
        fb_counted = sem("recount_tiles_counted")
        fb_copied = sem("recount_tiles_copied")
        fb_split = sem("recount_tiles_split")
        fb_stored = sem("recount_tiles_stored")
        fb_free = sem("recount_parts_free")
        fb_deg = sem("recount_degrees")
        fb_degout = sem("recount_degrees_copied")
        dinv_ready = sem("dinv_ready")
        f_ready = sem("row_factors_ready")
        FT = 7

        def must_recount(eng):
            eng.wait_ge(fb_flag, 1)
            return eng.value_load(recount[0:1, 0:1], min_val=0, max_val=1)

        with nc.Block() as block:
            @block.vector
            def _(dve):
                link = chain(dve, fb_check)
                dve.tensor_reduce(missed[:, 0:1], deg[:], AX.X, ALU.add).then_inc(fb_sum, 1)
                dve.wait_ge(fb_all, 1)
                link(dve.tensor_scalar(missed[:, 0:1], missed[:, 1:2], float(E + NP), None, ALU.not_equal))
                dve.tensor_copy(recount[:], missed[:, 0:1]).then_inc(fb_flag, 1)
                flag = must_recount(dve)
                with dve.If(flag > 0):
                    link = chain(dve, fb_steps)
                    dve.memset(zero16, 0.0).then_inc(fb_zero, 1)
                    for r in range(-(-CHP // P)):
                        n = min(P, CHP - r * P)
                        dve.wait_ge(fb_loaded, 16 * r + 16)
                        dve.tensor_scalar(eint[0:n, 0], eraw[0:n, 0], ~(P - 1), None, ALU.bitwise_and)
                        link(dve.tensor_scalar(eint[0:n, 1], eraw[0:n, 0], P - 1, None, ALU.bitwise_and))
                        dve.tensor_copy(eflt[0:n, SRC_TILE], eint[0:n, 0])
                        dve.tensor_copy(eflt[0:n, SRC_LOW], eint[0:n, 1])
                        link(dve.tensor_copy(eflt[0:n, DST], eraw[0:n, 1]))
                        dve.wait_ge(fb_turned, r + 1)
                        for v in range(3):
                            ins = dve.tensor_copy(etables[:, v, r * P:r * P + n], ps[:, r % 8, v * P:v * P + n])
                        ins.then_inc(fb_kept, 1)
                    dve.wait_ge(fb_kept, -(-CHP // P))
                    dve.wait_ge(fb_iota, 1)
                    code_of, far_of = etables[:, ECODE], etables[:, EFAR]
                    with dve.Fori(0, T) as t:
                        steps = [0]

                        def step(ins):
                            steps[0] += 1
                            ins.then_inc(fb_tile, 1)
                            dve.wait_ge(fb_tile, t * FT + steps[0])
                        step(dve.tensor_scalar(far_of, etables[:, DST], 0.0, FAR, ALU.is_lt, ALU.mult))
                        step(dve.tensor_scalar(code_of, etables[:, DST], float(P), FAR, ALU.is_ge, ALU.mult))
                        step(dve.tensor_tensor(far_of, far_of, code_of, ALU.add))
                        step(dve.tensor_tensor(code_of, etables[:, SRC_TILE], etables[:, DST], ALU.add))
                        step(dve.tensor_tensor(code_of, code_of, far_of, ALU.add))
                        step(dve.tensor_scalar(far_of, etables[:, DST], float(P), None, ALU.subtract))
                        step(dve.tensor_copy(etables[:, DST], far_of))
                        dve.sem_inc(passed, 1)
                        with dve.Fori(0, CHP // 2) as j:
                            for b in range(2):
                                dve.wait_ge(fb_used, t * CHP + j * 2 + (b + 1))
                                at = bass.ds(j * 2 + b, 1)
                                dve.tensor_scalar(narrowhot[:, b], col16[:, 0:P], etables[:, SRC_LOW, at], None,
                                                  ALU.is_equal)
                                dve.tensor_scalar(widehot[:, b], colwide, etables[:, ECODE, at], None, ALU.is_equal
                                                  ).then_inc(fb_hot, 1)
                        dve.wait_ge(fb_counted, t + 1)
                        for a in range(8):
                            ins = dve.tensor_copy(countf[:, a * CB:(a + 1) * CB], ps[:, a, 0:CB])
                        ins.then_inc(fb_copied, 1)
                        dve.wait_ge(fb_copied, t * 4 + 1)
                        blk = countf[:, bass.ds(t * P, P)]
                        dve.tensor_tensor(blk, blk, ident[:], ALU.add).then_inc(fb_copied, 1)
                        dve.wait_ge(fb_copied, t * 4 + 2)
                        dve.wait_ge(fb_free, t + 1)
                        whole = countf.rearrange("p (t n) -> p t n", t=T)
                        dve.tensor_copy(countparts[:, 0], whole).then_inc(fb_copied, 1)
                        dve.wait_ge(fb_copied, t * 4 + 3)
                        dve.tensor_tensor(countparts[:, 1], whole, countparts[:, 0], ALU.subtract).then_inc(fb_split, 1)
                        dve.sem_inc(fb_copied, 1)
                link = chain(dve, f_ready)
                dve.wait_ge(dinv_ready, 1)
                for f, a in ((f_y1, R_W1), (f_z1, R_Y1), (f_y2, R_W2), (f_z2, R_Y2)):
                    link(dve.tensor_scalar(f[:], dinv[:], c(a), None, ALU.mult))

            @block.gpsimd
            def _(pool):
                pool.wait_ge(fb_sum, 1)
                pool.partition_all_reduce(missed[:, 1:2], missed[:, 0:1], P, RADD
                                          ).then_inc(fb_all, 1)
                flag = must_recount(pool)
                with pool.If(flag > 0):
                    pool.iota(colwide, pattern=[[1, NP]], base=0, channel_multiplier=0,
                              allow_small_or_imprecise_dtypes=True).then_inc(fb_iota, 1)
                    pool.wait_ge(fb_degout, T)
                pool.tensor_tensor(dinv[:], deg[:], half[:], ALU.pow).then_inc(dinv_ready, 1)

            @block.tensor
            def _(pe):
                flag = must_recount(pe)
                with pe.If(flag > 0):
                    for r in range(-(-CHP // P)):
                        n = min(P, CHP - r * P)
                        pe.wait_ge(fb_steps, 2 * r + 2)
                        for v in range(3):
                            ins = pe.transpose(ps[:, r % 8, v * P:v * P + n], eflt[0:n, v], ident[0:n, 0:n])
                        ins.then_inc(fb_turned, 1)
                    pe.wait_ge(fb_kept, -(-CHP // P))
                    pe.wait_ge(fb_zero, 1)
                    pe.sem_inc(fb_used, 2)
                    with pe.Fori(0, T) as t:
                        for a in range(8):
                            pe.matmul(ps[:, a, 0:CB], zero16[:, 0:P], zero16[:, 0:CB], start=True, stop=False)
                        with pe.Fori(0, CHP // 2) as j:
                            for b in range(2):
                                pe.wait_ge(fb_hot, t * CHP + j * 2 + (b + 1))
                                for a in range(8):
                                    ins = pe.matmul(ps[:, a, 0:CB], narrowhot[:, b], widehot[:, b, a * CB:(a + 1) * CB],
                                                    start=False, stop=False)
                                ins.then_inc(fb_used, 1)
                        for a in range(8):
                            ins = pe.matmul(ps[:, a, 0:CB], zero16[:, 0:P], zero16[:, 0:CB], start=False, stop=True)
                        ins.then_inc(fb_counted, 1)
                        pe.wait_ge(fb_split, t + 1)
                        for i in range(T):
                            for h in range(2):
                                ins = pe.matmul(ps[:, 0, 0:1], countparts[:, h, i, :], ones16[:],
                                                start=(i == 0 and h == 0), stop=(i == T - 1 and h == 1))
                        ins.then_inc(fb_deg, 1)
                        pe.wait_ge(fb_degout, t + 1)

            @block.scalar
            def _(act):
                flag = must_recount(act)
                with act.If(flag > 0):
                    with act.Fori(0, T) as t:
                        act.wait_ge(fb_deg, t + 1)
                        act.copy(deg[:, bass.ds(t, 1)], ps[:, 0, 0:1]).then_inc(fb_degout, 1)

            @block.sync
            def _(sp):
                flag = must_recount(sp)
                with sp.If(flag > 0):
                    for r in range(-(-CHP // P)):
                        n = min(P, CHP - r * P)
                        if r > 0:
                            sp.wait_ge(fb_steps, 2 * r)
                        sp.dma_start(eraw[0:n].rearrange("p v e -> p (v e)"),
                                     edges[r * P:r * P + n].rearrange("c v e -> c (v e)")).then_inc(fb_loaded, 16)
                    sp.sem_inc(fb_free, 1)
                    with sp.Fori(0, T) as t:
                        sp.wait_ge(fb_split, t + 1)
                        one = bass.ds(t, 1)
                        for dram, h in ((counts_dram, 0), (low_counts_dram, 1)):
                            sp.dma_start(dram[one].rearrange("t p n -> (t p) n"),
                                         countparts[:, h].rearrange("p t n -> p (t n)")).then_inc(fb_stored, 16)
                        sp.wait_ge(fb_stored, t * 32 + 32)
                        sp.wait_ge(fb_deg, t + 1)
                        sp.sem_inc(fb_free, 1)

        w2raw = z32(8192, K * D).rearrange("p (k n) -> p k n", k=K)
        p45_w1 = sem("p4_w1_product")
        p45_y1h = sem("p4_y1_high")
        p45_y1l = sem("p4_y1_low")
        w2_loaded = sem("w2_loaded")

        with nc.Block() as block:
            @block.sync
            def _(sp):
                sp.dma_start(w2raw, w["W2"].rearrange("(k p) n -> p k n", p=P)).then_inc(w2_loaded, 16)

            @block.tensor
            def _(pe):
                pe.sem_inc(p45_y1l, 2)
                with pe.Fori(0, T // 2) as i:
                    for b in range(2):
                        t = i * 2 + b
                        pe.wait_ge(p45_y1l, t + 1)
                        split_product(pe, ps[:, b, :], xparts, bass.ds(t * P, P), w12parts).then_inc(p45_w1, 1)

            @block.scalar
            def _(act):
                with act.Fori(0, T // 2) as i:
                    for b in range(2):
                        t = i * 2 + b
                        one = bass.ds(t, 1)
                        act.wait_ge(p45_w1, t + 1)
                        act.activation(y1[:, one, 0, :].rearrange("p t n -> p (t n)"), ps[:, b, :], ACT.Copy,
                                       scale=f_y1[:, one]).then_inc(p45_y1h, 1)

            @block.vector
            def _(dve):
                with dve.Fori(0, T // 2) as i:
                    for b in range(2):
                        t = i * 2 + b
                        one = bass.ds(t, 1)
                        dve.wait_ge(p45_y1h, t + 1)
                        dve.scalar_tensor_tensor(out=y1[:, one, 1, :].rearrange("p t n -> p (t n)"), in0=ps[:, b, :],
                                                 scalar=f_y1[:, one], in1=y1[:, one, 0, :].rearrange("p t n -> p (t n)"),
                                                 op0=ALU.mult, op1=ALU.subtract).then_inc(p45_y1l, 1)

        cbuf = z32(0, NP).bitcast(F16).rearrange("p (b t n) -> p b t n", b=2, t=T)

        def pair_of(at):
            return z32(at, 2 * D).rearrange("p (b n) -> p b n", b=2)

        zbuf = pair_of(3840)

        clow = z32(8960, NP // 2).bitcast(F16).rearrange("p (t n) -> p t n", t=T)

        def load_counts(sp, loaded, low_loaded, used):
            flag = must_recount(sp)

            def low_counts(t):
                with sp.If(flag > 0):
                    sp.dma_start(clow.rearrange("p t n -> p (t n)"),
                                 low_counts_dram[bass.ds(t, 1)].rearrange("t p n -> (t p) n")).then_inc(low_loaded, 16)

            for b in range(2):
                sp.dma_start(cbuf[:, b].rearrange("p t n -> p (t n)"), counts_dram[b]).then_inc(loaded[b], 16)
            low_counts(0)
            with sp.Fori(0, LOOPS) as i:
                for b in range(2):
                    sp.wait_ge(used, i * 2 + (b + 1))
                    sp.dma_start(cbuf[:, b].rearrange("p t n -> p (t n)"),
                                 counts_dram[bass.ds(i * 2 + (b + 2), 1)].rearrange("t p n -> (t p) n")
                                 ).then_inc(loaded[b], 16)
                    low_counts(i * 2 + (b + 1))
            sp.wait_ge(used, T - 1)
            low_counts(T - 1)

        def aggregate(pe, y, t, b, flag, low_loaded):
            pe.matmul(ps[:, b, :], cbuf[:, b, 0, :], y[:, 0, 0, :], start=True, stop=False)
            with pe.If(flag > 0):
                pe.wait_ge(low_loaded, t * 16 + 16)
                for i in range(T):
                    for h in range(2):
                        pe.matmul(ps[:, b, :], clow[:, i, :], y[:, i, h, :], start=False, stop=False)
            for i in range(T):
                for h in range(2):
                    if i + h > 0:
                        ins = pe.matmul(ps[:, b, :], cbuf[:, b, i, :], y[:, i, h, :], start=False,
                                        stop=(i == T - 1 and h == 1))
            return ins

        hbuf = pair_of(4864)
        hparts = z32(5888, 1024).bitcast(F16).rearrange("p (b h k n) -> p b h k n", b=2, h=2, k=K)
        p6_c = [sem(f"p6_counts_loaded{b}") for b in range(2)]
        p6_low = sem("p6_low_counts_loaded")
        p6_agg = sem("p6_aggregated")
        p6_split = sem("p6_w2_split")
        p6_z = sem("p6_z_ready")
        p6_stats = sem("p6_stats")
        p6_aggr = sem("p6_moments")
        p6_var = sem("p6_variance_plus_eps")
        p6_rstd = sem("p6_rstd_ready")
        p6_norm = sem("p6_normalised")
        p6_gam = sem("p6_gamma_applied")
        p6_beta = sem("p6_beta_applied")
        p6_h = sem("p6_h_ready")
        p6_turned = sem("p6_h_transposed")
        p6_hh = sem("p6_h_high")
        p6_hl = sem("p6_h_low")
        p6_w2 = sem("p6_w2_product")
        p6_y2h = sem("p6_y2_high")
        p6_y2l = sem("p6_y2_low")
        rstd6 = wide

        with nc.Block() as block:
            @block.sync
            def _(sp):
                load_counts(sp, p6_c, p6_low, p6_agg)

            @block.tensor
            def _(pe):
                def agg(t, b, i):
                    pe.wait_ge(p6_c[b], i * 16 + 16)
                    pe.wait_ge(p6_z, t + 1)
                    aggregate(pe, y1, t, b, flag, p6_low).then_inc(p6_agg, 1)

                def turn(t, b):
                    pe.wait_ge(p6_h, t + 1)
                    pe.wait_ge(p6_hl, t + 1)
                    for k in range(K):
                        ins = pe.transpose(ps[:, 2 + b, k * P:(k + 1) * P], hbuf[:, b, k * P:(k + 1) * P], ident[:])
                    ins.then_inc(p6_turned, 1)

                def multiply(t, b):
                    pe.wait_ge(p6_split, 2)
                    pe.wait_ge(p6_hl, t + 3)
                    pe.wait_ge(p6_y2l, t + 1)
                    split_product(pe, ps[:, 4 + b, :], hparts[:, b], slice(0, P), w12parts).then_inc(p6_w2, 1)

                flag = must_recount(pe)
                pe.sem_inc(p6_z, 2)
                pe.sem_inc(p6_hl, 2)
                pe.sem_inc(p6_w2, 2)
                pe.sem_inc(p6_y2l, 2)
                agg(0, 0, 0)
                agg(1, 1, 0)
                with pe.Fori(0, LOOPS) as i:
                    for b in range(2):
                        turn(i * 2 + b, b)
                        agg(i * 2 + (b + 2), b, i + 1)
                        multiply(i * 2 + b, b)
                for b in range(2):
                    turn(T - 2 + b, b)
                    multiply(T - 2 + b, b)

            @block.vector
            def _(dve):
                def norm(t, b):
                    one = bass.ds(t, 1)
                    dve.wait_ge(p6_agg, t + 1)
                    if not isinstance(t, int):
                        dve.wait_ge(p6_h, t - 1)
                    dve.scalar_tensor_tensor(out=zbuf[:, b], in0=ps[:, b, :], scalar=f_z1[:, one], in1=rows[:, B1],
                                             op0=ALU.mult, op1=ALU.add).then_inc(p6_z, 1)
                    dve.wait_ge(p6_z, t + 3)
                    dve.bn_stats(stats[:, b], zbuf[:, b]).then_inc(p6_stats, 1)
                    wait_apart(dve, p6_stats, t + 1, passed)
                    dve.bn_aggr(aggr[:, b], stats[:, b]).then_inc(p6_aggr, 1)
                    dve.wait_ge(p6_aggr, t + 1)
                    dve.tensor_scalar(veps[:, b:b + 1], aggr[:, b, 1:2], EPS, None, ALU.add).then_inc(p6_var, 1)
                    dve.wait_ge(p6_rstd, t + 1)
                    dve.tensor_scalar(zbuf[:, b], zbuf[:, b], aggr[:, b, 0:1], rstd6[:, b:b + 1],
                                      ALU.subtract, ALU.mult).then_inc(p6_norm, 1)

                def h_low(t, b):
                    dve.wait_ge(p6_hh, t + 1)
                    dve.scalar_tensor_tensor(out=hparts[:, b, 1], in0=ps[:, 2 + b, :].rearrange("p (k n) -> p k n", k=K),
                                             scalar=c(S_H), in1=hparts[:, b, 0], op0=ALU.mult, op1=ALU.subtract
                                             ).then_inc(p6_hl, 1)

                def y2_low(t, b):
                    one = bass.ds(t, 1)
                    dve.wait_ge(p6_y2h, t + 1)
                    dve.scalar_tensor_tensor(out=y2[:, one, 1, :].rearrange("p t n -> p (t n)"), in0=ps[:, 4 + b, :],
                                             scalar=f_y2[:, one], in1=y2[:, one, 0, :].rearrange("p t n -> p (t n)"),
                                             op0=ALU.mult, op1=ALU.subtract).then_inc(p6_y2l, 1)

                dve.wait_ge(w2_loaded, 16)
                split_weight(dve, w12parts, w2raw, c(S_W2), chain(dve, p6_split))
                norm(0, 0)
                norm(1, 1)
                with dve.Fori(0, LOOPS) as i:
                    for b in range(2):
                        h_low(i * 2 + b, b)
                        norm(i * 2 + (b + 2), b)
                        y2_low(i * 2 + b, b)
                for b in range(2):
                    h_low(T - 2 + b, b)
                    y2_low(T - 2 + b, b)

            @block.gpsimd
            def _(pool):
                with pool.Fori(0, T // 2) as i:
                    for b in range(2):
                        t = i * 2 + b
                        pool.wait_ge(p6_var, t + 1)
                        pool.tensor_tensor(rstd6[:, b:b + 1], veps[:, b:b + 1], half[:, 0:1], ALU.pow
                                           ).then_inc(p6_rstd, 1)
                        pool.wait_ge(p6_norm, t + 1)
                        pool.tensor_tensor(zbuf[:, b], zbuf[:, b], rows[:, G1], ALU.mult).then_inc(p6_gam, 1)
                        pool.wait_ge(p6_gam, t + 1)
                        pool.tensor_tensor(zbuf[:, b], zbuf[:, b], rows[:, BE1], ALU.add).then_inc(p6_beta, 1)

            @block.scalar
            def _(act):
                def gelu(t, b):
                    act.wait_ge(p6_beta, t + 1)
                    act.wait_ge(p6_turned, t + 1)
                    act.activation(hbuf[:, b], zbuf[:, b], ACT.Gelu).then_inc(p6_h, 1)

                def h_high(t, b):
                    act.wait_ge(p6_turned, t + 3)
                    act.wait_ge(p6_w2, t + 1)
                    act.activation(hparts[:, b, 0], ps[:, 2 + b, :].rearrange("p (k n) -> p k n", k=K), ACT.Copy,
                                   scale=c(S_H)).then_inc(p6_hh, 1)

                def y2_high(t, b):
                    one = bass.ds(t, 1)
                    act.wait_ge(p6_w2, t + 3)
                    act.activation(y2[:, one, 0, :].rearrange("p t n -> p (t n)"), ps[:, 4 + b, :], ACT.Copy,
                                   scale=f_y2[:, one]).then_inc(p6_y2h, 1)

                act.sem_inc(p6_turned, 2)
                gelu(0, 0)
                h_high(0, 0)
                gelu(1, 1)
                y2_high(0, 0)
                with act.Fori(0, LOOPS) as i:
                    for b in (1, 0):
                        t = i * 2 + (2 - b)
                        h_high(t, b)
                        gelu(t + 1, 1 - b)
                        y2_high(t, b)
                h_high(T - 1, 1)
                y2_high(T - 1, 1)

        xbuf = pair_of(4864)
        ubuf7 = pair_of(5888)
        xnbuf = pair_of(6912)
        dev = pair_of(7936)
        p7_c = [sem(f"p7_counts_loaded{b}") for b in range(2)]
        p7_xu = [sem(f"p7_x_and_mix_loaded{b}") for b in range(2)]
        p7_low = sem("p7_low_counts_loaded")
        p7_agg = sem("p7_aggregated")
        p7_z = sem("p7_z_ready")
        p7_stats = sem("p7_stats")
        p7_aggr = sem("p7_moments")
        p7_var = sem("p7_variance_plus_eps")
        p7_rstd = sem("p7_rstd_ready")
        p7_norm = sem("p7_normalised")
        p7_xn = sem("p7_xn_ready")
        p7_mix = sem("p7_mix_steps")
        p7_pre = sem("p7_pool_steps")
        p7_gelu = sem("p7_gelu_done")
        p7_new = sem("p7_new_x_ready")
        p7_nst = sem("p7_new_stats")
        p7_nag = sem("p7_new_moments")
        p7_nvar = sem("p7_new_variance_plus_eps")
        p7_nrstd = sem("p7_new_rstd")
        p7_dev = sem("p7_deviation")
        p7_amax = sem("p7_row_maximum")

        with nc.Block() as block:
            @block.sync
            def _(sp):
                load_counts(sp, p7_c, p7_low, p7_agg)

            @block.tensor
            def _(pe):
                flag = must_recount(pe)
                pe.sem_inc(p7_z, 2)
                with pe.Fori(0, T // 2) as i:
                    for b in range(2):
                        pe.wait_ge(p7_c[b], i * 16 + 16)
                        pe.wait_ge(p7_z, i * 2 + (b + 1))
                        aggregate(pe, y2, i * 2 + b, b, flag, p7_low).then_inc(p7_agg, 1)

            @block.scalar
            def _(act):
                act.sem_inc(p7_new, 2)
                with act.Fori(0, T // 2) as i:
                    for b in range(2):
                        t = i * 2 + b
                        one = bass.ds(t, 1)
                        act.wait_ge(p7_new, t + 1)
                        act.dma_start(xbuf[:, b], x_t[one].rearrange("t p n -> (t p) n")).then_inc(p7_xu[b], 16)
                        act.dma_start(ubuf7[:, b], mix_dram[one].rearrange("t p n -> (t p) n")).then_inc(p7_xu[b], 16)
                        act.wait_ge(p7_pre, t * 4 + 3)
                        act.activation(zbuf[:, b], zbuf[:, b], ACT.Gelu).then_inc(p7_gelu, 1)

            @block.vector
            def _(dve):
                def first_half(t, b, i):
                    one = bass.ds(t, 1)
                    dve.wait_ge(p7_xu[b], i * 32 + 32)
                    dve.tensor_scalar(xnbuf[:, b], xbuf[:, b], xmean[:, one], xrstd[:, one], ALU.subtract, ALU.mult
                                      ).then_inc(p7_xn, 1)
                    dve.scalar_tensor_tensor(out=ubuf7[:, b], in0=ubuf7[:, b], scalar=mixs[:, one], in1=rows[:, MIXC],
                                             op0=ALU.mult, op1=ALU.add).then_inc(p7_mix, 1)
                    dve.wait_ge(p7_xn, t + 1)
                    dve.wait_ge(p7_mix, t * 2 + 1)
                    dve.scalar_tensor_tensor(out=ubuf7[:, b], in0=ubuf7[:, b], scalar=0.0, in1=xnbuf[:, b],
                                             op0=ALU.max, op1=ALU.add).then_inc(p7_mix, 1)
                    dve.wait_ge(p7_agg, t + 1)
                    dve.scalar_tensor_tensor(out=zbuf[:, b], in0=ps[:, b, :], scalar=f_z2[:, one], in1=rows[:, B2],
                                             op0=ALU.mult, op1=ALU.add).then_inc(p7_z, 1)
                    dve.wait_ge(p7_z, t + 3)
                    dve.bn_stats(stats[:, b], zbuf[:, b]).then_inc(p7_stats, 1)
                    wait_apart(dve, p7_stats, t + 1, passed)
                    dve.bn_aggr(aggr[:, b], stats[:, b]).then_inc(p7_aggr, 1)
                    dve.wait_ge(p7_aggr, t + 1)
                    dve.tensor_scalar(veps[:, b:b + 1], aggr[:, b, 1:2], EPS, None, ALU.add).then_inc(p7_var, 1)
                    dve.wait_ge(p7_rstd, t + 1)
                    dve.tensor_scalar(zbuf[:, b], zbuf[:, b], aggr[:, b, 0:1], rstd6[:, b:b + 1],
                                      ALU.subtract, ALU.mult).then_inc(p7_norm, 1)

                def second_half(t, b):
                    one = bass.ds(t, 1)
                    new = xnew[:, one, :].rearrange("p t n -> p (t n)")
                    dve.wait_ge(p7_gelu, t + 1)
                    dve.wait_ge(p7_pre, t * 4 + 4)
                    dve.tensor_tensor(new, ubuf7[:, b], zbuf[:, b], ALU.add).then_inc(p7_new, 1)
                    wait_apart(dve, p7_new, t + 3, passed)
                    dve.bn_stats(nst[:, b], new).then_inc(p7_nst, 1)
                    wait_apart(dve, p7_nst, t + 1, passed)
                    dve.bn_aggr(nag[:, b], nst[:, b]).then_inc(p7_nag, 1)
                    dve.wait_ge(p7_nag, t + 1)
                    dve.tensor_copy(nmean[:, one], nag[:, b, 0:1])
                    dve.tensor_scalar(nveps[:, b:b + 1], nag[:, b, 1:2], EPS, None, ALU.add).then_inc(p7_nvar, 1)
                    dve.wait_ge(p7_nrstd, t + 1)
                    dve.tensor_scalar(dev[:, b], new, nag[:, b, 0:1], nrstd[:, one], ALU.subtract, ALU.mult
                                      ).then_inc(p7_dev, 1)
                    dve.wait_ge(p7_dev, t + 1)
                    dve.tensor_reduce(namax[:, one], dev[:, b], AX.X, ALU.max, apply_absolute_value=True
                                      ).then_inc(p7_amax, 1)

                first_half(0, 0, 0)
                first_half(1, 1, 0)
                second_half(0, 0)
                with dve.Fori(0, LOOPS) as i:
                    for b in range(2):
                        first_half(i * 2 + (b + 2), b, i + 1)
                        second_half(i * 2 + (b + 1), 1 - b)
                second_half(T - 1, 1)

            @block.gpsimd
            def _(pool):
                def first_half(t, b):
                    pool.wait_ge(p7_var, t + 1)
                    pool.tensor_tensor(rstd6[:, b:b + 1], veps[:, b:b + 1], half[:, 0:1], ALU.pow).then_inc(p7_rstd, 1)
                    pool.wait_ge(p7_norm, t + 1)
                    pool.tensor_tensor(zbuf[:, b], zbuf[:, b], rows[:, G2], ALU.mult).then_inc(p7_pre, 1)
                    pool.wait_ge(p7_pre, t * 4 + 1)
                    pool.tensor_tensor(zbuf[:, b], zbuf[:, b], rows[:, BE2], ALU.add).then_inc(p7_pre, 1)
                    pool.wait_ge(p7_pre, t * 4 + 2)
                    pool.tensor_tensor(zbuf[:, b], zbuf[:, b], xnbuf[:, b], ALU.add).then_inc(p7_pre, 1)
                    pool.wait_ge(p7_mix, t * 2 + 2)
                    pool.tensor_tensor(ubuf7[:, b], ubuf7[:, b], xbuf[:, b], ALU.add).then_inc(p7_pre, 1)

                def second_half(t, b):
                    pool.wait_ge(p7_nvar, t + 1)
                    pool.tensor_tensor(nrstd[:, bass.ds(t, 1)], nveps[:, b:b + 1], half[:, 0:1], ALU.pow
                                       ).then_inc(p7_nrstd, 1)

                first_half(0, 0)
                first_half(1, 1)
                second_half(0, 0)
                with pool.Fori(0, LOOPS) as i:
                    for b in range(2):
                        first_half(i * 2 + (b + 2), b)
                        second_half(i * 2 + (b + 1), 1 - b)
                second_half(T - 1, 1)

        q32 = pair_of(0)
        qpow = pair_of(1024)
        qbf = z32(2048, D).bitcast(BF16).rearrange("p (b n) -> p b n", b=2)
        qT = z32(2560, D).bitcast(BF16).rearrange("p (b k n) -> p b k n", b=2, k=K)
        obuf = pair_of(3072)
        qscale = z32(4096, T)
        qshift = z32(4096 + T, T)
        p8_setup = sem("p8_setup_steps")
        p8_max = sem("p8_maximum_ready")
        p8_all = sem("p8_maximum_over_partitions")
        p8_scaled = sem("p8_scaled")
        p8_q = sem("p8_quantise_steps")
        p8_big = sem("p8_rounding_added")
        p8_qbf = sem("p8_rounded")
        p8_turned = sem("p8_transposed")
        p8_qt = sem("p8_transposes_copied")
        p8_mm = sem("p8_products")
        p8_o = sem("p8_outputs_ready")
        p8_out = [sem(f"p8_outputs_stored{b}") for b in range(2)]
        p8_ofree = sem("p8_output_buffers_free")
        QS = 3

        with nc.Block() as block:
            @block.gpsimd
            def _(pool):
                pool.wait_ge(p8_max, 1)
                pool.partition_all_reduce(c(A_X), c(TMP), P, RMAX).then_inc(p8_all, 1)
                with pool.Fori(0, T // 2) as i:
                    for b in range(2):
                        t = i * 2 + b
                        pool.wait_ge(p8_q, t * QS + QS)
                        pool.tensor_tensor(q32[:, b], q32[:, b], qpow[:, b], ALU.add).then_inc(p8_big, 1)

            @block.vector
            def _(dve):
                link = chain(dve, p8_setup)
                link(dve.tensor_tensor(namax[:], namax[:], rowmask[:], ALU.mult))
                dve.tensor_reduce(c(TMP), namax[:], AX.X, ALU.max).then_inc(p8_max, 1)
                dve.wait_ge(p8_all, 1)
                link(dve.tensor_scalar(c(TMP), c(A_X), 1e-12, None, ALU.max))
                link(dve.reciprocal(c(TMP2), c(TMP)))
                link(dve.tensor_scalar(c(X_SC), c(TMP2), FP8_MAX, None, ALU.mult))
                link(dve.reciprocal(c(TMP), c(X_SC)))
                link(dve.reciprocal(c(TMP2), c(W_SC)))
                link(dve.tensor_tensor(c(X_F), c(TMP), c(TMP2), ALU.mult))
                link(dve.tensor_scalar(qscale, nrstd[:], c(X_SC), None, ALU.mult))
                link(dve.scalar_tensor_tensor(out=qshift, in0=nmean[:], scalar=-1.0, in1=qscale,
                                              op0=ALU.mult, op1=ALU.mult))

                def quantise(t, b):
                    n = t * QS
                    dve.wait_ge(p8_scaled, t + 1)
                    dve.tensor_scalar(q32[:, b], q32[:, b], FP8_MAX, -FP8_MAX, ALU.min, ALU.max).then_inc(p8_q, 1)
                    dve.wait_ge(p8_q, n + 1)
                    dve.tensor_scalar(qpow[:, b].bitcast(I32), q32[:, b].bitcast(I32), EXPONENT, None,
                                      ALU.bitwise_and).then_inc(p8_q, 1)
                    dve.wait_ge(p8_q, n + 2)
                    dve.tensor_scalar(qpow[:, b], qpow[:, b], 2.0 ** -6, 1.5 * 2.0 ** 20, ALU.max, ALU.mult
                                      ).then_inc(p8_q, 1)

                def rounded(t, b):
                    dve.wait_ge(p8_big, t + 1)
                    dve.wait_ge(p8_turned, t + 1)
                    dve.tensor_tensor(qbf[:, b], q32[:, b], qpow[:, b], ALU.subtract).then_inc(p8_qbf, 1)

                def output(t, b):
                    dve.wait_ge(p8_mm, t + 1)
                    dve.wait_ge(p8_ofree, t + 1)
                    dve.scalar_tensor_tensor(out=obuf[:, b], in0=ps[:, 2 + b, :], scalar=c(X_F),
                                             in1=xnew[:, bass.ds(t, 1), :].rearrange("p t n -> p (t n)"),
                                             op0=ALU.mult, op1=ALU.add).then_inc(p8_o, 1)

                quantise(0, 0)
                quantise(1, 1)
                rounded(0, 0)
                with dve.Fori(0, LOOPS) as i:
                    for b in range(2):
                        quantise(i * 2 + (b + 2), b)
                        rounded(i * 2 + (b + 1), 1 - b)
                        output(i * 2 + b, b)
                rounded(T - 1, 1)
                for b in range(2):
                    output(T - 2 + b, b)

            @block.tensor
            def _(pe):
                def turn(t, b):
                    pe.wait_ge(p8_qbf, t + 3)
                    pe.wait_ge(p8_qt, t + 1)
                    bank = ps[:, b, 0:D // 2].bitcast(BF16)
                    for k in range(K):
                        ins = pe.transpose(bank[:, k * P:(k + 1) * P], qbf[:, b, k * P:(k + 1) * P], identb[:])
                    ins.then_inc(p8_turned, 1)

                def multiply(t, b):
                    pe.wait_ge(p8_qt, t + 3)
                    pe.wait_ge(p8_o, t + 1)
                    for k in range(K):
                        ins = pe.matmul(ps[:, 2 + b, :], qT[:, b, k, :], wffn[:, k, :], start=(k == 0), stop=(k == K - 1))
                    ins.then_inc(p8_mm, 1)

                pe.sem_inc(p8_qt, 2)
                pe.sem_inc(p8_o, 2)
                pe.sem_inc(p8_turned, 2)
                turn(0, 0)
                with pe.Fori(0, LOOPS) as i:
                    for b in range(2):
                        turn(i * 2 + (b + 1), 1 - b)
                        multiply(i * 2 + b, b)
                turn(T - 1, 1)
                multiply(T - 2, 0)
                multiply(T - 1, 1)

            @block.scalar
            def _(act):
                def scaled(t, b):
                    one = bass.ds(t, 1)
                    act.wait_ge(p8_qbf, t + 1)
                    act.activation(q32[:, b], xnew[:, one, :].rearrange("p t n -> p (t n)"), ACT.Identity,
                                   bias=qshift[:, one], scale=qscale[:, one]).then_inc(p8_scaled, 1)

                def turned(t, b):
                    act.wait_ge(p8_turned, t + 3)
                    act.wait_ge(p8_o, t + 1)
                    act.copy(qT[:, b].rearrange("p k n -> p (k n)"), ps[:, b, 0:D // 2].bitcast(BF16)
                             ).then_inc(p8_qt, 1)

                act.sem_inc(p8_qbf, 2)
                act.wait_ge(p8_setup, 9)
                scaled(0, 0)
                scaled(1, 1)
                with act.Fori(0, LOOPS) as i:
                    for b in range(2):
                        scaled(i * 2 + (b + 2), b)
                        turned(i * 2 + b, b)
                turned(T - 2, 0)
                turned(T - 1, 1)

            @block.sync
            def _(sp):
                sp.sem_inc(p8_ofree, 2)
                with sp.Fori(0, T // 2) as i:
                    for b in range(2):
                        t = i * 2 + b
                        sp.wait_ge(p8_o, t + 3)
                        sp.dma_start(out_t[bass.ds(t, 1)].rearrange("t p n -> (t p) n"), obuf[:, b]
                                     ).then_inc(p8_out[b], 16)
                    for b in range(2):
                        sp.wait_ge(p8_out[b], i * 16 + 16)
                    sp.sem_inc(p8_ofree, 2)


_VECTORS = {"b1": "L0_gnn_b1", "g1": "L0_gnn_gamma1", "be1": "L0_gnn_beta1", "b2": "L0_gnn_b2",
            "g2": "L0_gnn_gamma2", "be2": "L0_gnn_beta2", "bq": "L0_mix_bq", "bk": "L0_mix_bk", "bv": "L0_mix_bv",
            "bo": "L0_mix_bo", "scale": "L0_mix_bn_scale", "bias": "L0_mix_bn_bias", "mean": "L0_mix_bn_mean",
            "var": "L0_mix_bn_var"}
_MATRICES = {"Wq": "L0_mix_Wq", "Wk": "L0_mix_Wk", "Wv": "L0_mix_Wv", "Wo": "L0_mix_Wo", "W1": "L0_gnn_W1",
             "W2": "L0_gnn_W2", "Wf": "L0_ffn_weight"}


def kernel(**inputs):
    import numpy as np
    import concourse.bacc as bacc
    from concourse import mybir as mb
    from concourse.bass_utils import run_bass_kernel_spmd as run

    nc = bacc.Bacc("TRN2", target_bir_lowering=False, num_devices=1)
    x = np.zeros((NP, D), np.asarray(inputs["x"]).dtype)
    x[:N] = inputs["x"]
    src, dst = np.asarray(inputs["src"]), np.asarray(inputs["dst"])
    edges = np.zeros(((CH + 1), 2, P), src.dtype)
    edges[:, 1] = 2 * NP
    for v, a in enumerate((src, dst)):
        full = E // P
        edges[:full, v] = a[:full * P].reshape(full, P)
        edges[full, v, :E - full * P] = a[full * P:]
    arrays = {"in_x": x, "in_edges": edges}
    for short, name in {**_VECTORS, **_MATRICES}.items():
        arrays["in_" + short] = np.ascontiguousarray(inputs[name])
    aps = {k: nc.dram_tensor(k, v.shape, mb.dt.from_np(v.dtype), kind="ExternalInput").ap() for k, v in arrays.items()}
    out = nc.dram_tensor("out", (NP, D), mb.dt.float32, kind="ExternalOutput").ap()
    gps_layer_kernel(nc, aps["in_x"], aps["in_edges"], {k[3:]: v for k, v in aps.items()}, out)
    r = run(nc, [arrays], core_ids=[0])
    return r.results[0]["out"][:N]
```

```python
from contextlib import ExitStack

import concourse.bass as bass
from concourse import mybir

ALU = mybir.AluOpType
ACT = mybir.ActivationFunctionType
AX = mybir.AxisListType
F32 = mybir.dt.float32
F16 = mybir.dt.float16
BF16 = mybir.dt.bfloat16
I32 = mybir.dt.int32
RMAX = bass.bass_isa.ReduceOp.max
RADD = bass.bass_isa.ReduceOp.add

P = 128
N = 3750
D = 512
K = D // P
T = -(-N // P)
NP = T * P
E = 123750
CH = -(-E // P)
WIN = 8
WPT = P // WIN
NWIN = T * WPT
SPAN = 4
ACT_SPAN = 1
POOL_CHUNK = ACT_SPAN
AHEAD = 4
CODES = T * WIN
QW = 4
PW = NWIN // QW
GROUPS = [(g, min(512, N - g)) for g in range(0, N, 512)]
FAR = 16384.0
XSCALE = 1024.0
ROOT_D = 22.7
TOP = 32768.0
EXPONENT = 0x7F800000
FP8_MAX = 448.0
EPS = 1e-5
LOOPS = (T - 2) // 2

B1, G1, BE1, B2, G2, BE2, MIXC = range(7)
WQ, WK, WV, WO, W1, W2, WF = range(7)
A_W1, A_W2, A_M, A_WVO, A_C, A_FFN, A_G1, A_BE1 = range(8)
S_W1, S_W2, S_M, S_WVO, S_G, S_Y1, S_H, S_Y2 = range(8, 16)
R_W1, R_W2, R_M, R_WVO, R_G, R_Y1, R_H, R_Y2 = range(16, 24)
F_U, F_G, F_S, F_Y1, F_Y2, X_SC, X_F, W_SC, BQBK, A_X, TMP, TMP2 = range(24, 36)


def wait_apart(eng, s, value, passed):
    eng.wait_ge(s, value)
    eng.sem_inc(passed, 1)


def low_part(dve, parts, raw, scale):
    return dve.scalar_tensor_tensor(out=parts[:, 1], in0=raw, scalar=scale, in1=parts[:, 0],
                                    op0=ALU.mult, op1=ALU.subtract)


def split_weight(dve, parts, raw, scale, link):
    link(dve.tensor_scalar(parts[:, 0], raw, scale, None, ALU.mult))
    link(low_part(dve, parts, raw, scale))


def store_tiles(sp, ready, start, store, stored, free):
    def one(t, b):
        sp.wait_ge(ready, t + (start + 1))
        store(t, b).then_inc(stored[b], 16)

    one(0, 0)
    with sp.Fori(0, LOOPS) as i:
        for b in (1, 0):
            one(i * 2 + (2 - b), b)
            sp.wait_ge(stored[1 - b], i * 16 + 16)
            sp.sem_inc(free, 1)
    one(T - 1, 1)
    for b in range(2):
        sp.wait_ge(stored[b], 16 * T // 2)


def split_product(pe, out, lhs, at, rhs):
    for k in range(K):
        for l, r in ((0, 0), (0, 1), (1, 0)):
            ins = pe.matmul(out, lhs[:, l, k, at], rhs[:, r, k, :], start=(k == 0 and l == 0 and r == 0),
                            stop=(k == K - 1 and l == 1))
    return ins


def gps_layer_kernel(nc, x, edges, w, out):
    counts_dram = nc.dram_tensor("counts_dram", [T, P, NP], F16).ap()
    low_counts_dram = nc.dram_tensor("low_counts_dram", [T, P, NP], F16).ap()
    mix_dram = nc.dram_tensor("mix_dram", [T, P, D], F32).ap()
    x_t = x.rearrange("(t p) d -> t p d", p=P)
    out_t = out.rearrange("(t p) d -> t p d", p=P)

    ctx = ExitStack()
    with ctx:
        def sb(name, shape, dt=F32):
            return ctx.enter_context(nc.sbuf_tensor(name, shape, dt))

        def sem(name):
            return ctx.enter_context(nc.semaphore(name))

        regionA = sb("regionA", [P, T * D])
        regionB = sb("regionB", [P, T * D])
        regionZ = sb("regionZ", [P, 12376])
        mparts = sb("mparts", [P, 2, K, D], F16)
        w12parts = sb("w12parts", [P, 2, K, D], F16)
        wffn = sb("wffn", [P, K, D], BF16)
        rows = sb("rows", [P, 7, D])
        ident = sb("ident", [P, P])
        ident16 = sb("ident16", [P, P], F16)
        identb = sb("identb", [P, P], BF16)
        col16 = sb("col16", [P, D], F16)
        ones = sb("ones", [P, 1])
        ones16 = sb("ones16", [P, 1], F16)
        half = sb("half", [P, T])
        rowmask = sb("rowmask", [P, T])
        deg = sb("deg", [P, T])
        cs = sb("cs", [P, T])
        missed = sb("missed", [P, 2])
        recount = sb("recount", [P, 1], I32)
        dinv = sb("dinv", [P, T])
        xmean = sb("xmean", [P, T])
        xrstd = sb("xrstd", [P, T])
        lowcols = sb("lowcols", [P, 2])
        rowbias = sb("rowbias", [P, T])
        mixs = sb("mixs", [P, T])
        nmean = sb("nmean", [P, T])
        nrstd = sb("nrstd", [P, T])
        namax = sb("namax", [P, T])
        f_y1 = sb("f_y1", [P, T])
        f_z1 = sb("f_z1", [P, T])
        f_y2 = sb("f_y2", [P, T])
        f_z2 = sb("f_z2", [P, T])
        sc = sb("sc", [P, 36])
        wide = sb("wide", [P, 8])
        cg = sb("cg", [P, 2, K])
        stats = sb("stats", [P, 2, 6])
        nst = sb("nst", [P, 2, 6])
        nag = sb("nag", [P, 2, 2])
        nveps = sb("nveps", [P, 2])
        aggr = sb("aggr", [P, 2, 2])
        veps = sb("veps", [P, 2])
        xdot = sb("xdot", [P, 2])
        mx = sb("mx", [P, 2, 8])
        soft = sb("soft", [P, 2, 5])
        bcols = sb("bcols", [P, 4, K])
        ps = ctx.enter_context(nc.psum_tensor("ps", [P, 8, 512], F32))

        xparts = regionA[:, :].bitcast(F16).rearrange("p (h k n) -> p h k n", h=2, k=K)
        y1 = regionB[:, :].bitcast(F16).rearrange("p (t h n) -> p t h n", t=T, h=2)
        y2 = regionA[:, :].bitcast(F16).rearrange("p (t h n) -> p t h n", t=T, h=2)
        xnew = regionB[:, :].rearrange("p (t n) -> p t n", t=T)

        def z32(at, n):
            return regionZ[:, at:at + n]

        def c(i):
            return sc[:, i:i + 1]

        passed = sem("waits_passed")
        dve_steps = sem("vector_engine_steps")

        wvoparts = z32(0, 2048).bitcast(F16).rearrange("p (h k n) -> p h k n", h=2, k=K)
        bvorow = z32(2048, D)
        wqbkrow = z32(2560, D)
        NJ = QW * SPAN
        NE = NJ * P
        tables = regionZ[0:PW, 7168:7168 + 2 * NE].bitcast(I32).rearrange("p (j v e) -> p j v e", j=NJ, v=2)
        t_src, t_dst = tables[:, :, 0, :], tables[:, :, 1, :]
        t_code = regionZ[0:PW, 3072:3072 + NE].rearrange("p (j e) -> p j e", j=NJ)
        t_far = regionZ[0:PW, 5120:5120 + NE].rearrange("p (j e) -> p j e", j=NJ)
        lastdst = regionZ[0:1, 3072:3072 + CH]
        lastdst_f = regionZ[0:1, 4096:4096 + CH]
        behind = z32(5120, 512)
        xin = z32(3072, 2 * D).rearrange("p (b n) -> p b n", b=2)
        norm_x = [sem(f"norm_x_loaded{b}") for b in range(2)]
        oneblock = z32(5632, P)
        mixrows = w12parts[:, :, :, :].rearrange("p h k n -> p (h k n)").bitcast(F32).rearrange("p (r n) -> p r n", r=4)
        wraw = regionA[:, 0:7 * K * D].rearrange("p (w k n) -> p w k n", w=7, k=K)
        reps = regionA[:, 7 * K * D:7 * K * D + 2 * D].rearrange("p (b k n) -> p b k n", b=2, k=K)

        wt = regionB[:, 0:3 * K * D].rearrange("p (w k n) -> p w k n", w=3, k=K)
        mraw = regionB[:, 3 * K * D:4 * K * D].rearrange("p (k n) -> p k n", k=K)
        wvoraw = regionB[:, 4 * K * D:5 * K * D].rearrange("p (k n) -> p k n", k=K)
        reps2 = regionB[:, 5 * K * D:5 * K * D + D].rearrange("p (k n) -> p k n", k=K)
        vardiag = regionB[:, 10752:10752 + D].rearrange("p (k n) -> p k n", k=K)
        onesq = regionB[:, 11264:11264 + P]
        onerow = regionB[0:1, 11392:11392 + P]
        BO, MEAN, SCALE, BIAS = range(4)
        BQ, BK, BV, VAR = range(4)
        rep = [reps[:, 0], reps[:, 1], reps2]
        at = T * D - 2 * SPAN * NWIN
        code = regionB[:, at:at + SPAN * NWIN].rearrange("p (s w) -> p s w", s=SPAN)
        low = regionB[:, at + SPAN * NWIN:T * D].rearrange("p (s w) -> p s w", s=SPAN)

        thr = sb("thr", [P, QW])
        starts = sb("starts", [P, QW, 3])
        chunkf = sb("chunkf", [P, NJ])
        chunki = sb("chunki", [P, NJ], I32)

        wsem = [sem(f"weight_loaded{i}") for i in range(7)]
        rows_loaded = sem("rows_loaded")
        mixrows_loaded = sem("mix_rows_loaded")
        cols_loaded = sem("bias_columns_loaded")
        last_loaded = sem("last_destinations_loaded")
        prep_const = sem("prep_constants")
        prep_zeroed = sem("prep_zeroed")
        prep_lastf = sem("prep_last_destinations_float")
        prep_rep = sem("prep_last_destinations_repeated")
        prep_chunks = sem("prep_chunks_of_windows")
        prep_gathered = sem("prep_edges_gathered")
        prep_coded = sem("prep_edges_coded")
        prep_turned = sem("prep_codes_transposed")
        prep_kept = sem("prep_codes_kept")
        weights_rep = sem("weights_bias_columns_repeated")
        weights_turned = sem("weights_weights_transposed")
        weights_turned_out = sem("weights_transposes_copied")
        weights_made = sem("weights_products_made")
        weights_out = sem("weights_products_copied")
        weights_var = sem("weights_variance_ready")
        weights_root = sem("weights_root_ready")
        weights_diag = sem("weights_root_diagonal_ready")
        weights_scales = sem("weights_scales_ready")
        weights_high = sem("weights_high_parts_ready")
        weights_max = sem("weights_maxima_ready")
        weights_all = sem("weights_maxima_over_partitions")

        counted = {}

        def chain(eng, s):
            def link(ins):
                counted[s.name] = counted.get(s.name, 0) + 1
                ins.then_inc(s, 1)
                eng.wait_ge(s, counted[s.name])
            return link

        with nc.Block() as block:
            @block.sync
            def _(sp):
                with nc.allow_non_contiguous_dma(reason="one word of each chunk, 967 in all"):
                    sp.dma_start(lastdst.bitcast(I32), edges[0:CH, 1, P - 1:P].rearrange("c e -> e c")
                                 ).then_inc(last_loaded, 16)
                with nc.allow_non_contiguous_dma(reason="four vectors of 512 words down the partitions"):
                    for r, name in enumerate(("bq", "bk", "bv", "var")):
                        sp.dma_start(bcols[:, r], w[name].rearrange("(k p) -> p k", p=P)).then_inc(cols_loaded, 16)
                for i, name in ((WQ, "Wq"), (WK, "Wk"), (WV, "Wv"), (WO, "Wo"), (W1, "W1"), (W2, "W2"), (WF, "Wf")):
                    sp.dma_start(wraw[:, i], w[name].rearrange("(k p) n -> p k n", p=P)).then_inc(wsem[i], 16)
                for r, name in ((BO, "bo"), (MEAN, "mean"), (SCALE, "scale"), (BIAS, "bias")):
                    sp.dma_start(mixrows[:, r], w[name].rearrange("(a n) -> a n", a=1).to_broadcast([P, D])
                                 ).then_inc(mixrows_loaded, 16)
                for r, name in ((B1, "b1"), (G1, "g1"), (BE1, "be1"), (B2, "b2"), (G2, "g2"), (BE2, "be2")):
                    sp.dma_start(rows[:, r], w[name].rearrange("(a n) -> a n", a=1).to_broadcast([P, D])
                                 ).then_inc(rows_loaded, 16)

                sp.wait_ge(prep_turned, NJ)
                for b in range(2):
                    sp.dma_start(xin[:, b], x_t[b]).then_inc(norm_x[b], 16)

            @block.gpsimd
            def _(pool):
                pool.memset(ident[:], 0.0).then_inc(prep_zeroed, 1)
                pool.memset(ident16[:], 0.0).then_inc(prep_zeroed, 1)
                pool.memset(identb[:], 0.0).then_inc(prep_zeroed, 1)
                pool.memset(rowmask[:], 1.0).then_inc(prep_zeroed, 1)
                pool.iota(thr[:], pattern=[[WIN * PW, QW]], base=0, channel_multiplier=WIN,
                          allow_small_or_imprecise_dtypes=True).then_inc(prep_const, 1)
                pool.memset(onerow, 1.0).then_inc(prep_const, 1)
                pool.memset(half[:], -0.5).then_inc(prep_const, 1)
                pool.wait_ge(prep_zeroed, 4)
                for t in (ident, ident16, identb):
                    pool.affine_select(out=t[:], in_=t[:], compare_op=ALU.not_equal, fill=1.0, base=0,
                                       pattern=[[-1, P]], channel_multiplier=1).then_inc(prep_const, 1)
                pool.affine_select(out=rowmask[:], in_=rowmask[:], compare_op=ALU.is_gt, fill=0.0, base=N,
                                   pattern=[[-P, T]], channel_multiplier=-1).then_inc(prep_const, 1)
                pool.iota(col16[:], pattern=[[1, D]], base=0, channel_multiplier=0,
                          allow_small_or_imprecise_dtypes=True).then_inc(prep_const, 1)
                pool.memset(ones[:], 1.0).then_inc(prep_const, 1)
                pool.memset(ones16[:], 1.0).then_inc(prep_const, 1)
                pool.wait_ge(prep_const, 10)
                pool.wait_ge(weights_var, 1)
                pool.tensor_tensor(bcols[:, VAR], bcols[:, VAR], half[:, 0:K], ALU.pow).then_inc(weights_root, 1)
                pool.wait_ge(prep_chunks, 1)
                for j in range(NJ):
                    pool.indirect_dma_start(
                        out=tables[:, j].rearrange("p v e -> p (v e)"), out_offset=None,
                        in_=edges.rearrange("c v e -> c (v e)"),
                        in_offset=bass.IndirectOffsetOnAxis(ap=chunki[0:PW, j:j + 1], axis=0),
                    ).then_inc(prep_gathered, 16)
                pool.wait_ge(weights_max, 1)
                pool.partition_all_reduce(sc[:, 0:8], wide[:], P, RMAX).then_inc(weights_all, 1)

            @block.tensor
            def _(pe):
                pe.wait_ge(prep_const, 10)
                pe.wait_ge(prep_lastf, 1)
                pe.matmul(ps[:, 0, 0:512], onerow, lastdst_f[:, 0:512], start=True, stop=True)
                pe.matmul(ps[:, 1, 0:CH - 512], onerow, lastdst_f[:, 512:CH], start=True, stop=True
                          ).then_inc(prep_rep, 1)
                for j in range(3 * K):
                    m, i = divmod(j, K)
                    if i == 0:
                        pe.wait_ge(wsem[m], 16)
                    if j >= 6:
                        pe.wait_ge(weights_turned_out, j - 5)
                    for a in range(K):
                        ins = pe.transpose(ps[:, 2 + j % 6, a * P:(a + 1) * P], wraw[:, m, a, i * P:(i + 1) * P], ident[:])
                    ins.then_inc(weights_turned, 1)
                pe.wait_ge(weights_turned_out, 3 * K)
                pe.wait_ge(prep_chunks, 1)
                for a in range(K):
                    for i in range(K):
                        ins = pe.matmul(ps[:, a, :], wt[:, WQ, i, a * P:(a + 1) * P], wt[:, WK, i, :],
                                        start=(i == 0), stop=(i == K - 1))
                    ins.then_inc(weights_made, 1)
                pe.wait_ge(wsem[WO], 16)
                for a in range(K):
                    for i in range(K):
                        ins = pe.matmul(ps[:, 4 + a, :], wt[:, WV, i, a * P:(a + 1) * P], wraw[:, WO, i, :],
                                        start=(i == 0), stop=(i == K - 1))
                    ins.then_inc(weights_made, 1)
                pe.wait_ge(weights_diag, 1)
                pe.wait_ge(weights_out, K)
                for k in range(K):
                    ins = pe.matmul(ps[:, 0, k * P:(k + 1) * P], onesq, vardiag[:, k], start=True, stop=True)
                ins.then_inc(weights_made, 1)
                pe.wait_ge(weights_rep, 1)
                for i in range(K):
                    ins = pe.matmul(ps[:, 1, :], rep[BK][:, i], wt[:, WQ, i, :], start=(i == 0), stop=(i == K - 1))
                ins.then_inc(weights_made, 1)
                for i in range(K):
                    ins = pe.matmul(ps[:, 2, :], rep[BV][:, i], wraw[:, WO, i, :], start=(i == 0), stop=(i == K - 1))
                ins.then_inc(weights_made, 1)
                for b in range(K):
                    for i in range(K):
                        ins = pe.matmul(ps[:, 3, b:b + 1], wt[:, WK, i, b * P:(b + 1) * P], bcols[:, BQ, i:i + 1],
                                        start=(i == 0), stop=(i == K - 1))
                for i in range(K):
                    ins = pe.matmul(ps[:, 3, K:K + 1], rep[BQ][:, i], bcols[:, BK, i:i + 1],
                                    start=(i == 0), stop=(i == K - 1))
                ins.then_inc(weights_made, 1)
                pe.wait_ge(weights_out, K + 2)
                pe.wait_ge(prep_coded, 1)
                for j in range(NJ):
                    if j >= 2:
                        pe.wait_ge(prep_kept, j - 1)
                    pe.transpose(ps[:, j % 2, 0:PW], t_code[:, j], ident[0:PW, 0:PW])
                    pe.transpose(ps[:, j % 2, P:P + PW], t_src[:, j].bitcast(F32), ident[0:PW, 0:PW]
                                 ).then_inc(prep_turned, 1)

            @block.scalar
            def _(act):
                for j in range(3 * K):
                    m, i = divmod(j, K)
                    act.wait_ge(weights_turned, j + 1)
                    act.copy(wt[:, m, i, :], ps[:, 2 + j % 6, :]).then_inc(weights_turned_out, 1)
                for a in range(K):
                    act.wait_ge(weights_made, a + 1)
                    act.copy(mraw[:, a, :], ps[:, a, :]).then_inc(weights_out, 1)
                for j in range(NJ):
                    g, s = divmod(j, SPAN)
                    act.wait_ge(prep_turned, j + 1)
                    act.copy(code[:, s, g * PW:(g + 1) * PW], ps[:, j % 2, 0:PW])
                    act.activation(low[:, s, g * PW:(g + 1) * PW], ps[:, j % 2, P:P + PW], ACT.Copy,
                                   scale=-1.0 if s < ACT_SPAN else 1.0).then_inc(prep_kept, 1)
                act.wait_ge(weights_scales, 1)
                for parts, raw, s in ((w12parts, wraw[:, W1], S_W1), (mparts, mraw, S_M)):
                    act.activation(parts[:, 0], raw, ACT.Copy, scale=c(s)).then_inc(weights_high, 1)

            @block.vector
            def _(dve):
                link = chain(dve, dve_steps)
                dve.wait_ge(last_loaded, 16)
                dve.tensor_copy(lastdst_f, lastdst.bitcast(I32)).then_inc(prep_lastf, 1)
                dve.wait_ge(cols_loaded, 16 * 4)
                dve.tensor_scalar(bcols[:, VAR], bcols[:, VAR], EPS, None, ALU.add).then_inc(weights_var, 1)
                dve.wait_ge(prep_const, 10)
                dve.wait_ge(prep_rep, 1)
                for g in range(QW):
                    for h, (a, n) in enumerate(((0, 512), (512, CH - 512))):
                        link(dve.tensor_scalar(behind[:, 0:n], ps[:, h, 0:n], thr[:, g:g + 1], None, ALU.is_lt,
                                               ALU.add, accum_out=starts[:, g, h:h + 1]))
                    link(dve.tensor_tensor(starts[:, g, 2:3], starts[:, g, 0:1], starts[:, g, 1:2], ALU.add))
                    for s in range(SPAN):
                        ins = dve.tensor_scalar(chunkf[:, g * SPAN + s:g * SPAN + s + 1], starts[:, g, 2:3],
                                                float(s), float(CH), ALU.add, ALU.min)
                    link(ins)
                dve.tensor_copy(chunki[:], chunkf[:]).then_inc(prep_chunks, 1)

                link = chain(dve, dve_steps)
                dve.wait_ge(prep_chunks, 1)
                link(dve.memset(oneblock, 1.0))
                for b in range(3):
                    for i in range(K):
                        ins = dve.tensor_scalar(rep[b][:, i], oneblock, bcols[:, b, i:i + 1], None, ALU.mult)
                link(ins)
                dve.sem_inc(weights_rep, 1)
                dve.wait_ge(weights_root, 1)
                for k in range(K):
                    ins = dve.tensor_scalar(vardiag[:, k], ident[:], bcols[:, VAR, k:k + 1], None, ALU.mult)
                link(ins)
                dve.memset(onesq, 1.0).then_inc(weights_diag, 1)

                def largest(i, ap):
                    return dve.tensor_reduce(wide[:, i:i + 1], ap, AX.X, ALU.max, apply_absolute_value=True)

                def flat(ap):
                    return ap.rearrange("p k n -> p (k n)")
                for i, a in ((W1, A_W1), (W2, A_W2), (WF, A_FFN)):
                    dve.wait_ge(wsem[i], 16)
                    largest(a, flat(wraw[:, i]))
                dve.wait_ge(weights_out, K)
                largest(A_M, flat(mraw))
                src_f, dst_f = t_src.bitcast(F32), t_dst.bitcast(F32)
                dve.wait_ge(prep_gathered, 16 * NJ)
                link(dve.tensor_scalar(t_code.bitcast(I32), t_src, 7, None, ALU.logical_shift_right))
                link(dve.tensor_scalar(t_src, t_src, P - 1, None, ALU.bitwise_and))
                link(dve.tensor_copy(t_code, t_code.bitcast(I32)))
                link(dve.tensor_copy(src_f, t_src))
                link(dve.tensor_copy(dst_f, t_dst))
                for g in range(QW):
                    js = slice(g * SPAN, (g + 1) * SPAN)
                    ins = dve.tensor_scalar(dst_f[:, js], dst_f[:, js], thr[0:PW, g:g + 1], None, ALU.subtract)
                link(ins)
                link(dve.scalar_tensor_tensor(out=t_code, in0=t_code, scalar=float(WIN), in1=dst_f,
                                              op0=ALU.mult, op1=ALU.add))
                link(dve.tensor_scalar(t_far, dst_f, 0.0, FAR, ALU.is_lt, ALU.mult))
                link(dve.tensor_scalar(dst_f, dst_f, float(WIN), FAR, ALU.is_ge, ALU.mult))
                link(dve.tensor_tensor(t_far, t_far, dst_f, ALU.add))
                dve.tensor_tensor(t_code, t_code, t_far, ALU.add).then_inc(prep_coded, 1)
                dve.wait_ge(mixrows_loaded, 16 * 4)
                dve.wait_ge(weights_made, 2 * K + 1)
                link(dve.tensor_tensor(mixrows[:, SCALE], mixrows[:, SCALE], ps[:, 0, :], ALU.mult))
                dve.wait_ge(weights_made, 2 * K + 2)
                link(dve.tensor_copy(wqbkrow, ps[:, 1, :]))
                dve.sem_inc(weights_out, 2)
                link(dve.tensor_tensor(mixrows[:, BO], mixrows[:, BO], mixrows[:, MEAN], ALU.subtract))
                link(dve.tensor_tensor(mixrows[:, BO], mixrows[:, BO], mixrows[:, SCALE], ALU.mult))
                link(dve.tensor_tensor(rows[:, MIXC], mixrows[:, BO], mixrows[:, BIAS], ALU.add))
                for a in range(K):
                    ins = dve.tensor_tensor(wvoraw[:, a, :], ps[:, 4 + a, :], mixrows[:, SCALE], ALU.mult)
                link(ins)
                dve.wait_ge(weights_made, 2 * K + 3)
                link(dve.tensor_tensor(bvorow, ps[:, 2, :], mixrows[:, SCALE], ALU.mult))
                dve.wait_ge(weights_made, 2 * K + 4)
                link(dve.tensor_copy(cg[:, 0, :], ps[:, 3, 0:K]))
                link(dve.tensor_copy(c(BQBK), ps[:, 3, K:K + 1]))

                dve.wait_ge(rows_loaded, 16 * 6)
                largest(A_G1, rows[:, G1])
                largest(A_BE1, rows[:, BE1])
                for i, ap in ((A_WVO, flat(wvoraw)), (A_C, cg[:, 0, :])):
                    ins = largest(i, ap)
                link(ins)
                dve.sem_inc(weights_max, 1)
                dve.wait_ge(weights_all, 1)
                dve.tensor_copy(sc[:, S_W1:S_WVO + 1], sc[:, A_W1:A_WVO + 1])
                dve.scalar_tensor_tensor(out=c(S_G), in0=c(A_M), scalar=ROOT_D * ROOT_D, in1=c(A_C),
                                         op0=ALU.mult, op1=ALU.add)
                dve.tensor_scalar(c(S_Y1), c(A_W1), ROOT_D * ROOT_D, None, ALU.mult)
                dve.scalar_tensor_tensor(out=c(S_H), in0=c(A_G1), scalar=ROOT_D, in1=c(A_BE1),
                                         op0=ALU.mult, op1=ALU.add)
                link(dve.tensor_tensor(c(TMP), c(A_G1), c(A_BE1), ALU.add))
                link(dve.tensor_scalar(c(S_Y2), c(TMP), ROOT_D * ROOT_D, c(A_W2), ALU.mult, ALU.mult))
                scales = sc[:, S_W1:S_Y2 + 1]
                link(dve.tensor_scalar(scales, scales, 1e-20, None, ALU.max))
                link(dve.reciprocal(sc[:, R_W1:R_Y2 + 1], scales))
                link(dve.tensor_scalar(scales, sc[:, R_W1:R_Y2 + 1], TOP, None, ALU.mult))
                link(dve.tensor_scalar(scales.bitcast(I32), scales.bitcast(I32), EXPONENT, None, ALU.bitwise_and))
                dve.sem_inc(weights_scales, 1)
                link(dve.reciprocal(sc[:, R_W1:R_Y2 + 1], scales))
                dve.tensor_scalar(c(F_U), c(R_WVO), 1.0 / XSCALE, None, ALU.mult)
                dve.tensor_scalar(c(F_S), c(R_G), 1.0 / XSCALE, None, ALU.mult)
                dve.tensor_scalar(cg[:, 1, :], cg[:, 0, :], c(S_G), None, ALU.mult)
                for f, back, up in ((F_G, R_M, S_G), (F_Y1, R_W1, S_Y1)):
                    dve.scalar_tensor_tensor(out=c(f), in0=c(back), scalar=1.0 / XSCALE, in1=c(up),
                                             op0=ALU.mult, op1=ALU.mult)
                link(dve.tensor_tensor(c(F_Y2), c(R_W2), c(R_H), ALU.mult))
                link(dve.tensor_tensor(c(F_Y2), c(F_Y2), c(S_Y2), ALU.mult))
                split_weight(dve, wvoparts, wvoraw, c(S_WVO), link)
                dve.wait_ge(weights_high, 1)
                link(low_part(dve, w12parts, wraw[:, W1], c(S_W1)))

        xn = z32(4096, 2 * D).rearrange("p (b n) -> p b n", b=2)
        ubuf = z32(5120, 2 * D).rearrange("p (b n) -> p b n", b=2)
        junk = z32(6144, D)
        norm_u = [sem(f"norm_mix_stored{b}") for b in range(2)]
        norm_ufree = sem("norm_mix_buffers_free")
        norm_moments = sem("norm_moments")
        norm_var = sem("norm_variance_plus_eps")
        norm_rstd = sem("norm_rstd_ready")
        norm_xn = sem("norm_xn_ready")
        norm_bias = sem("norm_row_bias_done")
        norm_turned = sem("norm_xn_transposed")
        norm_xh = sem("norm_high_parts")
        norm_xl = sem("norm_low_parts")
        norm_wvo = sem("norm_wvo_product")
        norm_ubuf = sem("norm_mix_tile_scaled")
        norm_added = sem("norm_mix_tile_ready")
        norm_kept = sem("norm_mean_and_row_bias_kept")

        with nc.Block() as block:
            @block.sync
            def _(sp):
                store_tiles(sp, norm_added, 0, lambda t, b: sp.dma_start(
                    mix_dram[bass.ds(t, 1)].rearrange("t p n -> (t p) n"), ubuf[:, b]), norm_u, norm_ufree)

            @block.gpsimd
            def _(pool):
                def root(t, b):
                    pool.wait_ge(norm_var, t + 1)
                    pool.tensor_tensor(xrstd[:, bass.ds(t, 1)], veps[:, b:b + 1], half[:, 0:1], ALU.pow
                                       ).then_inc(norm_rstd, 1)

                def keep(t, b):
                    one = bass.ds(t, 1)
                    pool.wait_ge(norm_bias, t + 1)
                    pool.tensor_copy(xmean[:, one], aggr[:, b, 0:1])
                    pool.tensor_copy(rowbias[:, one], xdot[:, b:b + 1]).then_inc(norm_kept, 1)

                def add_bias(t, b):
                    pool.wait_ge(norm_ubuf, t + 3)
                    pool.tensor_tensor(ubuf[:, b], ubuf[:, b], bvorow, ALU.add).then_inc(norm_added, 1)

                root(0, 0)
                root(1, 1)
                keep(0, 0)
                root(2, 0)
                with pool.Fori(0, LOOPS - 1) as i:
                    for b in (1, 0):
                        keep(i * 2 + (2 - b), b)
                        root(i * 2 + (4 - b), b)
                        add_bias(i * 2 + (1 - b), 1 - b)
                keep(T - 3, 1)
                root(T - 1, 1)
                for t in (T - 2, T - 1):
                    keep(t, t % 2)
                for t in range(T - 4, T):
                    add_bias(t, t % 2)

            @block.vector
            def _(dve):
                def norm(t, b, i):
                    dve.wait_ge(norm_x[b], i * 16 + 16)
                    if not isinstance(t, int):
                        dve.wait_ge(norm_kept, t - 1)
                    dve.bn_stats(stats[:, b], xin[:, b]).then_inc(norm_moments, 1)
                    wait_apart(dve, norm_moments, t * 2 + 1, passed)
                    dve.bn_aggr(aggr[:, b], stats[:, b]).then_inc(norm_moments, 1)
                    dve.wait_ge(norm_moments, t * 2 + 2)
                    dve.tensor_scalar(veps[:, b:b + 1], aggr[:, b, 1:2], EPS, None, ALU.add).then_inc(norm_var, 1)

                def normalise(t, b):
                    dve.wait_ge(norm_rstd, t + 1)
                    dve.wait_ge(norm_turned, t + 1)
                    dve.tensor_scalar(xn[:, b], xin[:, b], aggr[:, b, 0:1], xrstd[:, bass.ds(t, 1)],
                                      ALU.subtract, ALU.mult).then_inc(norm_xn, 1)
                    dve.wait_ge(norm_xn, t + 1)
                    dve.tensor_tensor_reduce(out=junk, in0=xn[:, b], in1=wqbkrow, scale=1.0, scalar=0.0,
                                             op0=ALU.mult, op1=ALU.add, accum_out=xdot[:, b:b + 1]).then_inc(norm_bias, 1)

                def low_parts(t, b):
                    dve.wait_ge(norm_xh, t + 1)
                    at = bass.ds(t * P, P)
                    dve.scalar_tensor_tensor(out=xparts[:, 1, :, at], in0=ps[:, b, :].rearrange("p (k n) -> p k n", k=K),
                                             scalar=XSCALE, in1=xparts[:, 0, :, at], op0=ALU.mult, op1=ALU.subtract
                                             ).then_inc(norm_xl, 1)

                norm(0, 0, 0)
                normalise(0, 0)
                norm(1, 1, 0)
                normalise(1, 1)
                low_parts(0, 0)
                with dve.Fori(0, LOOPS) as i:
                    for b in range(2):
                        norm(i * 2 + (b + 2), b, i + 1)
                        low_parts(i * 2 + (b + 1), 1 - b)
                        normalise(i * 2 + (b + 2), b)
                low_parts(T - 1, 1)
                low_part(dve, mparts, mraw, c(S_M))
                dve.wait_ge(norm_kept, T)
                dve.tensor_scalar(rowbias[:], rowbias[:], c(BQBK), None, ALU.add)

            @block.scalar
            def _(act):
                def load(t, b):
                    act.dma_start(xin[:, b], x_t[bass.ds(t, 1)].rearrange("t p n -> (t p) n")).then_inc(norm_x[b], 16)

                def high_parts(t, b):
                    act.wait_ge(norm_turned, t + 3)
                    act.activation(xparts[:, 0, :, bass.ds(t * P, P)], ps[:, b, :].rearrange("p (k n) -> p k n", k=K),
                                   ACT.Copy, scale=XSCALE).then_inc(norm_xh, 1)

                def product(t, b):
                    act.wait_ge(norm_wvo, t + 1)
                    act.wait_ge(norm_ufree, t + 1)
                    act.activation(ubuf[:, b], ps[:, 4 + b, :], ACT.Copy, scale=c(F_U)).then_inc(norm_ubuf, 1)

                act.sem_inc(norm_ufree, 2)
                def slot(t, b):
                    act.wait_ge(norm_xn, t + 1)
                    load(t + 2, b)
                    high_parts(t + 1, 1 - b)

                high_parts(0, 0)
                slot(0, 0)
                with act.Fori(0, LOOPS - 1) as i:
                    for b in (1, 0):
                        slot(i * 2 + (2 - b), b)
                        product(i * 2 + (1 - b), 1 - b)
                slot(T - 3, 1)
                product(T - 4, 0)
                product(T - 3, 1)
                high_parts(T - 1, 1)
                product(T - 2, 0)
                product(T - 1, 1)

            @block.tensor
            def _(pe):
                def turn(t, b):
                    pe.wait_ge(norm_xn, t + 1)
                    pe.wait_ge(norm_xl, t + 1)
                    for k in range(K):
                        ins = pe.transpose(ps[:, b, k * P:(k + 1) * P], xn[:, b, k * P:(k + 1) * P], ident[:])
                    ins.then_inc(norm_turned, 1)

                def multiply(t, b):
                    pe.wait_ge(norm_xl, t + 3)
                    pe.wait_ge(norm_ubuf, t + 1)
                    split_product(pe, ps[:, 4 + b, :], xparts, bass.ds(t * P, P), wvoparts).then_inc(norm_wvo, 1)

                pe.sem_inc(norm_turned, 2)
                pe.sem_inc(norm_xl, 2)
                pe.sem_inc(norm_ubuf, 2)
                turn(0, 0)
                with pe.Fori(0, LOOPS) as i:
                    for b in range(2):
                        turn(i * 2 + (b + 1), 1 - b)
                        multiply(i * 2 + b, b)
                turn(T - 1, 1)
                multiply(T - 2, 0)
                multiply(T - 1, 1)

        score = z32(0, 2 * N).rearrange("p (b n) -> p b n", b=2)
        acc = z32(2 * N, N)
        gparts = z32(3 * N, 1024).bitcast(F16).rearrange("p (b h k n) -> p b h k n", b=2, h=2, k=K)
        NG = len(GROUPS)
        PARTS = [(a, min(1024, N - a)) for a in range(0, N, 1024)]
        NQ = len(PARTS)
        rowsums = wide[:, :].rearrange("p (b q) -> p b q", b=2)
        assert NQ == 4
        SB = 2
        WB = 4
        WPG = WPT // NG
        assert WPT == NG * WPG and WPG == 2
        RING = 8
        at = 0
        lowhot = regionB[:, at:at + RING * SPAN * P // 2].bitcast(F16).rearrange("p (r s n) -> p r s n", r=RING, s=SPAN)
        at += RING * SPAN * P // 2
        codehot = regionB[:, at:at + RING * SPAN * CODES // 2].bitcast(F16).rearrange(
            "p (r s n) -> p r s n", r=RING, s=SPAN)
        at += RING * SPAN * CODES // 2
        ctile = regionB[:, at:at + NP].bitcast(F16).rearrange("p (b t n) -> p b t n", b=2, t=T)
        at += NP
        squares = regionB[:, at:at + ACT_SPAN * P].bitcast(F16).rearrange("p (b s n) -> p b s n", b=2, s=ACT_SPAN)
        dinv_ready = sem("dinv_ready")
        recount_again = sem("recount_dinv_ready")
        recount_sum = sem("sum_of_degrees_ready")
        recount_all = sem("sum_of_degrees_over_partitions")
        recount_flag = sem("recount_flag_ready")
        att_g = sem("att_g_product")
        att_gb = sem("att_g_scaled")
        att_gh = sem("att_g_high")
        att_gl = sem("att_g_low")
        att_s = sem("att_scores")
        att_sc = sem("att_scores_copied")
        att_m = sem("att_softmax_steps")
        att_nb = sem("att_bias_ready")
        att_e = sem("att_exponentials")
        att_rz = sem("att_reciprocal_steps")
        att_acc = sem("att_columns_added")
        att_zero = sem("att_zeroed")
        att_col = sem("att_column_sums")
        att_square = sem("att_squares")
        att_col_kept = sem("att_source_column_kept")
        att_pool = sem("att_source_onehots_of_gpsimd")
        att_low = sem("att_source_onehots")
        att_code = sem("att_code_onehots")
        att_count = sem("att_windows_counted")
        att_wout = sem("att_windows_copied")
        att_loops = sem("att_self_loops_added")
        att_stored = [sem(f"att_counts_stored{b}") for b in range(2)]
        att_cfree = sem("att_count_buffers_free")
        att_deg = sem("att_degrees_ready")
        att_degout = sem("att_degrees_copied")

        def row_factors(link):
            for f, a in ((f_y1, F_Y1), (f_z1, R_Y1), (f_y2, F_Y2), (f_z2, R_Y2)):
                link(nc.vector.tensor_scalar(f[:], dinv[:], c(a), None, ALU.mult))

        with nc.Block() as block:
            @block.tensor
            def _(pe):
                def g_product(t, b):
                    pe.wait_ge(att_gl, t + 1)
                    if not isinstance(t, int):
                        pe.wait_ge(att_degout, t - 1)
                    at = bass.ds(t * P, P)
                    for j in range(K):
                        for k in range(K):
                            for l, r in ((0, 0), (0, 1), (1, 0)):
                                ins = pe.matmul(ps[:, b, j * P:(j + 1) * P], mparts[:, l, k, j * P:(j + 1) * P],
                                                xparts[:, r, k, at], start=(k == 0 and l == 0 and r == 0),
                                                stop=(k == K - 1 and l == 1))
                    ins.then_inc(att_g, 1)

                def degrees(t, b):
                    pe.wait_ge(att_loops, t + 1)
                    for i in range(T):
                        ins = pe.matmul(ps[:, 1 - b, 0:1], ctile[:, b, i, :], ones16[:], start=(i == 0), stop=(i == T - 1))
                    ins.then_inc(att_deg, 1)

                def scores_and_counts(t, b, degrees_of=None):
                    pe.wait_ge(att_gl, t + 3)
                    for g, (a, n) in enumerate(GROUPS):
                        pe.wait_ge(att_sc, t * NG + (g + 1))
                        for k in range(K):
                            for l, r in ((0, 0), (0, 1), (1, 0)):
                                ins = pe.matmul(ps[:, 2 + g % SB, 0:n], gparts[:, b, l, k, :], xparts[:, r, k, a:a + n],
                                                start=(k == 0 and l == 0 and r == 0), stop=(k == K - 1 and l == 1))
                        ins.then_inc(att_s, 1)
                        for v in range(WPG):
                            u = g * WPG + v
                            pe.wait_ge(att_low, t * WPT + (u + 3))
                            pe.wait_ge(att_pool, t * WPT + (u + 1))
                            pe.wait_ge(att_code, t * WPT + (u + 1))
                            pe.wait_ge(att_wout, t * WPT + (u + 1))
                            for s in range(SPAN):
                                ins = pe.matmul(ps[:, 4 + u % WB, 0:CODES], lowhot[:, u % RING, s], codehot[:, u % RING, s],
                                                start=(s == 0), stop=(s == SPAN - 1))
                            ins.then_inc(att_count, 1)
                        if g == NG // 2 and degrees_of is not None:
                            degrees(degrees_of, 1 - b)

                pe.sem_inc(att_gl, 2)
                pe.sem_inc(att_sc, SB)
                pe.sem_inc(att_count, RING)
                g_product(0, 0)
                g_product(1, 1)
                scores_and_counts(0, 0)
                with pe.Fori(0, LOOPS) as i:
                    for b in (1, 0):
                        t = i * 2 + (2 - b)
                        g_product(t + 1, 1 - b)
                        scores_and_counts(t, b, t - 1)
                scores_and_counts(T - 1, 1, T - 2)
                degrees(T - 1, 1)
                pe.wait_ge(att_acc, T + 2)
                pe.wait_ge(att_degout, T + 1)
                for t in range(T):
                    n = min(P, N - t * P)
                    bank, at = divmod(t, K)
                    ins = pe.transpose(ps[0:n, bank, at * P:(at + 1) * P], acc[:, t * P:t * P + n], ident[:])
                    if at == K - 1 or t == T - 1:
                        ins.then_inc(att_col, 1)

            @block.scalar
            def _(act):
                def g_scale(t, b):
                    act.wait_ge(att_g, t + 1)
                    for j in range(K):
                        bank = ps[:, b, j * P:(j + 1) * P]
                        ins = act.activation(bank, bank, ACT.Identity, bias=cg[:, 1, j:j + 1], scale=c(F_G))
                    ins.then_inc(att_gb, 1)
                    act.wait_ge(att_gb, t + 1)
                    if not isinstance(t, int):
                        act.wait_ge(att_s, (t - 1) * NG)
                    act.copy(gparts[:, b, 0], ps[:, b, :].rearrange("p (k n) -> p k n", k=K)).then_inc(att_gh, 1)

                def exponentials(t, b, part):
                    act.wait_ge(att_nb, t + 1)
                    a, n = PARTS[part]
                    act.activation(score[:, b, a:a + n], score[:, b, a:a + n], ACT.Exp, bias=soft[:, b, 2:3],
                                   scale=c(F_S), accum_out=rowsums[:, b, part:part + 1]).then_inc(att_e, 1)

                def source_squares(t, u):
                    n = t * WPT + (u + 1)
                    act.wait_ge(att_low, n)
                    for s in range(ACT_SPAN):
                        ins = act.activation(squares[:, u % 2, s], col16[:, 0:P], ACT.Square,
                                             bias=low[:, s, bass.ds(t * WPT + u, 1)])
                    ins.then_inc(att_square, 1)

                def source_onehots(t, u):
                    n = t * WPT + (u + 1)
                    act.wait_ge(att_square, n)
                    act.wait_ge(att_count, n)
                    act.activation(lowhot[:, u % RING, 0:ACT_SPAN], squares[:, u % 2], ACT.Relu, bias=ones[:],
                                   scale=-1.0).then_inc(att_low, 1)

                def windows(t, b, between):
                    act.wait_ge(att_cfree, t + 1)
                    for u in range(WPT):
                        ahead = u + AHEAD < WPT or not isinstance(t, int) or t < T - 1
                        if ahead:
                            source_squares(t, u + AHEAD)
                        between(u)
                        act.wait_ge(att_count, t * WPT + (u + 1 + RING))
                        act.copy(ctile[:, b, :, u * WIN:(u + 1) * WIN],
                                 ps[:, 4 + u % WB, 0:CODES].rearrange("p (t n) -> p t n", t=T)).then_inc(att_wout, 1)
                        if ahead:
                            source_onehots(t, u + AHEAD)

                def degree(t, b):
                    act.wait_ge(att_deg, t + 1)
                    act.copy(deg[:, bass.ds(t, 1)], ps[:, 1 - b, 0:1]).then_inc(att_degout, 1)

                act.sem_inc(att_wout, WB)
                act.sem_inc(att_low, 2)
                for u in range(AHEAD):
                    source_squares(0, u)
                    source_onehots(0, u)
                act.sem_inc(att_degout, 1)
                g_scale(0, 0)
                g_scale(1, 1)
                windows(0, 0, lambda u: None)
                with act.Fori(0, LOOPS) as i:
                    for b in (1, 0):
                        t = i * 2 + (2 - b)

                        def between(u):
                            if u == 1:
                                g_scale(t + 1, 1 - b)
                            if u in (2, 3, 5, 7):
                                exponentials(t - 1, 1 - b, (2, 3, 5, 7).index(u))
                            if u == WPT - 4:
                                degree(t - 1, 1 - b)
                        windows(t, b, between)

                def between(u):
                    if u < NQ:
                        exponentials(T - 2, 0, u)
                    if u == WPT - 4:
                        degree(T - 2, 0)
                windows(T - 1, 1, between)
                for part in range(NQ):
                    exponentials(T - 1, 1, part)
                degree(T - 1, 1)

            @block.gpsimd
            def _(pool):
                def self_loops(t, b):
                    pool.wait_ge(att_wout, t * WPT + (WPT + WB))
                    blk = ctile[:, b, bass.ds(t, 1), :].rearrange("p t n -> p (t n)")
                    pool.tensor_tensor(blk, blk, ident16[:], ALU.add).then_inc(att_loops, 1)

                def source_onehots(t, u):
                    n = t * WPT + (u + 1)
                    pool.tensor_copy(lowcols[:, u % 2:u % 2 + 1], low[:, POOL_CHUNK, bass.ds(t * WPT + u, 1)]
                                     ).then_inc(att_col_kept, 1)
                    pool.wait_ge(att_col_kept, n)
                    wait_apart(pool, att_count, n, passed)
                    pool.tensor_scalar(lowhot[:, u % RING, POOL_CHUNK], col16[:, 0:P], lowcols[:, u % 2:u % 2 + 1],
                                       None, ALU.is_equal).then_inc(att_pool, 1)

                def root(t):
                    one = bass.ds(t, 1)
                    pool.wait_ge(att_degout, t + 2)
                    pool.tensor_tensor(dinv[:, one], deg[:, one], half[:, 0:1], ALU.pow).then_inc(dinv_ready, 1)

                for u in range(WPT):
                    source_onehots(0, u)
                with pool.Fori(0, LOOPS) as i:
                    for b in (1, 0):
                        t = i * 2 + (2 - b)
                        for u in range(WPT):
                            source_onehots(t, u)
                            if u == RING // 2:
                                self_loops(t - 1, 1 - b)
                        root(t - 1)
                for u in range(WPT):
                    source_onehots(T - 1, u)
                    if u == RING // 2:
                        self_loops(T - 2, 0)
                root(T - 2)
                self_loops(T - 1, 1)
                root(T - 1)
                pool.wait_ge(recount_sum, 1)
                pool.partition_all_reduce(missed[:, 1:2], missed[:, 0:1], P, RADD).then_inc(recount_all, 1)

            @block.sync
            def _(sp):
                sp.sem_inc(att_cfree, 2)
                with sp.Fori(0, T // 2) as i:
                    for b in range(2):
                        t = i * 2 + b
                        sp.wait_ge(att_loops, t + 1)
                        sp.dma_start(counts_dram[bass.ds(t, 1)].rearrange("t p n -> (t p) n"),
                                     ctile[:, b].rearrange("p t n -> p (t n)")).then_inc(att_stored[b], 16)
                        sp.wait_ge(att_deg, t + 1)
                        sp.wait_ge(att_stored[b], i * 16 + 16)
                        sp.sem_inc(att_cfree, 1)

            @block.vector
            def _(dve):
                def g_split(t, b):
                    dve.wait_ge(att_gh, t + 1)
                    bank = ps[:, b, :].rearrange("p (k n) -> p k n", k=K)
                    dve.tensor_tensor(gparts[:, b, 1], bank, gparts[:, b, 0], ALU.subtract).then_inc(att_gl, 1)

                def code_onehots(t, u):
                    dve.wait_ge(att_count, t * WPT + (u + 1))
                    for s in range(SPAN):
                        ins = dve.tensor_scalar(codehot[:, u % RING, s], col16[:, 0:CODES],
                                                code[:, s, bass.ds(t * WPT + u, 1)], None, ALU.is_equal)
                    for s in range(POOL_CHUNK + 1, SPAN):
                        ins = dve.tensor_scalar(lowhot[:, u % RING, s], col16[:, 0:P],
                                                low[:, s, bass.ds(t * WPT + u, 1)], None, ALU.is_equal)
                    ins.then_inc(att_code, 1)

                def row_maximum(t, b, midway):
                    dve.wait_ge(att_acc, t + 1)
                    for g, (a, n) in enumerate(GROUPS):
                        if g < NG - 1 or not isinstance(t, int) or t < T - 1:
                            for v in range(WPG):
                                code_onehots(t, (g + 1) * WPG + v)
                        dve.wait_ge(att_s, t * NG + (g + 1))
                        dve.tensor_scalar(score[:, b, a:a + n], ps[:, 2 + g % SB, 0:n], 1.0, None, ALU.mult, ALU.max,
                                          accum_out=mx[:, b, g:g + 1]).then_inc(att_sc, 1)
                        midway(g)
                    dve.wait_ge(att_sc, t * NG + (NG + SB))
                    dve.tensor_reduce(soft[:, b, 0:1], mx[:, b, 0:NG], AX.X, ALU.max).then_inc(att_m, 1)
                    dve.wait_ge(att_m, t * 2 + 1)
                    one = bass.ds(t, 1)
                    dve.tensor_scalar(soft[:, b, 1:2], soft[:, b, 0:1], c(F_S), rowbias[:, one], ALU.mult, ALU.add
                                      ).then_inc(att_m, 1)
                    dve.wait_ge(att_m, t * 2 + 2)
                    dve.tensor_tensor(soft[:, b, 2:3], rowbias[:, one], soft[:, b, 1:2], ALU.subtract
                                      ).then_inc(att_nb, 1)

                def add_columns(t, b):
                    dve.wait_ge(att_e, t * NQ + NQ)
                    dve.tensor_reduce(soft[:, b, 3:4], rowsums[:, b], AX.X, ALU.add).then_inc(att_rz, 1)
                    dve.wait_ge(att_rz, t * 3 + 1)
                    dve.reciprocal(soft[:, b, 4:5], soft[:, b, 3:4]).then_inc(att_rz, 1)
                    dve.wait_ge(att_rz, t * 3 + 2)
                    dve.tensor_tensor(soft[:, b, 4:5], soft[:, b, 4:5], rowmask[:, bass.ds(t, 1)], ALU.mult
                                      ).then_inc(att_rz, 1)
                    dve.wait_ge(att_rz, t * 3 + 3)
                    dve.wait_ge(att_acc, t + 2)
                    dve.scalar_tensor_tensor(out=acc, in0=score[:, b], scalar=soft[:, b, 4:5], in1=acc,
                                             op0=ALU.mult, op1=ALU.add).then_inc(att_acc, 1)

                dve.memset(acc, 0.0).then_inc(att_zero, 1)
                dve.wait_ge(att_zero, 1)
                dve.sem_inc(att_acc, 2)
                g_split(0, 0)
                g_split(1, 1)
                for u in range(WPG):
                    code_onehots(0, u)
                row_maximum(0, 0, lambda g: None)
                with dve.Fori(0, LOOPS) as i:
                    for b in (1, 0):
                        t = i * 2 + (2 - b)

                        def midway(g):
                            if g == 1:
                                g_split(t + 1, 1 - b)
                            if g == NG // 2:
                                add_columns(t - 1, 1 - b)
                        row_maximum(t, b, midway)
                row_maximum(T - 1, 1, lambda g: add_columns(T - 2, 0) if g == NG // 2 else None)
                add_columns(T - 1, 1)
                link = chain(dve, dve_steps)
                link(dve.memset(cs[:], 0.0))
                dve.wait_ge(dinv_ready, T)
                row_factors(link)
                dve.tensor_reduce(missed[:, 0:1], deg[:], AX.X, ALU.add).then_inc(recount_sum, 1)
                last = N - (T - 1) * P
                for bank in range(-(-T // K)):
                    dve.wait_ge(att_col, bank + 1)
                    n = min(K, T - 1 - bank * K)
                    ins = dve.tensor_reduce(cs[:, bank * K:bank * K + n],
                                            ps[:, bank, 0:n * P].rearrange("p (t n) -> p t n", t=n), AX.X, ALU.add)
                bank, at = divmod(T - 1, K)
                link(dve.tensor_reduce(cs[0:last, T - 1:T], ps[0:last, bank, at * P:(at + 1) * P], AX.X, ALU.add))
                link(dve.tensor_scalar(mixs[:], cs[:], 1e-9, None, ALU.add))
                link(dve.reciprocal(mixs[:], mixs[:]))
                link(dve.tensor_tensor(mixs[:], mixs[:], cs[:], ALU.mult))
                dve.wait_ge(recount_all, 1)
                link(dve.tensor_scalar(missed[:, 0:1], missed[:, 1:2], float(E + NP), None, ALU.not_equal))
                dve.tensor_copy(recount[:], missed[:, 0:1]).then_inc(recount_flag, 1)

        CHP = CH + 1
        CB = NP // 8
        assert CHP % 2 == 0
        etables = regionB[:, 0:5 * CHP].rearrange("p (v c) -> p v c", v=5)
        SRC_TILE, SRC_LOW, DST, ECODE, EFAR = range(5)
        at = 5 * CHP
        colwide = regionB[:, at:at + NP]
        at += NP
        countf = regionB[:, at:at + NP]
        at += NP
        eraw = regionB[:, at:at + 2 * P].bitcast(I32).rearrange("p (v e) -> p v e", v=2)
        at += 2 * P
        eint = regionB[:, at:at + 2 * P].bitcast(I32).rearrange("p (v e) -> p v e", v=2)
        at += 2 * P
        eflt = regionB[:, at:at + 3 * P].rearrange("p (v e) -> p v e", v=3)
        widehot = z32(0, NP).bitcast(F16).rearrange("p (b n) -> p b n", b=2)
        narrowhot = z32(NP, P).bitcast(F16).rearrange("p (b n) -> p b n", b=2)
        countparts = z32(NP + P, NP).bitcast(F16).rearrange("p (h t n) -> p h t n", h=2, t=T)
        zero16 = z32(2 * NP + P, 256).bitcast(F16)
        recount_const = sem("recount_constants_ready")
        recount_loaded = sem("recount_chunks_loaded")
        recount_steps = sem("recount_load_steps")
        recount_turned = sem("recount_chunks_transposed")
        recount_kept = sem("recount_chunks_kept")
        recount_tile = sem("recount_tile_steps")
        recount_hot = sem("recount_onehots")
        recount_used = sem("recount_chunks_used")
        recount_counted = sem("recount_tiles_counted")
        recount_copied = sem("recount_tiles_copied")
        recount_split = sem("recount_tiles_split")
        recount_stored = sem("recount_tiles_stored")
        recount_free = sem("recount_parts_free")
        recount_deg = sem("recount_degrees")
        recount_degout = sem("recount_degrees_copied")
        FT = 7

        def must_recount(eng):
            eng.wait_ge(recount_flag, 1)
            return eng.value_load(recount[0:1, 0:1], min_val=0, max_val=1)

        with nc.Block() as block:
            @block.vector
            def _(dve):
                flag = must_recount(dve)
                with dve.If(flag > 0):
                    link = chain(dve, recount_steps)
                    dve.memset(zero16, 0.0).then_inc(recount_const, 1)
                    for r in range(-(-CHP // P)):
                        n = min(P, CHP - r * P)
                        dve.wait_ge(recount_loaded, 16 * r + 16)
                        dve.tensor_scalar(eint[0:n, 0], eraw[0:n, 0], ~(P - 1), None, ALU.bitwise_and)
                        link(dve.tensor_scalar(eint[0:n, 1], eraw[0:n, 0], P - 1, None, ALU.bitwise_and))
                        dve.tensor_copy(eflt[0:n, SRC_TILE], eint[0:n, 0])
                        dve.tensor_copy(eflt[0:n, SRC_LOW], eint[0:n, 1])
                        link(dve.tensor_copy(eflt[0:n, DST], eraw[0:n, 1]))
                        dve.wait_ge(recount_turned, r + 1)
                        for v in range(3):
                            ins = dve.tensor_copy(etables[:, v, r * P:r * P + n], ps[:, r % 8, v * P:v * P + n])
                        ins.then_inc(recount_kept, 1)
                    dve.wait_ge(recount_kept, -(-CHP // P))
                    dve.wait_ge(recount_const, 2)
                    code_of, far_of = etables[:, ECODE], etables[:, EFAR]
                    with dve.Fori(0, T) as t:
                        steps = [0]

                        def step(ins):
                            steps[0] += 1
                            ins.then_inc(recount_tile, 1)
                            dve.wait_ge(recount_tile, t * FT + steps[0])
                        step(dve.tensor_scalar(far_of, etables[:, DST], 0.0, FAR, ALU.is_lt, ALU.mult))
                        step(dve.tensor_scalar(code_of, etables[:, DST], float(P), FAR, ALU.is_ge, ALU.mult))
                        step(dve.tensor_tensor(far_of, far_of, code_of, ALU.add))
                        step(dve.tensor_tensor(code_of, etables[:, SRC_TILE], etables[:, DST], ALU.add))
                        step(dve.tensor_tensor(code_of, code_of, far_of, ALU.add))
                        step(dve.tensor_scalar(far_of, etables[:, DST], float(P), None, ALU.subtract))
                        step(dve.tensor_copy(etables[:, DST], far_of))
                        dve.sem_inc(passed, 1)
                        with dve.Fori(0, CHP // 2) as j:
                            for b in range(2):
                                dve.wait_ge(recount_used, t * CHP + j * 2 + (b + 1))
                                at = bass.ds(j * 2 + b, 1)
                                dve.tensor_scalar(narrowhot[:, b], col16[:, 0:P], etables[:, SRC_LOW, at], None,
                                                  ALU.is_equal)
                                dve.tensor_scalar(widehot[:, b], colwide, etables[:, ECODE, at], None, ALU.is_equal
                                                  ).then_inc(recount_hot, 1)
                        dve.wait_ge(recount_counted, t + 1)
                        for a in range(8):
                            ins = dve.tensor_copy(countf[:, a * CB:(a + 1) * CB], ps[:, a, 0:CB])
                        ins.then_inc(recount_copied, 1)
                        dve.wait_ge(recount_copied, t * 4 + 1)
                        blk = countf[:, bass.ds(t * P, P)]
                        dve.tensor_tensor(blk, blk, ident[:], ALU.add).then_inc(recount_copied, 1)
                        dve.wait_ge(recount_copied, t * 4 + 2)
                        dve.wait_ge(recount_free, t + 1)
                        whole = countf.rearrange("p (t n) -> p t n", t=T)
                        dve.tensor_copy(countparts[:, 0], whole).then_inc(recount_copied, 1)
                        dve.wait_ge(recount_copied, t * 4 + 3)
                        dve.tensor_tensor(countparts[:, 1], whole, countparts[:, 0], ALU.subtract).then_inc(recount_split, 1)
                        dve.sem_inc(recount_copied, 1)
                    dve.wait_ge(recount_again, 1)
                    row_factors(chain(dve, recount_steps))
                dve.sem_inc(passed, 1)

            @block.gpsimd
            def _(pool):
                flag = must_recount(pool)
                with pool.If(flag > 0):
                    pool.iota(colwide, pattern=[[1, NP]], base=0, channel_multiplier=0,
                              allow_small_or_imprecise_dtypes=True).then_inc(recount_const, 1)
                    pool.wait_ge(recount_degout, T)
                    pool.tensor_tensor(dinv[:], deg[:], half[:], ALU.pow).then_inc(recount_again, 1)

            @block.tensor
            def _(pe):
                flag = must_recount(pe)
                with pe.If(flag > 0):
                    for r in range(-(-CHP // P)):
                        n = min(P, CHP - r * P)
                        pe.wait_ge(recount_steps, 2 * r + 2)
                        for v in range(3):
                            ins = pe.transpose(ps[:, r % 8, v * P:v * P + n], eflt[0:n, v], ident[0:n, 0:n])
                        ins.then_inc(recount_turned, 1)
                    pe.wait_ge(recount_kept, -(-CHP // P))
                    pe.wait_ge(recount_const, 2)
                    pe.sem_inc(recount_used, 2)
                    with pe.Fori(0, T) as t:
                        for a in range(8):
                            pe.matmul(ps[:, a, 0:CB], zero16[:, 0:P], zero16[:, 0:CB], start=True, stop=False)
                        with pe.Fori(0, CHP // 2) as j:
                            for b in range(2):
                                pe.wait_ge(recount_hot, t * CHP + j * 2 + (b + 1))
                                for a in range(8):
                                    ins = pe.matmul(ps[:, a, 0:CB], narrowhot[:, b], widehot[:, b, a * CB:(a + 1) * CB],
                                                    start=False, stop=False)
                                ins.then_inc(recount_used, 1)
                        for a in range(8):
                            ins = pe.matmul(ps[:, a, 0:CB], zero16[:, 0:P], zero16[:, 0:CB], start=False, stop=True)
                        ins.then_inc(recount_counted, 1)
                        pe.wait_ge(recount_split, t + 1)
                        for i in range(T):
                            for h in range(2):
                                ins = pe.matmul(ps[:, 0, 0:1], countparts[:, h, i, :], ones16[:],
                                                start=(i == 0 and h == 0), stop=(i == T - 1 and h == 1))
                        ins.then_inc(recount_deg, 1)
                        pe.wait_ge(recount_degout, t + 1)

            @block.scalar
            def _(act):
                flag = must_recount(act)
                with act.If(flag > 0):
                    with act.Fori(0, T) as t:
                        act.wait_ge(recount_deg, t + 1)
                        act.copy(deg[:, bass.ds(t, 1)], ps[:, 0, 0:1]).then_inc(recount_degout, 1)

            @block.sync
            def _(sp):
                flag = must_recount(sp)
                with sp.If(flag > 0):
                    for r in range(-(-CHP // P)):
                        n = min(P, CHP - r * P)
                        if r > 0:
                            sp.wait_ge(recount_steps, 2 * r)
                        sp.dma_start(eraw[0:n].rearrange("p v e -> p (v e)"),
                                     edges[r * P:r * P + n].rearrange("c v e -> c (v e)")).then_inc(recount_loaded, 16)
                    sp.sem_inc(recount_free, 1)
                    with sp.Fori(0, T) as t:
                        sp.wait_ge(recount_split, t + 1)
                        one = bass.ds(t, 1)
                        for dram, h in ((counts_dram, 0), (low_counts_dram, 1)):
                            sp.dma_start(dram[one].rearrange("t p n -> (t p) n"),
                                         countparts[:, h].rearrange("p t n -> p (t n)")).then_inc(recount_stored, 16)
                        sp.wait_ge(recount_stored, t * 32 + 32)
                        sp.wait_ge(recount_deg, t + 1)
                        sp.sem_inc(recount_free, 1)

        y1_product = sem("y1_product")
        y1_high = sem("y1_high_part")
        y1_low = sem("y1_low_part")
        conv1_c = [sem(f"conv1_counts_loaded{b}") for b in range(2)]
        conv2_c = [sem(f"conv2_counts_loaded{b}") for b in range(2)]
        cbuf = z32(0, NP).bitcast(F16).rearrange("p (b t n) -> p b t n", b=2, t=T)

        def first_counts(sp, loaded, b):
            sp.dma_start(cbuf[:, b].rearrange("p t n -> p (t n)"), counts_dram[b]).then_inc(loaded[b], 16)


        with nc.Block() as block:
            @block.sync
            def _(sp):
                for b in range(2):
                    first_counts(sp, conv1_c, b)

            @block.tensor
            def _(pe):
                pe.sem_inc(y1_low, 2)
                with pe.Fori(0, T // 2) as i:
                    for b in range(2):
                        t = i * 2 + b
                        pe.wait_ge(y1_low, t + 1)
                        split_product(pe, ps[:, b, :], xparts, bass.ds(t * P, P), w12parts).then_inc(y1_product, 1)

            @block.scalar
            def _(act):
                with act.Fori(0, T // 2) as i:
                    for b in range(2):
                        t = i * 2 + b
                        one = bass.ds(t, 1)
                        act.wait_ge(y1_product, t + 1)
                        act.activation(y1[:, one, 0, :].rearrange("p t n -> p (t n)"), ps[:, b, :], ACT.Copy,
                                       scale=f_y1[:, one]).then_inc(y1_high, 1)

            @block.vector
            def _(dve):
                with dve.Fori(0, T // 2) as i:
                    for b in range(2):
                        t = i * 2 + b
                        one = bass.ds(t, 1)
                        dve.wait_ge(y1_high, t + 1)
                        dve.scalar_tensor_tensor(out=y1[:, one, 1, :].rearrange("p t n -> p (t n)"), in0=ps[:, b, :],
                                                 scalar=f_y1[:, one], in1=y1[:, one, 0, :].rearrange("p t n -> p (t n)"),
                                                 op0=ALU.mult, op1=ALU.subtract).then_inc(y1_low, 1)

        def pair_of(at):
            return z32(at, 2 * D).rearrange("p (b n) -> p b n", b=2)

        zbuf = pair_of(3840)

        clow = z32(8960, NP // 2).bitcast(F16).rearrange("p (t n) -> p t n", t=T)

        def load_counts(sp, loaded, low_loaded, used):
            flag = must_recount(sp)

            def low_counts(t):
                with sp.If(flag > 0):
                    sp.dma_start(clow.rearrange("p t n -> p (t n)"),
                                 low_counts_dram[bass.ds(t, 1)].rearrange("t p n -> (t p) n")).then_inc(low_loaded, 16)

            low_counts(0)
            with sp.Fori(0, LOOPS) as i:
                for b in range(2):
                    sp.wait_ge(used, i * 2 + (b + 1))
                    sp.dma_start(cbuf[:, b].rearrange("p t n -> p (t n)"),
                                 counts_dram[bass.ds(i * 2 + (b + 2), 1)].rearrange("t p n -> (t p) n")
                                 ).then_inc(loaded[b], 16)
                    low_counts(i * 2 + (b + 1))
            sp.wait_ge(used, T - 1)
            low_counts(T - 1)

        def aggregate(pe, y, t, b, flag, low_loaded):
            pe.matmul(ps[:, b, :], cbuf[:, b, 0, :], y[:, 0, 0, :], start=True, stop=False)
            with pe.If(flag > 0):
                pe.wait_ge(low_loaded, t * 16 + 16)
                for i in range(T):
                    for h in range(2):
                        pe.matmul(ps[:, b, :], clow[:, i, :], y[:, i, h, :], start=False, stop=False)
            for i in range(T):
                for h in range(2):
                    if i + h > 0:
                        ins = pe.matmul(ps[:, b, :], cbuf[:, b, i, :], y[:, i, h, :], start=False,
                                        stop=(i == T - 1 and h == 1))
            return ins

        def late_weight(i):
            at = T * D - (i + 1) * K * D
            return regionA[:, at:at + K * D].rearrange("p (k n) -> p k n", k=K)

        w2raw, wfraw, wtmp, wpow = (late_weight(i) for i in range(4))
        w2_loaded = sem("w2_loaded")
        wf_loaded = sem("last_weight_loaded")
        hbuf = pair_of(4864)
        hparts = z32(5888, 1024).bitcast(F16).rearrange("p (b h k n) -> p b h k n", b=2, h=2, k=K)
        conv1_low = sem("conv1_low_counts_loaded")
        conv1_agg = sem("conv1_aggregated")
        conv1_split = sem("conv1_w2_split")
        conv1_z = sem("conv1_z_ready")
        conv1_moments = sem("conv1_moments")
        conv1_var = sem("conv1_variance_plus_eps")
        conv1_rstd = sem("conv1_rstd_ready")
        conv1_norm = sem("conv1_normalised")
        conv1_beta = sem("conv1_beta_applied")
        conv1_h = sem("conv1_h_ready")
        conv1_turned = sem("conv1_h_transposed")
        conv1_hh = sem("conv1_h_high")
        conv1_hl = sem("conv1_h_low")
        conv1_w2 = sem("conv1_w2_product")
        conv1_y2h = sem("conv1_y2_high")
        conv1_y2l = sem("conv1_y2_low")
        rstd_pair = wide

        with nc.Block() as block:
            @block.sync
            def _(sp):
                sp.dma_start(w2raw, w["W2"].rearrange("(k p) n -> p k n", p=P)).then_inc(w2_loaded, 16)
                sp.dma_start(wfraw, w["Wf"].rearrange("(k p) n -> p k n", p=P)).then_inc(wf_loaded, 16)
                load_counts(sp, conv1_c, conv1_low, conv1_agg)
                for b in range(2):
                    sp.wait_ge(conv1_agg, T - 1 + b)
                    first_counts(sp, conv2_c, b)

            @block.tensor
            def _(pe):
                def agg(t, b, i):
                    pe.wait_ge(conv1_c[b], i * 16 + 16)
                    pe.wait_ge(conv1_z, t + 1)
                    aggregate(pe, y1, t, b, flag, conv1_low).then_inc(conv1_agg, 1)

                def turn(t, b):
                    pe.wait_ge(conv1_h, t + 1)
                    pe.wait_ge(conv1_hl, t + 1)
                    for k in range(K):
                        ins = pe.transpose(ps[:, 2 + b, k * P:(k + 1) * P], hbuf[:, b, k * P:(k + 1) * P], ident[:])
                    ins.then_inc(conv1_turned, 1)

                def multiply(t, b):
                    pe.wait_ge(conv1_split, 2)
                    pe.wait_ge(conv1_hl, t + 3)
                    pe.wait_ge(conv1_y2l, t + 1)
                    split_product(pe, ps[:, 4 + b, :], hparts[:, b], slice(0, P), w12parts).then_inc(conv1_w2, 1)

                flag = must_recount(pe)
                pe.sem_inc(conv1_z, 2)
                pe.sem_inc(conv1_hl, 2)
                pe.sem_inc(conv1_w2, 2)
                pe.sem_inc(conv1_y2l, 2)
                agg(0, 0, 0)
                agg(1, 1, 0)
                with pe.Fori(0, LOOPS) as i:
                    for b in range(2):
                        turn(i * 2 + b, b)
                        agg(i * 2 + (b + 2), b, i + 1)
                        multiply(i * 2 + b, b)
                for b in range(2):
                    turn(T - 2 + b, b)
                    multiply(T - 2 + b, b)

            @block.vector
            def _(dve):
                def norm(t, b):
                    one = bass.ds(t, 1)
                    dve.wait_ge(conv1_agg, t + 1)
                    if not isinstance(t, int):
                        dve.wait_ge(conv1_h, t - 1)
                    dve.scalar_tensor_tensor(out=zbuf[:, b], in0=ps[:, b, :], scalar=f_z1[:, one], in1=rows[:, B1],
                                             op0=ALU.mult, op1=ALU.add).then_inc(conv1_z, 1)
                    dve.wait_ge(conv1_z, t + 3)
                    dve.bn_stats(stats[:, b], zbuf[:, b]).then_inc(conv1_moments, 1)
                    wait_apart(dve, conv1_moments, t * 2 + 1, passed)
                    dve.bn_aggr(aggr[:, b], stats[:, b]).then_inc(conv1_moments, 1)
                    dve.wait_ge(conv1_moments, t * 2 + 2)
                    dve.tensor_scalar(veps[:, b:b + 1], aggr[:, b, 1:2], EPS, None, ALU.add).then_inc(conv1_var, 1)
                    dve.wait_ge(conv1_rstd, t + 1)
                    dve.tensor_scalar(zbuf[:, b], zbuf[:, b], aggr[:, b, 0:1], rstd_pair[:, b:b + 1],
                                      ALU.subtract, ALU.mult).then_inc(conv1_norm, 1)
                    dve.wait_ge(conv1_norm, t * 2 + 1)
                    dve.tensor_tensor(zbuf[:, b], zbuf[:, b], rows[:, G1], ALU.mult).then_inc(conv1_norm, 1)
                    dve.wait_ge(conv1_norm, t * 2 + 2)
                    dve.tensor_tensor(zbuf[:, b], zbuf[:, b], rows[:, BE1], ALU.add).then_inc(conv1_beta, 1)

                def h_low(t, b):
                    dve.wait_ge(conv1_hh, t + 1)
                    dve.scalar_tensor_tensor(out=hparts[:, b, 1], in0=ps[:, 2 + b, :].rearrange("p (k n) -> p k n", k=K),
                                             scalar=c(S_H), in1=hparts[:, b, 0], op0=ALU.mult, op1=ALU.subtract
                                             ).then_inc(conv1_hl, 1)

                def y2_low(t, b):
                    one = bass.ds(t, 1)
                    dve.wait_ge(conv1_y2h, t + 1)
                    dve.scalar_tensor_tensor(out=y2[:, one, 1, :].rearrange("p t n -> p (t n)"), in0=ps[:, 4 + b, :],
                                             scalar=f_y2[:, one], in1=y2[:, one, 0, :].rearrange("p t n -> p (t n)"),
                                             op0=ALU.mult, op1=ALU.subtract).then_inc(conv1_y2l, 1)

                dve.wait_ge(w2_loaded, 16)
                split_weight(dve, w12parts, w2raw, c(S_W2), chain(dve, conv1_split))
                norm(0, 0)
                norm(1, 1)
                link = chain(dve, dve_steps)
                dve.wait_ge(wf_loaded, 16)
                link(dve.tensor_scalar(c(TMP), c(A_FFN), 1e-12, None, ALU.max))
                link(dve.reciprocal(c(TMP2), c(TMP)))
                link(dve.tensor_scalar(c(W_SC), c(TMP2), FP8_MAX, None, ALU.mult))
                link(dve.tensor_scalar(wtmp, wfraw, c(W_SC), FP8_MAX, ALU.mult, ALU.min))
                link(dve.tensor_scalar(wtmp, wtmp, -FP8_MAX, None, ALU.max))
                link(dve.tensor_scalar(wpow.bitcast(I32), wtmp.bitcast(I32), EXPONENT, None, ALU.bitwise_and))
                link(dve.tensor_scalar(wpow, wpow, 2.0 ** -6, 1.5 * 2.0 ** 20, ALU.max, ALU.mult))
                link(dve.tensor_tensor(wtmp, wtmp, wpow, ALU.add))
                link(dve.tensor_tensor(wffn[:], wtmp, wpow, ALU.subtract))
                with dve.Fori(0, LOOPS) as i:
                    for b in range(2):
                        h_low(i * 2 + b, b)
                        norm(i * 2 + (b + 2), b)
                        y2_low(i * 2 + b, b)
                for b in range(2):
                    h_low(T - 2 + b, b)
                    y2_low(T - 2 + b, b)

            @block.gpsimd
            def _(pool):
                with pool.Fori(0, T // 2) as i:
                    for b in range(2):
                        t = i * 2 + b
                        pool.wait_ge(conv1_var, t + 1)
                        pool.tensor_tensor(rstd_pair[:, b:b + 1], veps[:, b:b + 1], half[:, 0:1], ALU.pow
                                           ).then_inc(conv1_rstd, 1)

            @block.scalar
            def _(act):
                def gelu(t, b):
                    act.wait_ge(conv1_beta, t + 1)
                    act.wait_ge(conv1_turned, t + 1)
                    act.activation(hbuf[:, b], zbuf[:, b], ACT.Gelu).then_inc(conv1_h, 1)

                def h_high(t, b):
                    act.wait_ge(conv1_turned, t + 3)
                    act.wait_ge(conv1_w2, t + 1)
                    act.activation(hparts[:, b, 0], ps[:, 2 + b, :].rearrange("p (k n) -> p k n", k=K), ACT.Copy,
                                   scale=c(S_H)).then_inc(conv1_hh, 1)

                def y2_high(t, b):
                    one = bass.ds(t, 1)
                    act.wait_ge(conv1_w2, t + 3)
                    act.activation(y2[:, one, 0, :].rearrange("p t n -> p (t n)"), ps[:, 4 + b, :], ACT.Copy,
                                   scale=f_y2[:, one]).then_inc(conv1_y2h, 1)

                act.sem_inc(conv1_turned, 2)
                gelu(0, 0)
                h_high(0, 0)
                gelu(1, 1)
                y2_high(0, 0)
                with act.Fori(0, LOOPS) as i:
                    for b in (1, 0):
                        t = i * 2 + (2 - b)
                        h_high(t, b)
                        gelu(t + 1, 1 - b)
                        y2_high(t, b)
                h_high(T - 1, 1)
                y2_high(T - 1, 1)

        xbuf = pair_of(4864)
        mixbuf = pair_of(5888)
        xnbuf = pair_of(6912)
        dev = pair_of(7936)
        conv2_xu = [sem(f"conv2_x_and_mix_loaded{b}") for b in range(2)]
        conv2_low = sem("conv2_low_counts_loaded")
        conv2_agg = sem("conv2_aggregated")
        conv2_z = sem("conv2_z_ready")
        conv2_moments = sem("conv2_moments")
        conv2_var = sem("conv2_variance_plus_eps")
        conv2_rstd = sem("conv2_rstd_ready")
        conv2_norm = sem("conv2_normalised")
        conv2_xn = sem("conv2_xn_ready")
        conv2_mix = sem("conv2_mix_steps")
        conv2_pre = sem("conv2_z_with_residual")
        conv2_sum = sem("conv2_mix_with_x")
        conv2_gelu = sem("conv2_gelu_done")
        conv2_new = sem("conv2_new_x_ready")
        conv2_new_moments = sem("conv2_new_moments")
        conv2_nvar = sem("conv2_new_variance_plus_eps")
        conv2_nrstd = sem("conv2_new_rstd")
        conv2_dev = sem("conv2_deviation")
        conv2_amax = sem("conv2_row_maximum")

        with nc.Block() as block:
            @block.sync
            def _(sp):
                load_counts(sp, conv2_c, conv2_low, conv2_agg)

            @block.tensor
            def _(pe):
                flag = must_recount(pe)
                pe.sem_inc(conv2_z, 2)
                with pe.Fori(0, T // 2) as i:
                    for b in range(2):
                        pe.wait_ge(conv2_c[b], i * 16 + 16)
                        pe.wait_ge(conv2_z, i * 2 + (b + 1))
                        aggregate(pe, y2, i * 2 + b, b, flag, conv2_low).then_inc(conv2_agg, 1)

            @block.scalar
            def _(act):
                act.sem_inc(conv2_new, 2)
                with act.Fori(0, T // 2) as i:
                    for b in range(2):
                        t = i * 2 + b
                        one = bass.ds(t, 1)
                        act.wait_ge(conv2_new, t + 1)
                        act.dma_start(xbuf[:, b], x_t[one].rearrange("t p n -> (t p) n")).then_inc(conv2_xu[b], 16)
                        act.dma_start(mixbuf[:, b], mix_dram[one].rearrange("t p n -> (t p) n")).then_inc(conv2_xu[b], 16)
                        act.wait_ge(conv2_pre, t + 1)
                        act.activation(zbuf[:, b], zbuf[:, b], ACT.Gelu).then_inc(conv2_gelu, 1)

            @block.vector
            def _(dve):
                def first_half(t, b, i):
                    one = bass.ds(t, 1)
                    dve.wait_ge(conv2_xu[b], i * 32 + 32)
                    dve.tensor_scalar(xnbuf[:, b], xbuf[:, b], xmean[:, one], xrstd[:, one], ALU.subtract, ALU.mult
                                      ).then_inc(conv2_xn, 1)
                    dve.scalar_tensor_tensor(out=mixbuf[:, b], in0=mixbuf[:, b], scalar=mixs[:, one], in1=rows[:, MIXC],
                                             op0=ALU.mult, op1=ALU.add).then_inc(conv2_mix, 1)
                    dve.wait_ge(conv2_xn, t + 1)
                    dve.wait_ge(conv2_mix, t * 2 + 1)
                    dve.scalar_tensor_tensor(out=mixbuf[:, b], in0=mixbuf[:, b], scalar=0.0, in1=xnbuf[:, b],
                                             op0=ALU.max, op1=ALU.add).then_inc(conv2_mix, 1)
                    dve.wait_ge(conv2_agg, t + 1)
                    dve.scalar_tensor_tensor(out=zbuf[:, b], in0=ps[:, b, :], scalar=f_z2[:, one], in1=rows[:, B2],
                                             op0=ALU.mult, op1=ALU.add).then_inc(conv2_z, 1)
                    dve.wait_ge(conv2_z, t + 3)
                    dve.bn_stats(stats[:, b], zbuf[:, b]).then_inc(conv2_moments, 1)
                    wait_apart(dve, conv2_moments, t * 2 + 1, passed)
                    dve.bn_aggr(aggr[:, b], stats[:, b]).then_inc(conv2_moments, 1)
                    dve.wait_ge(conv2_moments, t * 2 + 2)
                    dve.tensor_scalar(veps[:, b:b + 1], aggr[:, b, 1:2], EPS, None, ALU.add).then_inc(conv2_var, 1)
                    dve.wait_ge(conv2_rstd, t + 1)
                    dve.tensor_scalar(zbuf[:, b], zbuf[:, b], aggr[:, b, 0:1], rstd_pair[:, b:b + 1],
                                      ALU.subtract, ALU.mult).then_inc(conv2_norm, 1)
                    dve.wait_ge(conv2_norm, t * 3 + 1)
                    dve.tensor_tensor(zbuf[:, b], zbuf[:, b], rows[:, G2], ALU.mult).then_inc(conv2_norm, 1)
                    dve.wait_ge(conv2_norm, t * 3 + 2)
                    dve.tensor_tensor(zbuf[:, b], zbuf[:, b], rows[:, BE2], ALU.add).then_inc(conv2_norm, 1)
                    dve.wait_ge(conv2_norm, t * 3 + 3)
                    dve.tensor_tensor(zbuf[:, b], zbuf[:, b], xnbuf[:, b], ALU.add).then_inc(conv2_pre, 1)

                def second_half(t, b):
                    one = bass.ds(t, 1)
                    new = xnew[:, one, :].rearrange("p t n -> p (t n)")
                    dve.wait_ge(conv2_gelu, t + 1)
                    dve.wait_ge(conv2_sum, t + 1)
                    dve.tensor_tensor(new, mixbuf[:, b], zbuf[:, b], ALU.add).then_inc(conv2_new, 1)
                    wait_apart(dve, conv2_new, t + 3, passed)
                    dve.bn_stats(nst[:, b], new).then_inc(conv2_new_moments, 1)
                    wait_apart(dve, conv2_new_moments, t * 2 + 1, passed)
                    dve.bn_aggr(nag[:, b], nst[:, b]).then_inc(conv2_new_moments, 1)
                    dve.wait_ge(conv2_new_moments, t * 2 + 2)
                    dve.tensor_copy(nmean[:, one], nag[:, b, 0:1])
                    dve.tensor_scalar(nveps[:, b:b + 1], nag[:, b, 1:2], EPS, None, ALU.add).then_inc(conv2_nvar, 1)
                    dve.wait_ge(conv2_nrstd, t + 1)
                    dve.tensor_scalar(dev[:, b], new, nag[:, b, 0:1], nrstd[:, one], ALU.subtract, ALU.mult
                                      ).then_inc(conv2_dev, 1)
                    dve.wait_ge(conv2_dev, t + 1)
                    dve.tensor_reduce(namax[:, one], dev[:, b], AX.X, ALU.max, apply_absolute_value=True
                                      ).then_inc(conv2_amax, 1)

                with dve.Fori(0, T // 2) as i:
                    for b in range(2):
                        first_half(i * 2 + b, b, i)
                        second_half(i * 2 + b, b)

            @block.gpsimd
            def _(pool):
                def first_half(t, b):
                    pool.wait_ge(conv2_mix, t * 2 + 2)
                    pool.tensor_tensor(mixbuf[:, b], mixbuf[:, b], xbuf[:, b], ALU.add).then_inc(conv2_sum, 1)
                    pool.wait_ge(conv2_var, t + 1)
                    pool.tensor_tensor(rstd_pair[:, b:b + 1], veps[:, b:b + 1], half[:, 0:1], ALU.pow).then_inc(conv2_rstd, 1)

                def second_half(t, b):
                    pool.wait_ge(conv2_nvar, t + 1)
                    pool.tensor_tensor(nrstd[:, bass.ds(t, 1)], nveps[:, b:b + 1], half[:, 0:1], ALU.pow
                                       ).then_inc(conv2_nrstd, 1)

                with pool.Fori(0, T // 2) as i:
                    for b in range(2):
                        first_half(i * 2 + b, b)
                        second_half(i * 2 + b, b)

        q32 = pair_of(0)
        qpow = pair_of(1024)
        qbf = z32(2048, D).bitcast(BF16).rearrange("p (b n) -> p b n", b=2)
        qT = z32(2560, D).bitcast(BF16).rearrange("p (b k n) -> p b k n", b=2, k=K)
        obuf = pair_of(3072)
        qscale = z32(4096, T)
        qshift = z32(4096 + T, T)
        ffn_setup = sem("ffn_setup_steps")
        ffn_max = sem("ffn_maximum_ready")
        ffn_all = sem("ffn_maximum_over_partitions")
        ffn_scaled = sem("ffn_scaled")
        ffn_q = sem("ffn_quantise_steps")
        ffn_big = sem("ffn_rounding_added")
        ffn_qbf = sem("ffn_rounded")
        ffn_turned = sem("ffn_transposed")
        ffn_qt = sem("ffn_transposes_copied")
        ffn_mm = sem("ffn_products")
        ffn_o = sem("ffn_outputs_ready")
        ffn_out = [sem(f"ffn_outputs_stored{b}") for b in range(2)]
        ffn_ofree = sem("ffn_output_buffers_free")
        QS = 3

        with nc.Block() as block:
            @block.gpsimd
            def _(pool):
                pool.wait_ge(ffn_max, 1)
                pool.partition_all_reduce(c(A_X), c(TMP), P, RMAX).then_inc(ffn_all, 1)
                with pool.Fori(0, T // 2) as i:
                    for b in range(2):
                        t = i * 2 + b
                        pool.wait_ge(ffn_q, t * QS + QS)
                        pool.tensor_tensor(q32[:, b], q32[:, b], qpow[:, b], ALU.add).then_inc(ffn_big, 1)

            @block.vector
            def _(dve):
                link = chain(dve, ffn_setup)
                link(dve.tensor_tensor(namax[:], namax[:], rowmask[:], ALU.mult))
                dve.tensor_reduce(c(TMP), namax[:], AX.X, ALU.max).then_inc(ffn_max, 1)
                dve.wait_ge(ffn_all, 1)
                link(dve.tensor_scalar(c(TMP), c(A_X), 1e-12, None, ALU.max))
                link(dve.reciprocal(c(TMP2), c(TMP)))
                link(dve.tensor_scalar(c(X_SC), c(TMP2), FP8_MAX, None, ALU.mult))
                link(dve.tensor_scalar(qscale, nrstd[:], c(X_SC), None, ALU.mult))
                link(dve.scalar_tensor_tensor(out=qshift, in0=nmean[:], scalar=-1.0, in1=qscale,
                                              op0=ALU.mult, op1=ALU.mult))
                link(dve.reciprocal(c(TMP), c(X_SC)))
                link(dve.reciprocal(c(TMP2), c(W_SC)))
                link(dve.tensor_tensor(c(X_F), c(TMP), c(TMP2), ALU.mult))

                def clip(t, b):
                    n = t * QS
                    dve.wait_ge(ffn_scaled, t + 1)
                    dve.tensor_scalar(q32[:, b], q32[:, b], FP8_MAX, -FP8_MAX, ALU.min, ALU.max).then_inc(ffn_q, 1)
                    dve.wait_ge(ffn_q, n + 1)
                    dve.tensor_scalar(qpow[:, b].bitcast(I32), q32[:, b].bitcast(I32), EXPONENT, None,
                                      ALU.bitwise_and).then_inc(ffn_q, 1)

                def rounding(t, b):
                    dve.wait_ge(ffn_q, t * QS + 2)
                    dve.tensor_scalar(qpow[:, b], qpow[:, b], 2.0 ** -6, 1.5 * 2.0 ** 20, ALU.max, ALU.mult
                                      ).then_inc(ffn_q, 1)

                def rounded(t, b):
                    dve.wait_ge(ffn_big, t + 1)
                    dve.wait_ge(ffn_turned, t + 1)
                    dve.tensor_tensor(qbf[:, b], q32[:, b], qpow[:, b], ALU.subtract).then_inc(ffn_qbf, 1)

                def output(t, b):
                    dve.wait_ge(ffn_mm, t + 1)
                    dve.wait_ge(ffn_ofree, t + 1)
                    dve.scalar_tensor_tensor(out=obuf[:, b], in0=ps[:, 2 + b, :], scalar=c(X_F),
                                             in1=xnew[:, bass.ds(t, 1), :].rearrange("p t n -> p (t n)"),
                                             op0=ALU.mult, op1=ALU.add).then_inc(ffn_o, 1)

                clip(0, 0)
                rounding(0, 0)
                clip(1, 1)
                rounded(0, 0)
                rounding(1, 1)

                def slot(t, b):
                    clip(t + 2, b)
                    rounded(t + 1, 1 - b)
                    rounding(t + 2, b)

                slot(0, 0)
                with dve.Fori(0, LOOPS - 1) as i:
                    for b in (1, 0):
                        slot(i * 2 + (2 - b), b)
                        output(i * 2 + (1 - b), 1 - b)
                slot(T - 3, 1)
                output(T - 4, 0)
                rounded(T - 1, 1)
                for t in range(T - 3, T):
                    output(t, t % 2)

            @block.tensor
            def _(pe):
                def turn(t, b):
                    pe.wait_ge(ffn_qbf, t + 3)
                    pe.wait_ge(ffn_qt, t + 1)
                    bank = ps[:, b, 0:D // 2].bitcast(BF16)
                    for k in range(K):
                        ins = pe.transpose(bank[:, k * P:(k + 1) * P], qbf[:, b, k * P:(k + 1) * P], identb[:])
                    ins.then_inc(ffn_turned, 1)

                def multiply(t, b):
                    pe.wait_ge(ffn_qt, t + 3)
                    pe.wait_ge(ffn_o, t + 1)
                    for k in range(K):
                        ins = pe.matmul(ps[:, 2 + b, :], qT[:, b, k, :], wffn[:, k, :], start=(k == 0), stop=(k == K - 1))
                    ins.then_inc(ffn_mm, 1)

                pe.sem_inc(ffn_qt, 2)
                pe.sem_inc(ffn_o, 2)
                pe.sem_inc(ffn_turned, 2)
                turn(0, 0)
                with pe.Fori(0, LOOPS) as i:
                    for b in range(2):
                        turn(i * 2 + (b + 1), 1 - b)
                        multiply(i * 2 + b, b)
                turn(T - 1, 1)
                multiply(T - 2, 0)
                multiply(T - 1, 1)

            @block.scalar
            def _(act):
                def scaled(t, b):
                    one = bass.ds(t, 1)
                    act.wait_ge(ffn_qbf, t + 1)
                    act.activation(q32[:, b], xnew[:, one, :].rearrange("p t n -> p (t n)"), ACT.Identity,
                                   bias=qshift[:, one], scale=qscale[:, one]).then_inc(ffn_scaled, 1)

                def turned(t, b):
                    act.wait_ge(ffn_turned, t + 3)
                    act.wait_ge(ffn_o, t + 1)
                    act.copy(qT[:, b].rearrange("p k n -> p (k n)"), ps[:, b, 0:D // 2].bitcast(BF16)
                             ).then_inc(ffn_qt, 1)

                act.sem_inc(ffn_qbf, 2)
                act.wait_ge(ffn_setup, 6)
                scaled(0, 0)
                scaled(1, 1)
                with act.Fori(0, LOOPS) as i:
                    for b in range(2):
                        scaled(i * 2 + (b + 2), b)
                        turned(i * 2 + b, b)
                turned(T - 2, 0)
                turned(T - 1, 1)

            @block.sync
            def _(sp):
                sp.sem_inc(ffn_ofree, 2)
                store_tiles(sp, ffn_o, 2, lambda t, b: sp.dma_start(
                    out_t[bass.ds(t, 1)].rearrange("t p n -> (t p) n"), obuf[:, b]), ffn_out, ffn_ofree)


_VECTORS = {"b1": "L0_gnn_b1", "g1": "L0_gnn_gamma1", "be1": "L0_gnn_beta1", "b2": "L0_gnn_b2",
            "g2": "L0_gnn_gamma2", "be2": "L0_gnn_beta2", "bq": "L0_mix_bq", "bk": "L0_mix_bk", "bv": "L0_mix_bv",
            "bo": "L0_mix_bo", "scale": "L0_mix_bn_scale", "bias": "L0_mix_bn_bias", "mean": "L0_mix_bn_mean",
            "var": "L0_mix_bn_var"}
_MATRICES = {"Wq": "L0_mix_Wq", "Wk": "L0_mix_Wk", "Wv": "L0_mix_Wv", "Wo": "L0_mix_Wo", "W1": "L0_gnn_W1",
             "W2": "L0_gnn_W2", "Wf": "L0_ffn_weight"}


def kernel(**inputs):
    import numpy as np
    import concourse.bacc as bacc
    from concourse import mybir as mb
    from concourse.bass_utils import run_bass_kernel_spmd as run

    nc = bacc.Bacc("TRN2", target_bir_lowering=False, num_devices=1)
    x = np.zeros((NP, D), np.asarray(inputs["x"]).dtype)
    x[:N] = inputs["x"]
    src, dst = np.asarray(inputs["src"]), np.asarray(inputs["dst"])
    edges = np.zeros(((CH + 1), 2, P), src.dtype)
    edges[:, 1] = 2 * NP
    for v, a in enumerate((src, dst)):
        full = E // P
        edges[:full, v] = a[:full * P].reshape(full, P)
        edges[full, v, :E - full * P] = a[full * P:]
    arrays = {"in_x": x, "in_edges": edges}
    for short, name in {**_VECTORS, **_MATRICES}.items():
        arrays["in_" + short] = np.ascontiguousarray(inputs[name])
    aps = {k: nc.dram_tensor(k, v.shape, mb.dt.from_np(v.dtype), kind="ExternalInput").ap() for k, v in arrays.items()}
    out = nc.dram_tensor("out", (NP, D), mb.dt.float32, kind="ExternalOutput").ap()
    gps_layer_kernel(nc, aps["in_x"], aps["in_edges"], {k[3:]: v for k, v in aps.items()}, out)
    r = run(nc, [arrays], core_ids=[0])
    return r.results[0]["out"][:N]
```
